# Optimizing a Trainium2 kernel written in Bass

```python
import numpy as np
import jax
import jax.numpy as jnp

def _softmax(x, axis=-1):
    return jax.nn.softmax(x, axis=axis)

def _gelu(x):
    return jax.nn.gelu(x, approximate=True)

def _silu(x):
    return jax.nn.silu(x)

def _sigmoid(x):
    return jax.nn.sigmoid(x)

def _layernorm(x, axis=-1, eps=1e-05):
    m = jnp.mean(x, axis=axis, keepdims=True)
    v = jnp.var(x, axis=axis, keepdims=True)
    return (x - m) / jnp.sqrt(v + eps)

def _scatter_add(tgt, idx, src, axis=0):
    return tgt.at[idx].add(src)

def _segment_sum(src, seg, n):
    return jax.ops.segment_sum(src, seg, n)
kernel_name = 'mk_xattn_ffn_d1_seqx_r4_6dcad5'

def setup_inputs(seed: int=0):
    np.random.seed(seed)
    _w = jnp.asarray

    def _rec_inputs():
        import jax
        import jax.numpy as jnp
        _rk = jax.random.key(seed)
        x = 0.01048 + 0.1018 * jax.random.normal(jax.random.fold_in(_rk, 1), (4, 512, 512), jnp.float32)
        _lenS = 512 - jax.random.randint(jax.random.fold_in(_rk, 7), (4,), 0, max(1, 512 // 4) + 1, jnp.int32)
        _lenS2 = 512 - jax.random.randint(jax.random.fold_in(_rk, 8), (4,), 0, max(1, 512 // 4) + 1, jnp.int32)
        _ctx_512P = jax.random.normal(jax.random.fold_in(_rk, 11), (4, 16, 128), jnp.float32)
        _ctx_512c = jax.random.dirichlet(jax.random.fold_in(_rk, 511), 0.3 * jnp.ones((16,), jnp.float32), (4, 512))
        _ctx_512t = jnp.einsum('bsk,bkd->bsd', _ctx_512c, _ctx_512P)
        _ctx_512t = _ctx_512t * jax.lax.rsqrt(jnp.mean(jnp.square(_ctx_512t)) + 1e-12) * 0.953939
        ctx_512 = -0.000292821 + 1.00034 * (_ctx_512t + 0.3 * jax.random.normal(jax.random.fold_in(_rk, 611), (4, 512, 128), jnp.float32))
        return (x, ctx_512)
    x, ctx_512 = _rec_inputs()

    def _L0_xattn_setup():
        import jax, jax.numpy as jnp
        import numpy as np
        LRELU_ALPHA = 0.2
        MASK_VAL = -10000000000.0
        B, N, F_IN = (4, 512, 128)
        H, F_OUT = (8, 64)
        F_HID = H * F_OUT

        def gat_layer(x, adj, W, a_self, a_neigh, b):
            feat = jnp.einsum('nf,hfo->hno', x, W)
            attn_self = jnp.einsum('hno,ho->hn', feat, a_self)
            attn_neigh = jnp.einsum('hno,ho->hn', feat, a_neigh)
            e = attn_self[:, :, None] + attn_neigh[:, None, :]
            e = jax.nn.leaky_relu(e, LRELU_ALPHA)
            e = e + MASK_VAL * (1.0 - adj)[None, :, :]
            alpha = jax.nn.softmax(e, axis=-1)
            out = jnp.einsum('hnm,hmo->hno', alpha, feat) + b[:, None, :]
            out = jnp.transpose(out, (1, 0, 2)).reshape(out.shape[1], -1)
            return jax.nn.elu(out)
        key = jax.random.key(seed)
        ks = jax.random.split(key, 10)
        feats = jax.random.normal(ks[0], (B, N, F_IN), dtype=jnp.float32)
        a = (jax.random.uniform(ks[1], (B, N, N)) < 0.01).astype(jnp.float32)
        adj = jnp.maximum(a, jnp.eye(N, dtype=jnp.float32)[None])
        s0 = 1.0 / np.sqrt(F_IN)
        s1 = 1.0 / np.sqrt(F_HID)
        return {'feats': feats, 'adj': adj, 'W0': jax.random.normal(ks[2], (H, F_IN, F_OUT), dtype=jnp.float32) * s0, 'a_self0': jax.random.normal(ks[3], (H, F_OUT), dtype=jnp.float32) * 0.1, 'a_neigh0': jax.random.normal(ks[4], (H, F_OUT), dtype=jnp.float32) * 0.1, 'b0': jnp.zeros((H, F_OUT), dtype=jnp.float32), 'W1': jax.random.normal(ks[5], (H, F_HID, F_OUT), dtype=jnp.float32) * s1, 'a_self1': jax.random.normal(ks[6], (H, F_OUT), dtype=jnp.float32) * 0.1, 'a_neigh1': jax.random.normal(ks[7], (H, F_OUT), dtype=jnp.float32) * 0.1, 'b1': jnp.zeros((H, F_OUT), dtype=jnp.float32)}
    _L0_xattn_all = _L0_xattn_setup()
    _L0_xattn_in = {k: v for k, v in _L0_xattn_all.items() if k in ('W0', 'a_self0', 'a_neigh0', 'b0', 'W1', 'a_self1', 'a_neigh1', 'b1')}
    del _L0_xattn_all

    def _L0_ffn_setup():
        import math
        import jax, jax.numpy as jnp
        import numpy as np
        from jax import lax
        D = 512
        I = 256
        E = 32
        K = 4
        NG = 8
        TKG = 3
        NSH = 2
        SCALE = 2.5
        CF = 1.25
        B, S = (2, 512)

        def _router(x, router_w, e_bias):
            scores = jax.nn.sigmoid(x @ router_w.T)
            sc = scores + e_bias[None, :]
            T = x.shape[0]
            gs = sc.reshape(T, NG, E // NG)
            group_scores = lax.top_k(gs, 2)[0].sum(-1)
            _, gidx = lax.top_k(group_scores, TKG)
            gmask = jnp.zeros((T, NG), sc.dtype).at[jnp.arange(T)[:, None], gidx].set(1.0)
            smask = jnp.repeat(gmask, E // NG, axis=1)
            masked = jnp.where(smask > 0, sc, 0.0)
            _, topk_idx = lax.top_k(masked, K)
            topk_w = jnp.take_along_axis(scores, topk_idx, axis=1)
            topk_w = topk_w / (topk_w.sum(-1, keepdims=True) + 1e-20)
            topk_w = topk_w * SCALE
            return (topk_idx.astype(jnp.int32), topk_w)

        def _moe_forward(hidden_states, router_w, e_bias, W_gate, W_up, W_down, shared_gate, shared_up, shared_down):
            b, s, d = hidden_states.shape
            T = b * s
            C = int(math.ceil(CF * T / E))
            EC = E * C
            x = hidden_states.reshape(T, d)
            topk_idx, topk_w = _router(x, router_w, e_bias)
            expert_flat = topk_idx.reshape(-1)
            w_flat = topk_w.reshape(-1)
            tok_flat = jnp.repeat(jnp.arange(T, dtype=jnp.int32), K)
            sort_ix = jnp.argsort(expert_flat)
            e_sorted = expert_flat[sort_ix]
            tok_s = tok_flat[sort_ix]
            w_s = w_flat[sort_ix]
            counts = jnp.zeros(E, jnp.int32).at[e_sorted].add(1)
            group_start = jnp.concatenate([jnp.zeros(1, jnp.int32), jnp.cumsum(counts)[:-1].astype(jnp.int32)])
            pos = jnp.arange(T * K, dtype=jnp.int32) - group_start[e_sorted]
            valid = pos < C
            dest = e_sorted * C + jnp.where(valid, pos, 0)
            slots_token = jnp.zeros(EC, jnp.int32).at[dest].add(jnp.where(valid, tok_s, 0))
            slots_w = jnp.zeros(EC, w_s.dtype).at[dest].add(jnp.where(valid, w_s, 0.0))
            Xp = x[slots_token].reshape(E, C, d)
            G = jnp.einsum('ecd,edi->eci', Xp, W_gate)
            U = jnp.einsum('ecd,edi->eci', Xp, W_up)
            Y = jnp.einsum('eci,eid->ecd', jax.nn.silu(G) * U, W_down)
            Yf = Y.reshape(EC, d) * slots_w[:, None]
            out = jnp.zeros((T, d), x.dtype).at[slots_token].add(Yf)
            shared = jax.nn.silu(x @ shared_gate.T) * (x @ shared_up.T) @ shared_down.T
            return (out + shared).reshape(b, s, d)
        key = jax.random.key(seed)
        ks = jax.random.split(key, 8)

        def rn(k, shape, scale=0.02):
            return jax.random.normal(k, shape, jnp.float32) * scale
        return {'hidden_states': jax.random.normal(ks[0], (B, S, D), jnp.float32), 'router_w': rn(ks[1], (E, D)), 'e_bias': jnp.zeros((E,), jnp.float32), 'W_gate': rn(ks[2], (E, D, I)), 'W_up': rn(ks[3], (E, D, I)), 'W_down': rn(ks[4], (E, I, D)), 'shared_gate': rn(ks[5], (I * NSH, D)), 'shared_up': rn(ks[6], (I * NSH, D)), 'shared_down': rn(ks[7], (D, I * NSH))}
    _L0_ffn_all = _L0_ffn_setup()
    _L0_ffn_in = {k: v for k, v in _L0_ffn_all.items() if k in ('router_w', 'e_bias', 'W_gate', 'W_up', 'W_down', 'shared_gate', 'shared_up', 'shared_down')}
    del _L0_ffn_all
    return {'x': x, 'ctx_512': ctx_512, 'L0_xattn_W0': _L0_xattn_in['W0'], 'L0_xattn_a_self0': _L0_xattn_in['a_self0'], 'L0_xattn_a_neigh0': _L0_xattn_in['a_neigh0'], 'L0_xattn_b0': _L0_xattn_in['b0'], 'L0_xattn_W1': _L0_xattn_in['W1'], 'L0_xattn_a_self1': _L0_xattn_in['a_self1'], 'L0_xattn_a_neigh1': _L0_xattn_in['a_neigh1'], 'L0_xattn_b1': _L0_xattn_in['b1'], 'L0_ffn_router_w': _L0_ffn_in['router_w'], 'L0_ffn_e_bias': _L0_ffn_in['e_bias'], 'L0_ffn_W_gate': _L0_ffn_in['W_gate'], 'L0_ffn_W_up': _L0_ffn_in['W_up'], 'L0_ffn_W_down': _L0_ffn_in['W_down'], 'L0_ffn_shared_gate': _L0_ffn_in['shared_gate'], 'L0_ffn_shared_up': _L0_ffn_in['shared_up'], 'L0_ffn_shared_down': _L0_ffn_in['shared_down']}

def reference(x, ctx_512, L0_xattn_W0, L0_xattn_a_self0, L0_xattn_a_neigh0, L0_xattn_b0, L0_xattn_W1, L0_xattn_a_self1, L0_xattn_a_neigh1, L0_xattn_b1, L0_ffn_router_w, L0_ffn_e_bias, L0_ffn_W_gate, L0_ffn_W_up, L0_ffn_W_down, L0_ffn_shared_gate, L0_ffn_shared_up, L0_ffn_shared_down):
    import jax
    import jax.numpy as jnp

    def _L0_xattn_ref(feats, adj, W0, a_self0, a_neigh0, b0, W1, a_self1, a_neigh1, b1):
        import jax, jax.numpy as jnp
        import numpy as np
        LRELU_ALPHA = 0.2
        MASK_VAL = -10000000000.0
        B, N, F_IN = (4, 512, 128)
        H, F_OUT = (8, 64)
        F_HID = H * F_OUT

        def gat_layer(x, adj, W, a_self, a_neigh, b):
            feat = jnp.einsum('nf,hfo->hno', x, W)
            attn_self = jnp.einsum('hno,ho->hn', feat, a_self)
            attn_neigh = jnp.einsum('hno,ho->hn', feat, a_neigh)
            e = attn_self[:, :, None] + attn_neigh[:, None, :]
            e = jax.nn.leaky_relu(e, LRELU_ALPHA)
            e = e + MASK_VAL * (1.0 - adj)[None, :, :]
            alpha = jax.nn.softmax(e, axis=-1)
            out = jnp.einsum('hnm,hmo->hno', alpha, feat) + b[:, None, :]
            out = jnp.transpose(out, (1, 0, 2)).reshape(out.shape[1], -1)
            return jax.nn.elu(out)

        def per_graph(x, a):
            h = gat_layer(x, a, W0, a_self0, a_neigh0, b0)
            return gat_layer(h, a, W1, a_self1, a_neigh1, b1)
        return jax.vmap(per_graph)(feats, adj)

    def _L0_ffn_ref(hidden_states, router_w, e_bias, W_gate, W_up, W_down, shared_gate, shared_up, shared_down):
        import math
        import jax, jax.numpy as jnp
        import numpy as np
        from jax import lax
        D = 512
        I = 256
        E = 32
        K = 4
        NG = 8
        TKG = 3
        NSH = 2
        SCALE = 2.5
        CF = 1.25
        B, S = (2, 512)

        def _router(x, router_w, e_bias):
            scores = jax.nn.sigmoid(x @ router_w.T)
            sc = scores + e_bias[None, :]
            T = x.shape[0]
            gs = sc.reshape(T, NG, E // NG)
            group_scores = lax.top_k(gs, 2)[0].sum(-1)
            _, gidx = lax.top_k(group_scores, TKG)
            gmask = jnp.zeros((T, NG), sc.dtype).at[jnp.arange(T)[:, None], gidx].set(1.0)
            smask = jnp.repeat(gmask, E // NG, axis=1)
            masked = jnp.where(smask > 0, sc, 0.0)
            _, topk_idx = lax.top_k(masked, K)
            topk_w = jnp.take_along_axis(scores, topk_idx, axis=1)
            topk_w = topk_w / (topk_w.sum(-1, keepdims=True) + 1e-20)
            topk_w = topk_w * SCALE
            return (topk_idx.astype(jnp.int32), topk_w)

        def _moe_forward(hidden_states, router_w, e_bias, W_gate, W_up, W_down, shared_gate, shared_up, shared_down):
            b, s, d = hidden_states.shape
            T = b * s
            C = int(math.ceil(CF * T / E))
            EC = E * C
            x = hidden_states.reshape(T, d)
            topk_idx, topk_w = _router(x, router_w, e_bias)
            expert_flat = topk_idx.reshape(-1)
            w_flat = topk_w.reshape(-1)
            tok_flat = jnp.repeat(jnp.arange(T, dtype=jnp.int32), K)
            sort_ix = jnp.argsort(expert_flat)
            e_sorted = expert_flat[sort_ix]
            tok_s = tok_flat[sort_ix]
            w_s = w_flat[sort_ix]
            counts = jnp.zeros(E, jnp.int32).at[e_sorted].add(1)
            group_start = jnp.concatenate([jnp.zeros(1, jnp.int32), jnp.cumsum(counts)[:-1].astype(jnp.int32)])
            pos = jnp.arange(T * K, dtype=jnp.int32) - group_start[e_sorted]
            valid = pos < C
            dest = e_sorted * C + jnp.where(valid, pos, 0)
            slots_token = jnp.zeros(EC, jnp.int32).at[dest].add(jnp.where(valid, tok_s, 0))
            slots_w = jnp.zeros(EC, w_s.dtype).at[dest].add(jnp.where(valid, w_s, 0.0))
            Xp = x[slots_token].reshape(E, C, d)
            G = jnp.einsum('ecd,edi->eci', Xp, W_gate)
            U = jnp.einsum('ecd,edi->eci', Xp, W_up)
            Y = jnp.einsum('eci,eid->ecd', jax.nn.silu(G) * U, W_down)
            Yf = Y.reshape(EC, d) * slots_w[:, None]
            out = jnp.zeros((T, d), x.dtype).at[slots_token].add(Yf)
            shared = jax.nn.silu(x @ shared_gate.T) * (x @ shared_up.T) @ shared_down.T
            return (out + shared).reshape(b, s, d)
        return _moe_forward(hidden_states, router_w, e_bias, W_gate, W_up, W_down, shared_gate, shared_up, shared_down)
    x = x + _L0_xattn_ref(ctx_512, _layernorm(x, axis=-1), L0_xattn_W0, L0_xattn_a_self0, L0_xattn_a_neigh0, L0_xattn_b0, L0_xattn_W1, L0_xattn_a_self1, L0_xattn_a_neigh1, L0_xattn_b1)
    x = x + _L0_ffn_ref(_layernorm(x, axis=-1), L0_ffn_router_w, L0_ffn_e_bias, L0_ffn_W_gate, L0_ffn_W_up, L0_ffn_W_down, L0_ffn_shared_gate, L0_ffn_shared_up, L0_ffn_shared_down)
    return x

_drawn_inputs = setup_inputs


def setup_inputs(seed=0):
    import zlib

    import numpy as np

    out = dict(_drawn_inputs(seed))
    spreads = {'L0_xattn_b0': (0.0, 0.1), 'L0_xattn_b1': (0.0, 0.1), 'L0_ffn_e_bias': (0.0, 0.1)}
    factors = {}
    for name, (base, spread) in spreads.items():
        noise = np.random.default_rng([zlib.crc32(name.encode()), seed]).standard_normal(out[name].shape)
        drawn = base * np.exp(spread * noise) if base else spread * noise
        out[name] = jnp.asarray(drawn.astype(out[name].dtype))
    for name, factor in factors.items():
        out[name] = (out[name] * factor).astype(out[name].dtype)
    return out
```

```python
import concourse.bass as bass
from concourse import mybir
from contextlib import ExitStack

GRAPHS, SEQ, D = 4, 512, 512
P = 128
TPG = SEQ // P
TILES = GRAPHS * TPG
TOKENS = GRAPHS * SEQ
F_IN, HEADS, F_OUT = 128, 8, 64
F_HID = HEADS * F_OUT
KC = D // P
EXPERTS, GROUPS, GSIZE, TOP_GROUPS, TOP_K = 32, 8, 4, 3, 4
INNER = 256
IC = INNER // P
CAP = 80
ROW = D + EXPERTS
SCALE = 2.5
EPS = 1e-5
MASK = -1e10
SLOPE = 0.2
RING = 4
FIRST_SLOT = 3
XRING = 4
AHEAD = 3
ROUNDS = CAP // 8
RETIRED = -1.0
LOGIT_FACTOR = 4.1
ROUNDING = 40000.0


def xattn_moe(nc, x, ctx_in, W0, a_self0, a_neigh0, b0, W1, a_self1, a_neigh1, b1,
              router_w, e_bias, W_gate, W_up, W_down, shared_gate, shared_up, shared_down, out):
    f32, u32 = mybir.dt.float32, mybir.dt.uint32
    ALU = mybir.AluOpType
    ACT = mybir.ActivationFunctionType
    AX = mybir.AxisListType

    x_rows = x.rearrange("g s d -> (g s) d")
    out_rows = out.rearrange("g s d -> (g s) d")
    ctx_rows = ctx_in.rearrange("g s f -> (g s) f")
    idx_dram = nc.dram_tensor("idx_dram", (TOKENS, 1), u32).ap()
    rows_dram = nc.dram_tensor("rows_dram", (TOKENS, ROW), f32).ap()

    es = ExitStack()
    with es:
        def sb(name, shape, dt=f32):
            return es.enter_context(nc.sbuf_tensor(name, shape, dt))

        def sem(name):
            return es.enter_context(nc.semaphore(name))

        ident = sb("ident", [P, P])
        ones = sb("ones", [P, P])
        xs = sb("xs", [P, TILES, D])
        xnT = sb("xnT", [P, KC, TOKENS])
        w0 = sb("w0", [P, F_HID])
        w1 = sb("w1", [P, KC, F_HID])
        b0c = sb("b0c", [P, KC])
        b1r = sb("b1r", [P, F_HID])
        ebr = sb("ebr", [P, EXPERTS])
        ring = sb("ring", [P, RING, 3072])
        gu_buf = sb("gu_buf", [P, 4096])
        gT = gu_buf[:, 0:2048].rearrange("p (c i) -> p c i", c=KC)
        uT = gu_buf[:, 2048:4096].rearrange("p (c i) -> p c i", c=KC)
        xg = gu_buf[0:CAP, 0:XRING * ROW].rearrange("p (b r) -> p b r", b=XRING)
        ey = gu_buf[0:CAP, XRING * ROW:XRING * ROW + 3 * D].rearrange("p (b r) -> p b r", b=3)
        dT = sb("dT", [P, KC, D])
        rwraw = sb("rwraw", [EXPERTS, D])
        rwT = sb("rwT", [P, KC, EXPERTS])
        mx = sb("mx", [P, TILES, 8])
        ix = sb("ix", [P, TILES, 8], u32)
        ixg = sb("ixg", [P, TILES], u32)
        ix2 = sb("ix2", [P, TILES], u32)
        ctx_buf = sb("ctx_buf", [P, 4, SEQ])
        ctxg = ctx_buf[:, 0:2, :].rearrange("p b (t f) -> p b t f", f=F_IN)
        ctxT = ctx_buf[:, 2:4, :]
        h1T = sb("h1T", [P, 2, KC, SEQ])
        he = sb("he", [P, 2, SEQ])
        e1r = sb("e1r", [P, 4, SEQ])
        e1, hr = e1r[:, 0:2, :], e1r[:, 2:4, :]
        bn = sb("bn", [P, 2, 6])
        mv = sb("mv", [P, TILES, 2])
        ve = sb("ve", [P, TILES])
        half = sb("half", [P, TILES])
        r0 = sb("r0", [P, TILES])
        nt1 = sb("nt1", [P, TILES])
        rstd = sb("rstd", [P, TILES])
        nmr = sb("nmr", [P, TILES])
        xn = ctx_buf
        hT = h1T
        th = sb("th", [P, 2, SEQ])
        sg = sb("sg", [P, 2, SEQ])
        ob = he
        selT = e1r[0:EXPERTS, :, :].rearrange("p a b -> p (a b)")
        key = ctx_buf[0:EXPERTS, :, :].rearrange("p a b -> p (a b)")
        kk = sb("kk", [EXPERTS, CAP])
        kt = sb("kt", [EXPERTS, CAP])
        tokf = sb("tokf", [EXPERTS, CAP])
        tok = sb("tok", [CAP, EXPERTS], u32)
        RT = TPG * EXPERTS
        rth = sb("rth", [P, 2, TPG, EXPERTS])
        at = [0]

        def in_w1(*dims):
            n = 1
            for k in dims:
                n *= k
            at[0] += n
            names = "abcd"[:len(dims)]
            v = w1[:, :, :].rearrange("p c n -> p (c n)")[:, at[0] - n:at[0]]
            return v.rearrange(f"p ({' '.join(names)}) -> p {' '.join(names)}", **dict(zip(names, dims)))

        S = in_w1(TPG, EXPERTS)
        SB = in_w1(TPG, EXPERTS)
        rg = in_w1(8, TPG, GROUPS)
        rgi = sb("rgi", [P, TPG, 8], u32)
        rgm = sb("rgm", [P, TPG, 8])
        rgf = sb("rgf", [P, TPG, 8])
        eq = in_w1(TOP_K, TPG, EXPERTS)
        sel = in_w1(TILES, EXPERTS)
        den = sb("den", [P, TPG])
        wd = in_w1(TILES, EXPERTS)
        iota8 = sb("iota8", [P, TPG, GROUPS])
        iota32 = sb("iota32", [P, TPG, EXPERTS])
        flat = e1r[:, :, :].rearrange("p a b -> p (a b)")
        H2 = 2 * CAP
        xgT = flat[:, 0:3 * KC * CAP].rearrange("p (b c n) -> p b c n", b=3, c=KC)
        eh, ehT, et = (flat[:, o:o + 2 * H2].rearrange("p (b n) -> p b n", b=2)
                       for o in range(3 * KC * CAP, 3 * KC * CAP + 6 * H2, 2 * H2))

        bank = [es.enter_context(nc.psum_tensor(f"bank{i}", [P, 512], f32)) for i in range(8)]

        ld_x = [sem(f"ld_x{g}") for g in range(GRAPHS)]
        ld_sh = [sem(f"ld_sh{i}") for i in range(4)]
        ld_att = sem("ld_att")
        ld_eb = sem("ld_eb")
        ld_w = [sem(f"ld_w{i}") for i in range(RING)]
        consts = sem("consts")
        top_done, idx_done, idxg_ready = sem("top_done"), sem("idx_done"), sem("idxg_ready")
        idx_stored = [sem(f"idx_stored{g}") for g in range(GRAPHS)]
        idx2_ready = [sem(f"idx2_ready{g}") for g in range(GRAPHS)]
        ctxg_ready = [sem(f"ctxg_ready{g}") for g in range(GRAPHS)]
        tp_full, tp_free = sem("tp_full"), sem("tp_free")
        l1_full, l1_act, h1_ready = sem("l1_full"), sem("l1_act"), sem("h1_ready")
        l2_full, z_ready, ez_ready, x1_ready = sem("l2_full"), sem("z_ready"), sem("ez_ready"), sem("x1_ready")
        dve = sem("dve")
        ones_ready = sem("ones_ready")
        ve_ready, pow_ready, ln_ready, xn_ready = sem("ve_ready"), sem("pow_ready"), sem("ln_ready"), sem("xn_ready")
        rows_x, rows_w = sem("rows_x"), sem("rows_w")
        r_full, r_act, sel_ready, wd_ready = sem("r_full"), sem("r_act"), sem("sel_ready"), sem("wd_ready")
        gu_full, gu_act, hT_ready = sem("gu_full"), sem("gu_act"), sem("hT_ready")
        d_full, ob_ready = sem("d_full"), sem("ob_ready")
        ob_stored = [sem(f"ob_stored{i}") for i in range(2)]
        tok_ready = sem("tok_ready")
        xg_ready = [sem(f"xg_ready{i}") for i in range(XRING)]
        eg_full, eg_act, eh_ready = sem("eg_full"), sem("eg_act"), sem("eh_ready")
        ey_full, ey_ready = sem("ey_full"), sem("ey_ready")
        added = sem("added")

        G_SHARED, G_ROUTER = 0, 12
        G_CTX = 13
        G_XN = G_CTX + GRAPHS
        G_SEL = G_XN + TILES
        G_TOK = G_SEL + GRAPHS
        G_EXP = G_TOK + 1
        att_order = ["T0", "A0", "T1", "A1", "B0", "T2", "A2", "B1", "T3", "A3", "B2", "B3"]

        def ring_gate(e):
            return ring[:, (e + FIRST_SLOT) % RING, 0:1024].rearrange("p (c i) -> p c i", c=KC)

        def ring_up(e):
            return ring[:, (e + FIRST_SLOT) % RING, 1024:2048].rearrange("p (c i) -> p c i", c=KC)

        def ring_down(e):
            return ring[:, (e + FIRST_SLOT) % RING, 2048:3072].rearrange("p (c d) -> p c d", c=IC)

        def raw(i):
            return ring[:, i, 0:2048].rearrange("p (c k) -> p c k", c=KC)

        room = xnT[:, :, :].rearrange("p c n -> p (c n)")
        ctx_all = room[:, 0:TOKENS]
        absw = room[:, 2048:4096].rearrange("p (b n) -> p b n", b=4)
        arow = room[0:1, 4096:4096 + 5 * F_HID].rearrange("p (b n) -> p b n", b=5)
        sums = room[0:1, 6656:6656 + 2 * F_HID].rearrange("p (b n) -> p b n", b=2)
        mv0 = sb("mv0", [P, TILES, 2])
        chk = sb("chk", [P, 4, TILES, 2])
        worst = sb("worst", [P, 2])
        bound = sb("bound", [1, 16])
        heads = sb("heads", [1, 2, HEADS])
        fast_flag = sb("fast_flag", [1, 1], u32)
        ld_chk, absw_ready, absw_used, sums_full = sem("ld_chk"), sem("absw_ready"), sem("absw_used"), sem("sums_full")
        sums_ready, var0_ready, pow0_ready, worst_ready = sem("sums_ready"), sem("var0_ready"), sem("pow0_ready"), sem("worst_ready")
        worst_full, flag_ready = sem("worst_full"), sem("flag_ready")

        mask_dram = nc.dram_tensor("mask_dram", (TOKENS, SEQ), f32).ap()
        feat_dram = nc.dram_tensor("feat_dram", (TOKENS, F_HID), f32).ap()
        sn_dram = nc.dram_tensor("sn_dram", (2 * HEADS, TOKENS), f32).ap()
        hid_dram = [nc.dram_tensor(f"hid_dram{i}", (TOKENS, F_HID), f32).ap() for i in range(2)]
        g_x = room[:, 0:D]
        g_xT = room[:, D:2 * D].rearrange("p (c n) -> p c n", c=KC)
        g_a = room[:, 2 * D:4 * D].rearrange("p (b n) -> p b n", b=2)
        g_feat = room[:, 4 * D:5 * D]
        g_tmp = room[:, 5 * D:6 * D]
        g_mask = room[:, 6 * D:7 * D]
        g_neigh = room[:, 7 * D:8 * D]
        g_e = room[:, 8 * D:9 * D]
        g_p = room[:, 9 * D:10 * D]
        g_pT = room[:, 10 * D:11 * D]
        g_f = room[:, 11 * D:11 * D + KC * F_OUT].rearrange("p (c o) -> p c o", c=KC)
        g_b, g_xp, g_z, g_ez, g_h = (room[:, 12 * D + F_OUT * i:12 * D + F_OUT * i + F_OUT] for i in range(5))
        g_sn = room[:, 13 * D:13 * D + 2 * HEADS]
        g_snT = room[0:2 * HEADS, 13 * D + 32:13 * D + 32 + P]
        g_self, g_max, g_sum, g_ve, g_r0, g_r = (room[:, 14 * D + i:14 * D + i + 1] for i in range(6))
        g_bn = room[:, 14 * D + 16:14 * D + 22]
        g_mv = room[:, 14 * D + 24:14 * D + 26]
        g_load, g_const, g_store, g_done = sem("g_load"), sem("g_const"), sem("g_store"), sem("g_done")
        g_held = sem("g_held")
        g_pe, g_act, g_dve, g_pool = sem("g_pe"), sem("g_act"), sem("g_dve"), sem("g_pool")
        a_pair = [(a_self0, a_neigh0, b0), (a_self1, a_neigh1, b1)]

        block = es.enter_context(nc.Block())

        DVE_M, ACT_F, PE_F, DVE_F, PE_S, ACT_S, DVE_S = 10, 2, 3, 5, 2, 4, 8
        F_ROUNDS, S_ROUNDS = TILES, TILES * HEADS

        def held(eng, what, value):
            eng.wait_ge(what, value)
            eng.sem_inc(g_held)

        def slow_sync(sp):
            loads = stores = consts_in = 0
            with sp.Fori(0, TILES) as i:
                sp.dma_start(g_x, x_rows[bass.ds(i * P, P), :]).then_inc(g_load, 16)
                held(sp, g_dve, i * DVE_M + DVE_M)
                sp.dma_start(mask_dram[bass.ds(i * P, P), :], g_e).then_inc(g_store, 16)
                held(sp, g_store, i * 16 + 16)
            dve, loads, stores, act, pe = TILES * DVE_M, TILES * 16, TILES * 16, 0, 0
            for layer in range(2):
                sp.dma_start(g_a[:, 0, :], a_pair[layer][0].rearrange("h o -> (h o)").partition_broadcast(P)).then_inc(g_const, 16)
                sp.dma_start(g_a[:, 1, :], a_pair[layer][1].rearrange("h o -> (h o)").partition_broadcast(P)).then_inc(g_const, 16)
                with sp.Fori(0, TILES) as i:
                    src = ctx_rows if layer == 0 else hid_dram[0]
                    sp.dma_start(g_x[:, 0:src.shape[1]], src[bass.ds(i * P, P), :]).then_inc(g_load, 16)
                    held(sp, g_act, i * ACT_F + (act + ACT_F))
                    sp.dma_start(sn_dram[:, bass.ds(i * P, P)], g_snT).then_inc(g_store, 16)
                    sp.dma_start(feat_dram[bass.ds(i * P, P), :], g_feat).then_inc(g_store, 16)
                    held(sp, g_store, i * 32 + (stores + 32))
                act, dve, loads, stores = act + TILES * ACT_F, dve + TILES * DVE_F, loads + TILES * 16, stores + TILES * 32
                with sp.Fori(0, GRAPHS) as g:
                    with sp.Fori(0, TPG) as t:
                        with sp.Fori(0, HEADS) as h:
                            i = g * (TPG * HEADS) + t * HEADS + h
                            rows = g * SEQ + t * P
                            sp.dma_start(g_mask, mask_dram[bass.ds(rows, P), :]).then_inc(g_load, 16)
                            sp.dma_start(g_neigh, sn_dram[bass.ds(h + HEADS, 1), bass.ds(g * SEQ, SEQ)]
                                         .to_broadcast([P, SEQ])).then_inc(g_load, 16)
                            sp.dma_start(g_self, sn_dram[bass.ds(h, 1), bass.ds(rows, P)].rearrange("a p -> p a"),
                                         allow_slow_non_contiguous=True).then_inc(g_load, 16)
                            sp.dma_start(g_f, feat_dram[bass.ds(g * SEQ, SEQ), bass.ds(h * F_OUT, F_OUT)]
                                         .rearrange("(c p) o -> p c o", p=P)).then_inc(g_load, 16)
                            sp.dma_start(g_b, a_pair[layer][2][bass.ds(h, 1), :].to_broadcast([P, F_OUT])).then_inc(g_load, 16)
                            sp.dma_start(g_xp, x_rows[bass.ds(rows, P), bass.ds(h * F_OUT, F_OUT)]).then_inc(g_load, 16)
                            held(sp, g_dve, i * DVE_S + (dve + DVE_S))
                            sp.dma_start(hid_dram[layer][bass.ds(rows, P), bass.ds(h * F_OUT, F_OUT)], g_h).then_inc(g_store, 16)
                            held(sp, g_store, i * 16 + (stores + 16))
                act, dve, loads, stores = act + S_ROUNDS * ACT_S, dve + S_ROUNDS * DVE_S, loads + S_ROUNDS * 96, stores + S_ROUNDS * 16
            for g in range(GRAPHS):
                sp.dma_start(xs[:, TPG * g:TPG * g + TPG, :],
                             hid_dram[1][SEQ * g:SEQ * g + SEQ, :].rearrange("(p t) d -> p t d", p=P)).then_inc(g_done, 16)
            sp.wait_ge(g_done, 16 * GRAPHS)

        def slow_pool(pool):
            with pool.Fori(0, TILES) as i:
                pool.wait_ge(g_dve, i * DVE_M + 3)
                nc.gpsimd.tensor_tensor(g_r0, g_ve, half[:, 0:1], ALU.pow).then_inc(g_pool, 1)

        def slow_vector(v):
            def step(ins, n):
                ins.then_inc(g_dve, 1)
                held(v, g_dve, n)

            with v.Fori(0, TILES) as i:
                n = i * DVE_M
                v.wait_ge(g_load, i * 16 + 16)
                step(v.bn_stats(g_bn, g_x), n + 1)
                step(v.bn_aggr(g_mv, g_bn), n + 2)
                step(v.tensor_scalar(g_ve, g_mv[:, 1:2], EPS, None, ALU.add), n + 3)
                v.wait_ge(g_pool, i + 1)
                step(v.tensor_tensor(g_r, g_ve, g_r0, ALU.mult), n + 4)
                step(v.tensor_tensor(g_r, g_r, g_r0, ALU.mult), n + 5)
                step(v.tensor_scalar(g_r, g_r, -0.5, 1.5, ALU.mult, ALU.add), n + 6)
                step(v.tensor_tensor(g_r, g_r, g_r0, ALU.mult), n + 7)
                step(v.tensor_scalar(g_tmp, g_x, g_mv[:, 0:1], g_r, ALU.subtract, ALU.mult), n + 8)
                step(v.tensor_scalar(g_p, g_tmp, -1.0, 1.0, ALU.mult, ALU.add), n + 9)
                step(v.tensor_scalar(g_e, g_p, MASK, None, ALU.mult), n + 10)
            dve, loads, act, pe = TILES * DVE_M, TILES * 16, 0, 0
            for layer in range(2):
                v.wait_ge(g_const, 32 * (layer + 1))
                with v.Fori(0, TILES) as i:
                    n = i * DVE_F + dve
                    v.wait_ge(g_pe, i * PE_F + (pe + 2))
                    step(v.tensor_copy(g_feat, bank[1][:, :]), n + 1)
                    step(v.tensor_tensor(g_tmp, g_feat, g_a[:, 0, :], ALU.mult), n + 2)
                    step(v.reduce_sum(g_sn[:, 0:HEADS], g_tmp.rearrange("p (h o) -> p h o", h=HEADS), axis=AX.X), n + 3)
                    step(v.tensor_tensor(g_tmp, g_feat, g_a[:, 1, :], ALU.mult), n + 4)
                    step(v.reduce_sum(g_sn[:, HEADS:2 * HEADS], g_tmp.rearrange("p (h o) -> p h o", h=HEADS), axis=AX.X), n + 5)
                dve, pe, act, loads = dve + TILES * DVE_F, pe + TILES * PE_F, act + TILES * ACT_F, loads + TILES * 16
                with v.Fori(0, S_ROUNDS) as i:
                    n = i * DVE_S + dve
                    v.wait_ge(g_load, i * 96 + (loads + 96))
                    v.wait_ge(g_act, i * ACT_S + (act + 1))
                    step(v.scalar_tensor_tensor(g_p, g_e, SLOPE, g_e, ALU.mult, ALU.max), n + 1)
                    step(v.tensor_tensor(g_e, g_p, g_mask, ALU.add), n + 2)
                    step(v.reduce_max(g_max, g_e, axis=AX.X), n + 3)
                    step(v.tensor_scalar(g_max, g_max, -1.0, None, ALU.mult), n + 4)
                    v.wait_ge(g_act, i * ACT_S + (act + 2))
                    step(v.reciprocal(g_sum, g_sum), n + 5)
                    v.wait_ge(g_pe, i * PE_S + (pe + 2))
                    step(v.scalar_tensor_tensor(g_z, bank[1][:, 0:F_OUT], g_sum, g_b, ALU.mult, ALU.add), n + 6)
                    v.wait_ge(g_act, i * ACT_S + (act + 4))
                    step(v.tensor_scalar(g_ez, g_ez, 1.0, -1.0, ALU.min, ALU.add), n + 7)
                    if layer == 0:
                        step(v.scalar_tensor_tensor(g_h, g_z, 0.0, g_ez, ALU.max, ALU.add), n + 8)
                    else:
                        v.scalar_tensor_tensor(g_ez, g_z, 0.0, g_ez, ALU.max, ALU.add).then_inc(g_pool, 1)
                        v.wait_ge(g_pool, i + (TILES + 1))
                        step(v.tensor_tensor(g_h, g_ez, g_xp, ALU.add), n + 8)
                dve, pe, act, loads = dve + S_ROUNDS * DVE_S, pe + S_ROUNDS * PE_S, act + S_ROUNDS * ACT_S, loads + S_ROUNDS * 96
            v.wait_ge(g_done, 16 * GRAPHS)

        def slow_scalar(act_e):
            act, pe, dve, loads = 0, 0, TILES * DVE_M, TILES * 16
            for layer in range(2):
                kc = 1 if layer == 0 else KC
                with act_e.Fori(0, TILES) as i:
                    act_e.wait_ge(g_pe, i * PE_F + (pe + 1))
                    act_e.activation(g_xT[:, 0:kc, :], bank[0][:, 0:kc * P].rearrange("p (c n) -> p c n", c=kc), ACT.Copy).then_inc(g_act, 1)
                    act_e.wait_ge(g_pe, i * PE_F + (pe + 3))
                    act_e.activation(g_snT, bank[0][0:2 * HEADS, 0:P], ACT.Copy).then_inc(g_act, 1)
                dve, pe, act, loads = dve + TILES * DVE_F, pe + TILES * PE_F, act + TILES * ACT_F, loads + TILES * 16
                with act_e.Fori(0, S_ROUNDS) as i:
                    act_e.wait_ge(g_load, i * 96 + (loads + 96))
                    act_e.activation(g_e, g_neigh, ACT.Identity, bias=g_self).then_inc(g_act, 1)
                    act_e.wait_ge(g_dve, i * DVE_S + (dve + 4))
                    act_e.activation(g_tmp, g_e, ACT.Exp, bias=g_max, accum_out=g_sum).then_inc(g_act, 1)
                    act_e.wait_ge(g_pe, i * PE_S + (pe + 1))
                    act_e.activation(g_pT, bank[0][:, :], ACT.Copy).then_inc(g_act, 1)
                    act_e.wait_ge(g_dve, i * DVE_S + (dve + 6))
                    act_e.activation(g_ez, g_z, ACT.Exp).then_inc(g_act, 1)
                dve, pe, act, loads = dve + S_ROUNDS * DVE_S, pe + S_ROUNDS * PE_S, act + S_ROUNDS * ACT_S, loads + S_ROUNDS * 96

        def slow_tensor(pe_e):
            act, pe, dve, loads = 0, 0, TILES * DVE_M, TILES * 16
            for layer in range(2):
                kc = 1 if layer == 0 else KC
                w = w0[:, :].unsqueeze(1) if layer == 0 else w1
                with pe_e.Fori(0, TILES) as i:
                    pe_e.wait_ge(g_load, i * 16 + (loads + 16))
                    for c in range(kc):
                        last = pe_e.transpose(bank[0][:, P * c:P * c + P], g_x[:, P * c:P * c + P], ident[:, :])
                    last.then_inc(g_pe, 1)
                    pe_e.wait_ge(g_act, i * ACT_F + (act + 1))
                    for c in range(kc):
                        last = pe_e.matmul(bank[1][:, :], g_xT[:, c, :], w[:, c, :], start=(c == 0), stop=(c == kc - 1))
                    last.then_inc(g_pe, 1)
                    pe_e.wait_ge(g_dve, i * DVE_F + (dve + DVE_F))
                    pe_e.transpose(bank[0][0:2 * HEADS, 0:P], g_sn, ident[:, :]).then_inc(g_pe, 1)
                dve, act, loads = dve + TILES * DVE_F, act + TILES * ACT_F, loads + TILES * 16
                with pe_e.Fori(0, S_ROUNDS) as i:
                    pe_e.wait_ge(g_act, i * ACT_S + (act + 2))
                    for c in range(KC):
                        last = pe_e.transpose(bank[0][:, P * c:P * c + P], g_tmp[:, P * c:P * c + P], ident[:, :])
                    last.then_inc(g_pe, 1)
                    pe_e.wait_ge(g_act, i * ACT_S + (act + 3))
                    for c in range(KC):
                        last = pe_e.matmul(bank[1][:, 0:F_OUT], g_pT[:, P * c:P * c + P], g_f[:, c, :],
                                           start=(c == 0), stop=(c == KC - 1))
                    last.then_inc(g_pe, 1)
                dve, act, loads = dve + S_ROUNDS * DVE_S, act + S_ROUNDS * ACT_S, loads + S_ROUNDS * 96

        def unless_one_hot(eng, slow=None):
            eng.wait_ge(flag_ready, 1)
            one_hot = eng.value_load(fast_flag[0:1, 0:1], min_val=0, max_val=1)
            with eng.If(one_hot == 0):
                slow(eng)
            with eng.Else():
                eng.nop()

        @block.sync
        def _(sp):
            for g in range(GRAPHS):
                sp.dma_start(xs[:, TPG * g:TPG * g + TPG, :],
                             x[g].rearrange("(p t) d -> p t d", p=P)).then_inc(ld_x[g], 16)
            for i, w in enumerate((shared_gate, shared_up, shared_down)):
                sp.dma_start(raw(i), w.rearrange("(c p) k -> p c k", p=P)).then_inc(ld_sh[i], 16)
            sp.dma_start(rwraw[:, :], router_w).then_inc(ld_sh[3], 16)

            def load_expert(e):
                s = (e + FIRST_SLOT) % RING
                sp.dma_start(ring_gate(e), W_gate[e].rearrange("(p c) i -> p c i", c=KC)).then_inc(ld_w[s], 16)
                sp.dma_start(ring_up(e), W_up[e].rearrange("(p c) i -> p c i", c=KC)).then_inc(ld_w[s], 16)
                sp.dma_start(ring_down(e), W_down[e].rearrange("(c p) d -> p c d", p=P)).then_inc(ld_w[s], 16)

            for e in range(RING - FIRST_SLOT):
                load_expert(e)
            for g in range(GRAPHS):
                sp.wait_ge(idxg_ready, g + 1)
                sp.dma_start(idx_dram[SEQ * g:SEQ * g + SEQ, :].rearrange("(p t) o -> p (t o)", p=P),
                             ixg[:, TPG * g:TPG * g + TPG]).then_inc(idx_stored[g], 16)
            sp.wait_ge(tp_full, G_ROUTER)
            for e in range(RING - FIRST_SLOT, RING):
                load_expert(e)
            unless_one_hot(sp, slow_sync)
            for g in range(GRAPHS):
                sp.wait_ge(xn_ready, TPG * (g + 1))
                sp.dma_start(rows_dram[SEQ * g:SEQ * g + SEQ, 0:D].rearrange("(p t) d -> p t d", p=P),
                             xn[:, :, :]).then_inc(rows_x, 16)
            for g in range(GRAPHS):
                sp.wait_ge(wd_ready, g + 1)
                sp.dma_start(rows_dram[SEQ * g:SEQ * g + SEQ, D:ROW].rearrange("(p t) e -> p t e", p=P),
                             wd[:, TPG * g:TPG * g + TPG, :]).then_inc(rows_w, 16)
            for t in range(TILES):
                sp.wait_ge(ob_ready, t + 1)
                sp.dma_start(out[t // TPG].rearrange("(p t) d -> p t d", p=P)[:, t % TPG, :], ob[:, t % 2, :]).then_inc(ob_stored[t % 2], 16)
            for e in range(RING, EXPERTS):
                sp.wait_ge(ey_full, e - RING + 1)
                load_expert(e)

        @block.gpsimd
        def _(pool):
            pool.memset(ident[:, :], 0.0).then_inc(consts, 1)
            pool.wait_ge(consts, 1)
            pool.affine_select(out=ident[:, :], in_=ident[:, :], compare_op=ALU.not_equal, fill=1.0,
                               base=0, pattern=[[-1, P]], channel_multiplier=1).then_inc(consts, 1)
            pool.iota(iota8[:, :, :], [[0, TPG], [1, GROUPS]], base=0, channel_multiplier=0,
                      allow_small_or_imprecise_dtypes=True).then_inc(consts, 1)
            pool.iota(iota32[:, :, :], [[0, TPG], [1, EXPERTS]], base=0, channel_multiplier=0,
                      allow_small_or_imprecise_dtypes=True).then_inc(consts, 1)
            pool.memset(half[:, :], -0.5).then_inc(consts, 1)
            for g in range(GRAPHS):
                pool.wait_ge(idx_stored[g], 16)
                for t in range(TPG * g, TPG * g + TPG):
                    pool.indirect_dma_start(
                        out=ix2[:, t:t + 1], out_offset=None, in_=idx_dram,
                        in_offset=bass.IndirectOffsetOnAxis(ap=ixg[:, t:t + 1], axis=0)).then_inc(idx2_ready[g], 16)
                pool.wait_ge(idx2_ready[g], 16 * TPG)
                if g >= 2:
                    pool.wait_ge(tp_full, G_CTX + g - 1)
                for t in range(TPG):
                    pool.indirect_dma_start(
                        out=ctxg[:, g % 2, t, :], out_offset=None, in_=ctx_rows,
                        in_offset=bass.IndirectOffsetOnAxis(ap=ix2[:, TPG * g + t:TPG * g + t + 1], axis=0)
                    ).then_inc(ctxg_ready[g], 16)
            pool.wait_ge(consts, 5)
            pool.wait_ge(var0_ready, 1)
            nc.gpsimd.tensor_tensor(chk[:, 3, :, 1], chk[:, 3, :, 0], half[:, :], ALU.pow).then_inc(pow0_ready, 1)
            unless_one_hot(pool, slow_pool)
            for g in range(GRAPHS):
                s = slice(TPG * g, TPG * g + TPG)
                pool.wait_ge(ve_ready, g + 1)
                nc.gpsimd.tensor_tensor(r0[:, s], ve[:, s], half[:, s], ALU.pow).then_inc(pow_ready, 1)

            def gather(e):
                if e >= XRING:
                    pool.wait_ge(ey_ready, e - XRING + 1)
                pool.indirect_dma_start(
                    out=xg[:, e % XRING, :], out_offset=None, in_=rows_dram,
                    in_offset=bass.IndirectOffsetOnAxis(ap=tok[:, e:e + 1], axis=0)).then_inc(xg_ready[e % XRING], 16)

            pool.wait_ge(rows_x, 16 * GRAPHS)
            pool.wait_ge(tp_full, G_XN + TILES)
            pool.iota(key[:, :], [[-1, TOKENS]], base=TOKENS, channel_multiplier=0,
                      allow_small_or_imprecise_dtypes=True).then_inc(consts, 1)
            pool.wait_ge(rows_w, 16 * GRAPHS)
            pool.wait_ge(tp_free, G_TOK + 1)
            pool.wait_ge(gu_full, 4 * KC)
            for e in range(AHEAD):
                gather(e)
            for i in range(2):
                pool.wait_ge(ob_stored[i], 16 * (TILES // 2))
            for e in range(EXPERTS):
                if e + AHEAD < EXPERTS:
                    gather(e + AHEAD)
                pool.wait_ge(ey_ready, e + 1)
                if e:
                    pool.wait_ge(added, 16 * e)
                pool.indirect_dma_start(
                    out=out_rows, out_offset=bass.IndirectOffsetOnAxis(ap=tok[:, e:e + 1], axis=0),
                    in_=ey[:, e % 3, :], in_offset=None, compute_op=ALU.add).then_inc(added, 16)
            pool.wait_ge(added, 16 * EXPERTS)

        @block.scalar
        def _(act):
            act.dma_start(w0[:, :].rearrange("f (h o) -> f h o", h=HEADS),
                          W0.rearrange("h f o -> f h o")).then_inc(ld_att, 16)
            act.dma_start(b0c[:, :], b0.rearrange("h o -> (h o)").rearrange("(c p) -> p c", p=P),
                          allow_slow_non_contiguous=True).then_inc(ld_att, 16)
            for c in range(KC):
                act.dma_start(w1[:, c, :].rearrange("f (h o) -> f h o", h=HEADS),
                              W1[:, P * c:P * c + P, :].rearrange("h f o -> f h o")).then_inc(ld_att, 16)
            act.dma_start(b1r[:, :], b1.rearrange("h o -> (h o)").partition_broadcast(P)).then_inc(ld_att, 16)
            for i, a in enumerate((a_self0, a_neigh0, a_self1, a_neigh1, b0)):
                act.dma_start(arow[:, i, :], a.rearrange("h o -> (h o)").unsqueeze(0)).then_inc(ld_chk, 16)
            act.dma_start(ctx_all, ctx_in.rearrange("g (p t) f -> p g (t f)", p=P)).then_inc(ld_chk, 16)
            act.dma_start(ebr[:, :], e_bias.partition_broadcast(P)).then_inc(ld_eb, 16)

            def evac(n, dst, width=512, parts=P, shape=None):
                act.wait_ge(tp_full, n + 1)
                src = bank[n % 2][0:parts, 0:width]
                if shape:
                    src = src.rearrange("p (a b) -> p a b", a=shape)
                act.activation(dst, src, ACT.Copy).then_inc(tp_free, 1)

            for i, w in enumerate((gT, uT, dT)):
                for c in range(KC):
                    evac(G_SHARED + KC * i + c, w[:, c, :])
            evac(G_ROUTER, rwT[:, :, :], KC * EXPERTS, shape=KC)
            act.wait_ge(ld_att, 16 * 7)
            for c in range(KC + 1):
                if c == KC:
                    act.wait_ge(absw_used, 1)
                act.activation(absw[:, c % KC, :], w1[:, c, :] if c < KC else w0[:, :], ACT.Abs).then_inc(absw_ready, 1)
            for step in att_order:
                g = int(step[1])
                if step[0] == "T":
                    if g >= 2:
                        act.wait_ge(l1_full, KC * (g - 1))
                    evac(G_CTX + g, ctxT[:, g % 2, :])
                elif step[0] == "A":
                    for c in range(KC):
                        n = KC * g + c
                        act.wait_ge(l1_full, n + 1)
                        if n >= 2:
                            act.wait_ge(h1_ready, n - 1)
                        act.activation(he[:, n % 2, :], bank[2 + c][:, :], ACT.Exp, bias=b0c[:, c:c + 1])
                        act.activation(hr[:, n % 2, :], bank[2 + c][:, :], ACT.Relu,
                                       bias=b0c[:, c:c + 1]).then_inc(l1_act, 1)
                else:
                    for t in range(TPG):
                        n = TPG * g + t
                        act.wait_ge(z_ready, n + 1)
                        if n >= 2:
                            act.wait_ge(x1_ready, n - 1)
                        act.activation(th[:, n % 2, :], sg[:, n % 2, :], ACT.Exp).then_inc(ez_ready, 1)
            unless_one_hot(act, slow_scalar)
            for g in range(GRAPHS):
                act.wait_ge(ln_ready, g + 1)
                if g:
                    act.wait_ge(rows_x, 16 * g)
                for t in range(TPG):
                    n = TPG * g + t
                    act.activation(xn[:, t, :], xs[:, n, :], ACT.Identity, bias=nmr[:, n:n + 1],
                                   scale=rstd[:, n:n + 1]).then_inc(xn_ready, 1)
                for t in range(TPG):
                    n = TPG * g + t
                    evac(G_XN + n, xnT[:, :, P * n:P * n + P], shape=KC)
                act.wait_ge(r_full, g + 1)
                if g >= 2:
                    act.wait_ge(sel_ready, g - 1)
                act.activation(rth[:, g % 2, :, :], bank[6 + g % 2][:, 0:RT].rearrange("p (a b) -> p a b", a=TPG),
                               ACT.Tanh, scale=0.5).then_inc(r_act, 1)

            def gu(n):
                act.wait_ge(gu_full, n + 1)
                if n >= 2:
                    act.wait_ge(hT_ready, n - 1)
                act.activation(th[:, n % 2, :], bank[2 + n % 2][:, :], ACT.Tanh, scale=0.5).then_inc(gu_act, 1)

            for n in range(KC):
                gu(n)
            for g in range(GRAPHS):
                evac(G_SEL + g, selT[:, SEQ * g:SEQ * g + SEQ].rearrange("e (p t) -> e t p", t=TPG),
                     parts=EXPERTS, shape=TPG)
            for n in range(KC, 4 * KC):
                gu(n)
            evac(G_TOK, tok[:, :], EXPERTS, parts=CAP)

            def spread(e):
                if e >= 3:
                    act.wait_ge(eg_full, e - 2)
                evac(G_EXP + e, xgT[:, e % 3, :, :], KC * CAP, shape=KC)

            spread(0)
            for e in range(EXPERTS + 1):
                if e + 1 < EXPERTS:
                    spread(e + 1)
                if e < EXPERTS:
                    act.wait_ge(eg_full, e + 1)
                    if e >= 2:
                        act.wait_ge(eh_ready, e - 1)
                    act.activation(et[:, e % 2, :], bank[2 + e % 2][:, 0:2 * CAP], ACT.Tanh,
                                   scale=0.5).then_inc(eg_act, 1)
                if e:
                    y = e - 1
                    act.wait_ge(ey_full, y + 1)
                    if y >= 3:
                        act.wait_ge(added, 16 * (y - 2))
                    act.activation(ey[:, y % 3, :], bank[6 + y % 2][0:CAP, :], ACT.Copy,
                                   scale=xg[:, y % XRING, D + y:D + y + 1]).then_inc(ey_ready, 1)

        @block.vector
        def _(v):
            done = [0]

            def link(ins):
                done[0] += 1
                ins.then_inc(dve, 1)
                v.wait_ge(dve, done[0])

            v.memset(ones[:, :], 1.0).then_inc(ones_ready, 1)
            for t in range(TILES):
                g = t // TPG
                if t % TPG == 0:
                    v.wait_ge(ld_x[g], 16)
                v.max(mx[:, t, :], xs[:, t, :]).then_inc(top_done, 1)
                v.wait_ge(top_done, t + 1)
                v.max_index(ix[:, t, :], mx[:, t, :], xs[:, t, :]).then_inc(idx_done, 1)
                if t % TPG == TPG - 1:
                    v.wait_ge(idx_done, t + 1)
                    v.tensor_scalar(ixg[:, TPG * g:t + 1], ix[:, TPG * g:t + 1, 0], float(SEQ * g), None,
                                    ALU.add).then_inc(idxg_ready, 1)
            v.wait_ge(ld_att, 16 * 7)
            v.wait_ge(sums_full, 1)
            v.tensor_copy(sums[:, 0, :], bank[6][0:1, :])
            v.tensor_copy(sums[:, 1, :], bank[7][0:1, :]).then_inc(sums_ready, 1)

            def stats0(g):
                for t in range(TPG * g, TPG * g + TPG):
                    link(v.bn_stats(bn[:, t % 2, :], xs[:, t, :]))
                    link(v.bn_aggr(mv0[:, t, :], bn[:, t % 2, :]))

            def smallest_gap():
                v.tensor_scalar(chk[:, 3, :, 0], mv0[:, :, 1], EPS, None, ALU.add).then_inc(var0_ready, 1)
                v.wait_ge(ld_chk, 16 * 6)
                v.tensor_reduce(out=worst[:, 0:1], in_=ctx_all, op=ALU.max, axis=AX.X, apply_absolute_value=True)
                v.wait_ge(pow0_ready, 1)
                link(v.tensor_tensor(chk[:, 0, :, :], mx[:, :, 0:2], mv0[:, :, 0:1].to_broadcast([P, TILES, 2]), ALU.subtract))
                link(v.tensor_tensor(chk[:, 1, :, :], chk[:, 0, :, :], chk[:, 3, :, 1:2].to_broadcast([P, TILES, 2]), ALU.mult))
                link(v.tensor_scalar(chk[:, 0, :, :], chk[:, 1, :, :], -1.0, 1.0, ALU.mult, ALU.add))
                link(v.tensor_scalar(chk[:, 1, :, :], chk[:, 0, :, :], MASK, None, ALU.mult))
                link(v.tensor_tensor(chk[:, 2, :, 0], chk[:, 1, :, 1], chk[:, 1, :, 0], ALU.subtract))
                v.reduce_max(worst[:, 1:2], chk[:, 2, :, 0], axis=AX.X).then_inc(worst_ready, 1)

            def decide():
                b = [bound[:, i:i + 1] for i in range(16)]
                link(v.scalar_tensor_tensor(arow, arow, -1.0, arow, ALU.mult, ALU.max))
                v.tensor_reduce(out=b[0], in_=arow[:, 4, :], op=ALU.max, axis=AX.X)
                v.tensor_reduce(out=b[1], in_=sums[:, 0, :], op=ALU.max, axis=AX.X)
                v.tensor_tensor(arow[:, 0, :], arow[:, 0, :], arow[:, 1, :], ALU.add)
                link(v.tensor_tensor(arow[:, 2, :], arow[:, 2, :], arow[:, 3, :], ALU.add))
                v.tensor_tensor(arow[:, 0, :], arow[:, 0, :], sums[:, 0, :], ALU.mult)
                link(v.tensor_tensor(arow[:, 2, :], arow[:, 2, :], sums[:, 1, :], ALU.mult))
                v.reduce_sum(heads[:, 0, :], arow[:, 0, :].rearrange("p (h o) -> p h o", h=HEADS), axis=AX.X)
                link(v.reduce_sum(heads[:, 1, :], arow[:, 2, :].rearrange("p (h o) -> p h o", h=HEADS), axis=AX.X))
                link(v.reduce_max(bound[:, 2:4], heads[:, :, :], axis=AX.X))
                v.wait_ge(worst_full, 1)
                link(v.reduce_max(bound[:, 4:6], bank[0][0:1, 0:2 * P].rearrange("p (b n) -> p b n", b=2), axis=AX.X))
                v.tensor_tensor(b[6], b[4], b[2], ALU.mult)
                link(v.scalar_tensor_tensor(b[7], b[1], b[4], b[0], ALU.mult, ALU.add))
                link(v.scalar_tensor_tensor(b[8], b[7], 1.0, b[3], ALU.add, ALU.mult))
                link(v.tensor_tensor(b[9], b[6], b[8], ALU.max))
                link(v.tensor_scalar(b[10], b[9], LOGIT_FACTOR, ROUNDING, ALU.mult, ALU.add))
                link(v.tensor_tensor(b[11], b[10], b[5], ALU.add))
                v.tensor_scalar(fast_flag[:, :], b[11], 0.0, None, ALU.is_lt).then_inc(flag_ready, 1)

            for step in att_order:
                g = int(step[1])
                if step[0] == "A":
                    for c in range(KC):
                        n = KC * g + c
                        v.wait_ge(l1_act, n + 1)
                        if g >= 2 and c == 0:
                            v.wait_ge(l2_full, TPG * (g - 1))
                        link(v.tensor_scalar(e1[:, n % 2, :], he[:, n % 2, :], 1.0, -1.0, ALU.min, ALU.add))
                        v.tensor_tensor(h1T[:, g % 2, c, :], e1[:, n % 2, :], hr[:, n % 2, :], ALU.add).then_inc(h1_ready, 1)
                elif step[0] == "B":
                    if g == 0:
                        stats0(0)
                        stats0(1)
                    elif g == 1:
                        stats0(2)
                        stats0(3)
                        smallest_gap()
                    elif g == GRAPHS - 1:
                        decide()

                    def first(n):
                        v.wait_ge(l2_full, n + 1)
                        if n >= 2:
                            v.wait_ge(x1_ready, n - 1)
                        v.tensor_tensor(sg[:, n % 2, :], bank[6 + n % 2][:, :], b1r[:, :], ALU.add).then_inc(z_ready, 1)

                    def second(n):
                        v.wait_ge(ez_ready, n + 1)
                        link(v.tensor_scalar(e1[:, n % 2, :], th[:, n % 2, :], 1.0, -1.0, ALU.min, ALU.add))
                        link(v.scalar_tensor_tensor(e1[:, n % 2, :], sg[:, n % 2, :], 0.0, e1[:, n % 2, :],
                                                    ALU.max, ALU.add))
                        v.tensor_tensor(xs[:, n, :], xs[:, n, :], e1[:, n % 2, :], ALU.add).then_inc(x1_ready, 1)

                    first(TPG * g)
                    for t in range(TPG):
                        if t + 1 < TPG:
                            first(TPG * g + t + 1)
                        second(TPG * g + t)
            v.wait_ge(x1_ready, TILES)
            unless_one_hot(v, slow_vector)
            for g in range(GRAPHS):
                s = slice(TPG * g, TPG * g + TPG)
                for t in range(TPG * g, TPG * g + TPG):
                    v.wait_ge(x1_ready, t + 1)
                    link(v.bn_stats(bn[:, t % 2, :], xs[:, t, :]))
                    link(v.bn_aggr(mv[:, t, :], bn[:, t % 2, :]))
                v.tensor_scalar(ve[:, s], mv[:, s, 1], EPS, None, ALU.add).then_inc(ve_ready, 1)
            for g in range(GRAPHS):
                s = slice(TPG * g, TPG * g + TPG)
                v.wait_ge(ve_ready, g + 1)
                v.wait_ge(pow_ready, g + 1)
                link(v.tensor_tensor(nt1[:, s], ve[:, s], r0[:, s], ALU.mult))
                link(v.tensor_tensor(nt1[:, s], nt1[:, s], r0[:, s], ALU.mult))
                link(v.tensor_scalar(nt1[:, s], nt1[:, s], -0.5, 1.5, ALU.mult, ALU.add))
                link(v.tensor_tensor(rstd[:, s], r0[:, s], nt1[:, s], ALU.mult))
                v.scalar_tensor_tensor(nmr[:, s], mv[:, s, 0], -1.0, rstd[:, s], ALU.mult,
                                       ALU.mult).then_inc(ln_ready, 1)

            def route(g):
                v.wait_ge(r_act, g + 1)
                if g:
                    v.wait_ge(wd_ready, g)
                if g == 0:
                    v.wait_ge(ld_eb, 16)
                    v.wait_ge(consts, 5)
                link(v.tensor_scalar(S[:, :, :], rth[:, g % 2, :, :], 0.5, 0.5, ALU.mult, ALU.add))
                link(v.tensor_tensor(SB[:, :, :], S[:, :, :], ebr[:, :].unsqueeze(1).to_broadcast([P, TPG, EXPERTS]), ALU.add))
                q = SB[:, :, :].rearrange("p t (g j) -> p t g j", j=GSIZE)
                a, b, c, d, m, n, top, gs = (rg[:, i, :, :] for i in range(8))
                v.tensor_tensor(a, q[:, :, :, 0], q[:, :, :, 1], ALU.max)
                v.tensor_tensor(b, q[:, :, :, 0], q[:, :, :, 1], ALU.min)
                v.tensor_tensor(c, q[:, :, :, 2], q[:, :, :, 3], ALU.max)
                link(v.tensor_tensor(d, q[:, :, :, 2], q[:, :, :, 3], ALU.min))
                v.tensor_tensor(m, a, c, ALU.min)
                v.tensor_tensor(n, b, d, ALU.max)
                link(v.tensor_tensor(top, a, c, ALU.max))
                link(v.tensor_tensor(m, m, n, ALU.max))
                link(v.tensor_tensor(gs, top, m, ALU.add))
                for t in range(TPG):
                    ins = v.max(rgm[:, t, :], rg[:, 7, t, :])
                link(ins)
                for t in range(TPG):
                    ins = v.max_index(rgi[:, t, :], rgm[:, t, :], rg[:, 7, t, :])
                link(ins)
                link(v.tensor_copy(rgf[:, :, :], rgi[:, :, :]))
                for k in range(TOP_GROUPS):
                    ins = v.tensor_tensor(rg[:, k, :, :], iota8[:, :, :],
                                          rgf[:, :, k:k + 1].to_broadcast([P, TPG, GROUPS]), ALU.is_equal)
                link(ins)
                link(v.tensor_tensor(rg[:, 3, :, :], rg[:, 0, :, :], rg[:, 1, :, :], ALU.add))
                link(v.tensor_tensor(rg[:, 4, :, :], rg[:, 3, :, :], rg[:, 2, :, :], ALU.add))
                link(v.tensor_tensor(q, q, rg[:, 4, :, :].unsqueeze(3).to_broadcast([P, TPG, GROUPS, GSIZE]), ALU.mult))
                for t in range(TPG):
                    ins = v.max(rgm[:, t, :], SB[:, t, :])
                link(ins)
                for t in range(TPG):
                    ins = v.max_index(rgi[:, t, :], rgm[:, t, :], SB[:, t, :])
                link(ins)
                link(v.tensor_copy(rgf[:, :, :], rgi[:, :, :]))
                for k in range(TOP_K):
                    ins = v.tensor_tensor(eq[:, k, :, :], iota32[:, :, :],
                                          rgf[:, :, k:k + 1].to_broadcast([P, TPG, EXPERTS]), ALU.is_equal)
                link(ins)
                link(v.tensor_tensor(eq[:, 0:2, :, :], eq[:, 0:2, :, :], eq[:, 2:4, :, :], ALU.add))
                so = sel[:, TPG * g:TPG * g + TPG, :]
                v.tensor_tensor(so, eq[:, 0, :, :], eq[:, 1, :, :], ALU.add).then_inc(sel_ready, 1)
                v.wait_ge(sel_ready, g + 1)
                link(v.tensor_tensor(S[:, :, :], S[:, :, :], so, ALU.mult))
                link(v.reduce_sum(den[:, :], S[:, :, :], axis=AX.X))
                link(v.tensor_scalar(den[:, :], den[:, :], 1e-20, None, ALU.add))
                link(v.reciprocal(den[:, :], den[:, :]))
                v.scalar_tensor_tensor(wd[:, TPG * g:TPG * g + TPG, :], S[:, :, :], SCALE,
                                       den[:, :].unsqueeze(2).to_broadcast([P, TPG, EXPERTS]), ALU.mult,
                                       ALU.mult).then_inc(wd_ready, 1)

            def gu(n):
                tb = n // KC
                v.wait_ge(gu_act, n + 1)
                if n % KC == 0 and tb >= 2:
                    v.wait_ge(d_full, TPG * (tb - 1))
                link(v.scalar_tensor_tensor(sg[:, n % 2, :], th[:, n % 2, :], 1.0, bank[2 + n % 2][:, :],
                                            ALU.add, ALU.mult))
                v.scalar_tensor_tensor(hT[:, tb % 2, n % KC, :], sg[:, n % 2, :], 0.5, bank[4 + n % 2][:, :],
                                       ALU.mult, ALU.mult).then_inc(hT_ready, 1)

            def down(n):
                v.wait_ge(d_full, n + 1)
                if n >= 2:
                    v.wait_ge(ob_stored[n % 2], 16 * (n // 2))
                v.tensor_tensor(ob[:, n % 2, :], bank[6 + n % 2][:, :], xs[:, n, :], ALU.add).then_inc(ob_ready, 1)

            top_steps = []

            def top(r, part):
                k8 = kk[:, 8 * r:8 * r + 8]
                if part == 0:
                    link(v.max(k8, key[:, :]))
                elif r + 1 < ROUNDS:
                    link(v.match_replace(key[:, :], k8, key[:, :], RETIRED))

            route(0)
            route(1)
            route(2)
            gu(0)
            gu(1)
            route(3)
            gu(2)
            gu(3)
            v.wait_ge(tp_free, G_SEL + GRAPHS)
            v.wait_ge(consts, 6)
            link(v.scalar_tensor_tensor(key[:, :], selT[:, :], float(TOKENS), key[:, :], ALU.mult, ALU.add))
            steps = [(r, part) for r in range(ROUNDS) for part in range(2)]
            for tb in range(1, GRAPHS):
                for n in range(KC * tb, KC * tb + KC):
                    gu(n)
                    if steps:
                        top(*steps.pop(0))
                for n in range(TPG * (tb - 1), TPG * tb):
                    down(n)
                    if steps:
                        top(*steps.pop(0))
            link(v.tensor_scalar(kt[:, :], kk[:, :], float(TOKENS), float(TOKENS), ALU.is_gt, ALU.mult))
            v.scalar_tensor_tensor(tokf[:, :], kt[:, :], float(TOKENS), kk[:, :], ALU.add,
                                   ALU.subtract).then_inc(tok_ready, 1)
            for n in range(3 * KC, 4 * KC):
                down(n)
            for e in range(EXPERTS):
                v.wait_ge(eg_act, e + 1)
                link(v.scalar_tensor_tensor(eh[:, e % 2, :], et[:, e % 2, :], 1.0, bank[2 + e % 2][:, 0:2 * CAP],
                                            ALU.add, ALU.mult))
                if e >= 2:
                    v.wait_ge(ey_full, e - 1)
                v.scalar_tensor_tensor(ehT[:, e % 2, :], eh[:, e % 2, :], 0.5, bank[2 + e % 2][:, 2 * CAP:4 * CAP],
                                       ALU.mult, ALU.mult).then_inc(eh_ready, 1)

        @block.tensor
        def _(pe):
            def group(n, parts):
                if n >= 2:
                    pe.wait_ge(tp_free, n - 1)
                for dst, src in parts:
                    k = src.shape[0]
                    last = pe.transpose(dst(bank[n % 2]), src, ident[0:k, 0:k])
                last.then_inc(tp_full, 1)

            pe.wait_ge(consts, 2)
            for i in range(3):
                pe.wait_ge(ld_sh[i], 16)
                for c in range(KC):
                    group(G_SHARED + KC * i + c,
                          [(lambda b, r=r: b[:, P * r:P * r + P], raw(i)[:, r, P * c:P * c + P]) for r in range(KC)])
            pe.wait_ge(ld_sh[3], 16)
            group(G_ROUTER, [(lambda b, c=c: b[:, EXPERTS * c:EXPERTS * c + EXPERTS], rwraw[:, P * c:P * c + P])
                             for c in range(KC)])
            pe.wait_ge(ld_att, 16 * 7)
            pe.wait_ge(ones_ready, 1)
            for c in range(KC):
                pe.wait_ge(absw_ready, c + 1)
                last = pe.matmul(bank[7][0:1, :], ones[:, 0:1], absw[:, c, :], start=(c == 0), stop=(c == KC - 1))
            last.then_inc(absw_used, 1)
            pe.wait_ge(absw_ready, KC + 1)
            pe.matmul(bank[6][0:1, :], ones[:, 0:1], absw[:, 0, :], start=True, stop=True).then_inc(sums_full, 1)
            for step in att_order:
                g = int(step[1])
                if step[0] == "T":
                    pe.wait_ge(ctxg_ready[g], 16 * TPG)
                    group(G_CTX + g, [(lambda b, t=t: b[:, P * t:P * t + P], ctxg[:, g % 2, t, :]) for t in range(TPG)])
                elif step[0] == "A":
                    pe.wait_ge(tp_free, G_CTX + g + 1)
                    for c in range(KC):
                        n = KC * g + c
                        if g:
                            pe.wait_ge(l1_act, n - KC + 1)
                        pe.matmul(bank[2 + c][:, :], w0[:, P * c:P * c + P], ctxT[:, g % 2, :],
                                  start=True, stop=True).then_inc(l1_full, 1)
                else:
                    pe.wait_ge(h1_ready, KC * (g + 1))
                    if g == 0:
                        pe.wait_ge(sums_ready, 1)
                    if g == GRAPHS - 1:
                        pe.wait_ge(worst_ready, 1)
                        pe.wait_ge(tp_free, G_CTX + GRAPHS)
                        for c in range(2):
                            last = pe.transpose(bank[0][0:1, P * c:P * c + P], worst[:, c:c + 1], ident[:, :])
                        last.then_inc(worst_full, 1)
                    for t in range(TPG):
                        n = TPG * g + t
                        if n >= 2:
                            pe.wait_ge(z_ready, n - 1)
                        for c in range(KC):
                            last = pe.matmul(bank[6 + n % 2][:, :], h1T[:, g % 2, c, P * t:P * t + P], w1[:, c, :],
                                             start=(c == 0), stop=(c == KC - 1))
                        last.then_inc(l2_full, 1)
            unless_one_hot(pe, slow_tensor)
            for g in range(GRAPHS):
                for t in range(TPG):
                    n = TPG * g + t
                    pe.wait_ge(xn_ready, n + 1)
                    group(G_XN + n, [(lambda b, c=c: b[:, P * c:P * c + P], xn[:, t, P * c:P * c + P])
                                     for c in range(KC)])
                if g == 0:
                    pe.wait_ge(z_ready, TILES)
                if g >= 2:
                    pe.wait_ge(r_act, g - 1)
                for t in range(TPG):
                    n = TPG * g + t
                    pe.wait_ge(tp_free, G_XN + n + 1)
                    for c in range(KC):
                        last = pe.matmul(bank[6 + g % 2][:, EXPERTS * t:EXPERTS * t + EXPERTS],
                                         xnT[:, c, P * n:P * n + P], rwT[:, c, :], start=(c == 0), stop=(c == KC - 1))
                last.then_inc(r_full, 1)

            def gu(n):
                tb, i = n // KC, n % KC
                if n >= 2:
                    pe.wait_ge(hT_ready, n - 1)
                for b, w in ((2, gT), (4, uT)):
                    for c in range(KC):
                        last = pe.matmul(bank[b + n % 2][:, :], w[:, c, P * i:P * i + P],
                                         xnT[:, c, SEQ * tb:SEQ * tb + SEQ], start=(c == 0), stop=(c == KC - 1))
                last.then_inc(gu_full, 1)

            def down(tb):
                pe.wait_ge(hT_ready, KC * (tb + 1))
                for t in range(TPG):
                    n = TPG * tb + t
                    if n >= 2:
                        pe.wait_ge(ob_ready, n - 1)
                    else:
                        pe.wait_ge(r_act, GRAPHS)
                    for c in range(KC):
                        last = pe.matmul(bank[6 + n % 2][:, :], hT[:, tb % 2, c, P * t:P * t + P], dT[:, c, :],
                                         start=(c == 0), stop=(c == KC - 1))
                    last.then_inc(d_full, 1)

            pe.wait_ge(l1_act, KC * GRAPHS)
            for n in range(KC):
                gu(n)
            for g in range(GRAPHS):
                pe.wait_ge(sel_ready, g + 1)
                group(G_SEL + g, [(lambda b, t=t: b[0:EXPERTS, P * t:P * t + P], sel[:, TPG * g + t, :])
                                  for t in range(TPG)])
            for tb in range(1, GRAPHS):
                for n in range(KC * tb, KC * tb + KC):
                    gu(n)
                down(tb - 1)
            pe.wait_ge(tok_ready, 1)
            group(G_TOK, [(lambda b: b[0:CAP, 0:EXPERTS], tokf[:, :])])
            down(GRAPHS - 1)

            def spread(e):
                pe.wait_ge(xg_ready[e % XRING], 16 * (e // XRING + 1))
                group(G_EXP + e, [(lambda b, c=c: b[:, CAP * c:CAP * c + CAP], xg[:, e % XRING, c:D:KC])
                                  for c in range(KC)])

            def mix(e):
                pe.wait_ge(tp_free, G_EXP + e + 1)
                pe.wait_ge(ld_w[(e + FIRST_SLOT) % RING], 48 * (e // RING + 1))
                if e >= 2:
                    pe.wait_ge(eh_ready, e - 1)
                else:
                    pe.wait_ge(hT_ready, 4 * KC)
                b = bank[2 + e % 2]
                for j, w in enumerate((ring_gate(e), ring_up(e))):
                    for i in range(IC):
                        at = CAP * (IC * j + i)
                        for c in range(KC):
                            last = pe.matmul(b[:, at:at + CAP], w[:, c, P * i:P * i + P], xgT[:, e % 3, c, :],
                                             start=(c == 0), stop=(c == KC - 1))
                last.then_inc(eg_full, 1)

            def project(e):
                pe.wait_ge(eh_ready, e + 1)
                if e >= 2:
                    pe.wait_ge(ey_ready, e - 1)
                else:
                    pe.wait_ge(ob_ready, TILES)
                for i in range(IC):
                    last = pe.matmul(bank[6 + e % 2][0:CAP, :], ehT[:, e % 2, CAP * i:CAP * i + CAP],
                                     ring_down(e)[:, i, :], start=(i == 0), stop=(i == IC - 1))
                last.then_inc(ey_full, 1)

            spread(0)
            for e in range(EXPERTS + 1):
                if e + 1 < EXPERTS:
                    spread(e + 1)
                if e < EXPERTS:
                    mix(e)
                if e:
                    project(e - 1)


_INS = ['x', 'ctx_512', 'L0_xattn_W0', 'L0_xattn_a_self0', 'L0_xattn_a_neigh0', 'L0_xattn_b0', 'L0_xattn_W1',
        'L0_xattn_a_self1', 'L0_xattn_a_neigh1', 'L0_xattn_b1', 'L0_ffn_router_w', 'L0_ffn_e_bias',
        'L0_ffn_W_gate', 'L0_ffn_W_up', 'L0_ffn_W_down', 'L0_ffn_shared_gate', 'L0_ffn_shared_up',
        'L0_ffn_shared_down']
_OUTS = [((GRAPHS, SEQ, D), 'float32')]


def kernel(**inputs):
    import numpy as _np
    import concourse.bacc as _bacc
    from concourse import mybir as _mybir
    from concourse.bass_utils import run_bass_kernel_spmd as _run

    nc = _bacc.Bacc("TRN2", target_bir_lowering=False, num_devices=1)
    arrays, args = {}, []
    for name in _INS:
        a = _np.ascontiguousarray(inputs[name])
        arrays[f"in_{name}_dram"] = a
        args.append(nc.dram_tensor(f"in_{name}_dram", a.shape, _mybir.dt.from_np(a.dtype), kind="ExternalInput").ap())
    for i, (shape, dtype) in enumerate(_OUTS):
        dt = _mybir.dt.from_np(_np.dtype(dtype))
        args.append(nc.dram_tensor(f"out_{i}_dram", shape, dt, kind="ExternalOutput").ap())
    xattn_moe(nc, *args)
    r = _run(nc, [arrays], core_ids=[0])
    return r.results[0]["out_0_dram"]
```

```python
import concourse.bass as bass
from concourse import mybir
from contextlib import ExitStack

GRAPHS, SEQ, D = 4, 512, 512
P = 128
TPG = SEQ // P
TILES = GRAPHS * TPG
TOKENS = GRAPHS * SEQ
F_IN, HEADS, F_OUT = 128, 8, 64
F_HID = HEADS * F_OUT
KC = D // P
EXPERTS, GROUPS, GSIZE, TOP_GROUPS, TOP_K = 32, 8, 4, 3, 4
INNER = 256
IC = INNER // P
CAP = 80
ROW = D + EXPERTS
SCALE = 2.5
EPS = 1e-5
MASK = -1e10
SLOPE = 0.2
RING = 4
FIRST_SLOT = 3
XRING = 7
AHEAD = 5
ROUNDS = CAP // 8
RETIRED = -1.0
LOGIT_FACTOR = 4.1
ROUNDING = 40000.0


def xattn_moe(nc, x, ctx_in, W0, a_self0, a_neigh0, b0, W1, a_self1, a_neigh1, b1,
              router_w, e_bias, W_gate, W_up, W_down, shared_gate, shared_up, shared_down, out):
    f32, u32 = mybir.dt.float32, mybir.dt.uint32
    ALU = mybir.AluOpType
    ACT = mybir.ActivationFunctionType
    AX = mybir.AxisListType

    x_rows = x.rearrange("g s d -> (g s) d")
    out_rows = out.rearrange("g s d -> (g s) d")
    ctx_rows = ctx_in.rearrange("g s f -> (g s) f")
    idx_dram = nc.dram_tensor("idx_dram", (TOKENS, 1), u32).ap()
    rows_dram = nc.dram_tensor("rows_dram", (TOKENS, ROW), f32).ap()

    es = ExitStack()
    with es:
        def sb(name, shape, dt=f32):
            return es.enter_context(nc.sbuf_tensor(name, shape, dt))

        def sem(name):
            return es.enter_context(nc.semaphore(name))

        ident = sb("ident", [P, P])
        ones = sb("ones", [P, P])
        xs = sb("xs", [P, TILES, D])
        xnT = sb("xnT", [P, KC, TOKENS])
        w0 = sb("w0", [P, F_HID])
        w1 = sb("w1", [P, KC, F_HID])
        b0c = sb("b0c", [P, KC])
        b1r = sb("b1r", [P, F_HID])
        ebr = sb("ebr", [P, EXPERTS])
        ring = sb("ring", [P, RING, 3072])
        gT = sb("gT", [P, KC, D])
        uT = sb("uT", [P, KC, D])
        ob = xs[:, 0:2 * TPG, :].rearrange("p (b t) d -> p b t d", b=2)
        late = xs[0:CAP, 2 * TPG:TILES, :].rearrange("p t d -> p (t d)")
        xg = late[:, 0:XRING * ROW].rearrange("p (b r) -> p b r", b=XRING)
        dT = sb("dT", [P, KC, D])
        rwraw = sb("rwraw", [EXPERTS, D])
        rwT = sb("rwT", [P, KC, EXPERTS])
        mx = sb("mx", [P, TILES, 8])
        ix = sb("ix", [P, TILES, 8], u32)
        ixg = sb("ixg", [P, TILES], u32)
        ix2 = sb("ix2", [P, TILES], u32)
        ctx_buf = sb("ctx_buf", [P, 4, SEQ])
        ctxg = ctx_buf[:, 0:2, :].rearrange("p b (t f) -> p b t f", f=F_IN)
        ctxT = ctx_buf[:, 2:4, :]
        h1T = sb("h1T", [P, 2, KC, SEQ])
        he = sb("he", [P, 2, SEQ])
        e1r = sb("e1r", [P, 4, SEQ])
        e1, hr = e1r[:, 0:2, :], e1r[:, 2:4, :]
        bn0 = sb("bn0", [P, 2, 6])
        bn = sb("bn", [P, TPG, 6])
        minus_one = sb("minus_one", [P, 1])
        mv = sb("mv", [P, TILES, 2])
        ve = sb("ve", [P, TILES])
        half = sb("half", [P, TILES])
        r0 = sb("r0", [P, TILES])
        nt1 = sb("nt1", [P, TILES])
        rstd = sb("rstd", [P, TILES])
        nmr = sb("nmr", [P, TILES])
        xn = [ctx_buf, h1T[:, 1, :, :]]
        hT = h1T
        th = sb("th", [P, 2, SEQ])
        sg = sb("sg", [P, 2, SEQ])
        selT = e1r[0:EXPERTS, :, :].rearrange("p a b -> p (a b)")
        key = ctx_buf[0:EXPERTS, :, :].rearrange("p a b -> p (a b)")
        ey = ctx_buf[0:CAP, 0:3, :]
        kk = sb("kk", [EXPERTS, CAP])
        kt = sb("kt", [EXPERTS, CAP])
        tokf = sb("tokf", [EXPERTS, CAP])
        tok = sb("tok", [CAP, EXPERTS], u32)
        rth = sb("rth", [P, 2, TPG, EXPERTS])
        at = [0]

        def in_w1(*dims):
            n = 1
            for k in dims:
                n *= k
            at[0] += n
            names = "abcd"[:len(dims)]
            v = w1[:, :, :].rearrange("p c n -> p (c n)")[:, at[0] - n:at[0]]
            return v.rearrange(f"p ({' '.join(names)}) -> p {' '.join(names)}", **dict(zip(names, dims)))

        S = in_w1(TPG, EXPERTS)
        SB = in_w1(TPG, EXPERTS)
        rg = in_w1(8, TPG, GROUPS)
        rgi = sb("rgi", [P, TPG, 8], u32)
        rgm = sb("rgm", [P, TPG, 8])
        rgf = sb("rgf", [P, TPG, 8])
        eq = in_w1(TOP_K, TPG, EXPERTS)
        sel = in_w1(TILES, EXPERTS)
        den = sb("den", [P, TPG])
        wd = in_w1(TILES, EXPERTS)
        iota8 = sb("iota8", [P, TPG, GROUPS])
        iota32 = sb("iota32", [P, TPG, EXPERTS])
        flat = e1r[:, :, :].rearrange("p a b -> p (a b)")
        xgT = flat[:, 0:3 * KC * CAP].rearrange("p (b c n) -> p b c n", b=3, c=KC)
        ehT = flat[:, 3 * KC * CAP:3 * KC * CAP + 4 * CAP].rearrange("p (b n) -> p b n", b=2)

        bank = [es.enter_context(nc.psum_tensor(f"bank{i}", [P, 512], f32)) for i in range(8)]

        ld_x = [sem(f"ld_x{g}") for g in range(GRAPHS)]
        ld_sh = [sem(f"ld_sh{i}") for i in range(4)]
        ld_att = sem("ld_att")
        ld_eb = sem("ld_eb")
        ld_w = [sem(f"ld_w{i}") for i in range(RING)]
        consts = sem("consts")
        top_done, idx_done, idxg_ready = sem("top_done"), sem("idx_done"), sem("idxg_ready")
        idx_stored = [sem(f"idx_stored{g}") for g in range(GRAPHS)]
        idx2_ready = [sem(f"idx2_ready{g}") for g in range(GRAPHS)]
        ctxg_ready = [sem(f"ctxg_ready{g}") for g in range(GRAPHS)]
        tp_full, tp_free = sem("tp_full"), sem("tp_free")
        l1_full, l1_act, h1_ready = sem("l1_full"), sem("l1_act"), sem("h1_ready")
        l2_full, z_ready, ez_ready, x1_ready = sem("l2_full"), sem("z_ready"), sem("ez_ready"), sem("x1_ready")
        dve = sem("dve")
        ones_ready, bn_done = sem("ones_ready"), sem("bn_done")
        ve_ready, pow_ready, ln_ready, xn_ready = sem("ve_ready"), sem("pow_ready"), sem("ln_ready"), sem("xn_ready")
        rows_x, rows_w = [sem("rows_x0"), sem("rows_x1")], sem("rows_w")
        r_full, r_act, sel_ready, wd_ready = sem("r_full"), sem("r_act"), sem("sel_ready"), sem("wd_ready")
        x1_stored = sem("x1_stored")
        gu_full, gu_act, h_ready = sem("gu_full"), sem("gu_act"), sem("h_ready")
        y_full, y_ready = sem("y_full"), sem("y_ready")
        tok_ready = sem("tok_ready")
        xg_ready = [sem(f"xg_ready{i}") for i in range(XRING)]
        added = sem("added")

        att_order = ["W0", "T0", "A0", "W1", "T1", "A1", "W2", "R0", "S0", "B0", "T2", "A2", "B1", "T3", "A3", "B2", "B3"]
        G_STEP, G_XN = {}, 0
        for step in att_order:
            G_STEP[step] = G_XN
            G_XN += {"W": KC, "R": 1, "T": 1}.get(step[0], 0)
        G_X, G_L, n = {}, {}, G_XN
        for step in ("X0", "X1", "L0", "X2", "L1", "X3", "L2", "L3"):
            (G_X if step[0] == "X" else G_L)[int(step[1])] = n
            n += TPG if step[0] == "X" else 1
        G_SEL = n
        G_TOK = G_SEL + GRAPHS
        G_EXP = G_TOK + 1

        first_part = [("S", 0), ("S", 1), ("K", 0)] + [("S", n) for n in range(2, 2 * KC)] + [("D", n) for n in range(TPG)]
        shared_rest = []
        for g in range(1, GRAPHS):
            if g + 1 < GRAPHS:
                shared_rest += [("S", n) for n in range(KC * (g + 1), KC * (g + 2))]
            shared_rest += [("D", n) for n in range(TPG * g, TPG * (g + 1))]
        weight = {"S": 2, "D": 1}
        total, spent = sum(weight[k] for k, n in shared_rest), 0
        mixed_part = []
        for e in range(EXPERTS):
            mixed_part.append(("E", e))
            while shared_rest and spent + weight[shared_rest[0][0]] <= total * (e + 1) / EXPERTS:
                spent += weight[shared_rest[0][0]]
                mixed_part.append(shared_rest.pop(0))
            if e:
                mixed_part.append(("Y", e - 1))
        mixed_part += shared_rest + [("Y", EXPERTS - 1)]
        units = first_part + mixed_part
        hidden_no = {u: i for i, u in enumerate(u for u in units if u[0] in "SE")}
        output_no = {u: i for i, u in enumerate(u for u in units if u[0] in "DY")}
        adds = [u for u in units if u[0] == "Y" or u[0] == "D" and u[1] % TPG == TPG - 1]
        add_no = {u: i for i, u in enumerate(adds)}

        def ring_gate(e):
            return ring[:, (e + FIRST_SLOT) % RING, 0:1024].rearrange("p (c i) -> p c i", c=KC)

        def ring_up(e):
            return ring[:, (e + FIRST_SLOT) % RING, 1024:2048].rearrange("p (c i) -> p c i", c=KC)

        def ring_down(e):
            return ring[:, (e + FIRST_SLOT) % RING, 2048:3072].rearrange("p (c d) -> p c d", c=IC)

        def raw(i):
            return ring[:, i, 0:2048].rearrange("p (c k) -> p c k", c=KC)

        room = xnT[:, :, :].rearrange("p c n -> p (c n)")
        ctx_all = room[:, 0:TOKENS]
        absw = room[:, 2048:2048 + 5 * D].rearrange("p (b n) -> p b n", b=KC + 1)
        arow = sb("arow", [P, 2, 2, KC])
        sums = sb("sums", [P, 2, KC])
        prod = sb("prod", [P, 2, KC])
        mv0 = sb("mv0", [P, TILES, 2])
        chk = sb("chk", [P, 4, TILES, 2])
        worst4 = sb("worst4", [P, 4])
        worst = sb("worst", [P, 4])
        bound = sb("bound", [1, 16])
        fast_flag = sb("fast_flag", [1, 1], u32)
        ld_chk, absw_ready, sums_full = sem("ld_chk"), sem("absw_ready"), sem("sums_full")
        worst4_ready = sem("worst4_ready")
        sums_ready, var0_ready, pow0_ready, worst_ready = sem("sums_ready"), sem("var0_ready"), sem("pow0_ready"), sem("worst_ready")
        worst_full, flag_ready = sem("worst_full"), sem("flag_ready")

        mask_dram = nc.dram_tensor("mask_dram", (TOKENS, SEQ), f32).ap()
        feat_dram = nc.dram_tensor("feat_dram", (TOKENS, F_HID), f32).ap()
        sn_dram = nc.dram_tensor("sn_dram", (2 * HEADS, TOKENS), f32).ap()
        hid_dram = [nc.dram_tensor(f"hid_dram{i}", (TOKENS, F_HID), f32).ap() for i in range(2)]
        g_x = room[:, 0:D]
        g_xT = room[:, D:2 * D].rearrange("p (c n) -> p c n", c=KC)
        g_a = room[:, 2 * D:4 * D].rearrange("p (b n) -> p b n", b=2)
        g_feat = room[:, 4 * D:5 * D]
        g_tmp = room[:, 5 * D:6 * D]
        g_mask = room[:, 6 * D:7 * D]
        g_neigh = room[:, 7 * D:8 * D]
        g_e = room[:, 8 * D:9 * D]
        g_p = room[:, 9 * D:10 * D]
        g_pT = room[:, 10 * D:11 * D]
        g_f = room[:, 11 * D:11 * D + KC * F_OUT].rearrange("p (c o) -> p c o", c=KC)
        g_b, g_xp, g_z, g_ez, g_h = (room[:, 12 * D + F_OUT * i:12 * D + F_OUT * i + F_OUT] for i in range(5))
        g_sn = room[:, 13 * D:13 * D + 2 * HEADS]
        g_snT = room[0:2 * HEADS, 13 * D + 32:13 * D + 32 + P]
        g_self, g_max, g_sum, g_ve, g_r0, g_r = (room[:, 14 * D + i:14 * D + i + 1] for i in range(6))
        g_bn = room[:, 14 * D + 16:14 * D + 22]
        g_bn2 = room[:, 14 * D + 32:14 * D + 32 + 6 * TILES].rearrange("p (t b) -> p t b", t=TILES)
        g_mv = room[:, 14 * D + 24:14 * D + 26]
        g_load, g_const, g_store, g_done = sem("g_load"), sem("g_const"), sem("g_store"), sem("g_done")
        g_held, g_ln = sem("g_held"), sem("g_ln")
        g_pe, g_act, g_dve, g_pool = sem("g_pe"), sem("g_act"), sem("g_dve"), sem("g_pool")
        a_pair = [(a_self0, a_neigh0, b0), (a_self1, a_neigh1, b1)]

        block = es.enter_context(nc.Block())

        DVE_M, ACT_F, PE_F, DVE_F, PE_S, ACT_S, DVE_S = 10, 2, 3, 5, 2, 4, 8
        S_ROUNDS = TILES * HEADS
        DVE_PASSES = TILES * DVE_M + 2 * (TILES * DVE_F + S_ROUNDS * DVE_S)

        def held(eng, what, value):
            eng.wait_ge(what, value)
            eng.sem_inc(g_held)

        def slow_sync(sp):
            loads = stores = consts_in = 0
            with sp.Fori(0, TILES) as i:
                sp.dma_start(g_x, x_rows[bass.ds(i * P, P), :]).then_inc(g_load, 16)
                held(sp, g_dve, i * DVE_M + DVE_M)
                sp.dma_start(mask_dram[bass.ds(i * P, P), :], g_e).then_inc(g_store, 16)
                held(sp, g_store, i * 16 + 16)
            dve, loads, stores, act, pe = TILES * DVE_M, TILES * 16, TILES * 16, 0, 0
            for layer in range(2):
                sp.dma_start(g_a[:, 0, :], a_pair[layer][0].rearrange("h o -> (h o)").partition_broadcast(P)).then_inc(g_const, 16)
                sp.dma_start(g_a[:, 1, :], a_pair[layer][1].rearrange("h o -> (h o)").partition_broadcast(P)).then_inc(g_const, 16)
                with sp.Fori(0, TILES) as i:
                    src = ctx_rows if layer == 0 else hid_dram[0]
                    sp.dma_start(g_x[:, 0:src.shape[1]], src[bass.ds(i * P, P), :]).then_inc(g_load, 16)
                    held(sp, g_act, i * ACT_F + (act + ACT_F))
                    sp.dma_start(sn_dram[:, bass.ds(i * P, P)], g_snT).then_inc(g_store, 16)
                    sp.dma_start(feat_dram[bass.ds(i * P, P), :], g_feat).then_inc(g_store, 16)
                    held(sp, g_store, i * 32 + (stores + 32))
                act, dve, loads, stores = act + TILES * ACT_F, dve + TILES * DVE_F, loads + TILES * 16, stores + TILES * 32
                with sp.Fori(0, GRAPHS) as g:
                    with sp.Fori(0, TPG) as t:
                        with sp.Fori(0, HEADS) as h:
                            i = g * (TPG * HEADS) + t * HEADS + h
                            rows = g * SEQ + t * P
                            sp.dma_start(g_mask, mask_dram[bass.ds(rows, P), :]).then_inc(g_load, 16)
                            sp.dma_start(g_neigh, sn_dram[bass.ds(h + HEADS, 1), bass.ds(g * SEQ, SEQ)]
                                         .to_broadcast([P, SEQ])).then_inc(g_load, 16)
                            sp.dma_start(g_self, sn_dram[bass.ds(h, 1), bass.ds(rows, P)].rearrange("a p -> p a"),
                                         allow_slow_non_contiguous=True).then_inc(g_load, 16)
                            sp.dma_start(g_f, feat_dram[bass.ds(g * SEQ, SEQ), bass.ds(h * F_OUT, F_OUT)]
                                         .rearrange("(c p) o -> p c o", p=P)).then_inc(g_load, 16)
                            sp.dma_start(g_b, a_pair[layer][2][bass.ds(h, 1), :].to_broadcast([P, F_OUT])).then_inc(g_load, 16)
                            sp.dma_start(g_xp, x_rows[bass.ds(rows, P), bass.ds(h * F_OUT, F_OUT)]).then_inc(g_load, 16)
                            held(sp, g_dve, i * DVE_S + (dve + DVE_S))
                            sp.dma_start(hid_dram[layer][bass.ds(rows, P), bass.ds(h * F_OUT, F_OUT)], g_h).then_inc(g_store, 16)
                            held(sp, g_store, i * 16 + (stores + 16))
                act, dve, loads, stores = act + S_ROUNDS * ACT_S, dve + S_ROUNDS * DVE_S, loads + S_ROUNDS * 96, stores + S_ROUNDS * 16
            for g in range(GRAPHS):
                sp.dma_start(xs[:, TPG * g:TPG * g + TPG, :],
                             hid_dram[1][SEQ * g:SEQ * g + SEQ, :].rearrange("(p t) d -> p t d", p=P)).then_inc(g_done, 16)
            sp.wait_ge(g_done, 16 * GRAPHS)

        def slow_pool(pool):
            with pool.Fori(0, TILES) as i:
                pool.wait_ge(g_dve, i * DVE_M + 3)
                nc.gpsimd.tensor_tensor(g_r0, g_ve, half[:, 0:1], ALU.pow).then_inc(g_pool, 1)
            pool.wait_ge(g_dve, DVE_PASSES + 3)
            nc.gpsimd.tensor_tensor(r0[:, :], ve[:, :], half[:, :], ALU.pow).then_inc(g_pool, 1)

        def slow_vector(v):
            def step(ins, n):
                ins.then_inc(g_dve, 1)
                held(v, g_dve, n)

            with v.Fori(0, TILES) as i:
                n = i * DVE_M
                v.wait_ge(g_load, i * 16 + 16)
                step(v.bn_stats(g_bn, g_x), n + 1)
                step(v.bn_aggr(g_mv, g_bn), n + 2)
                step(v.tensor_scalar(g_ve, g_mv[:, 1:2], EPS, None, ALU.add), n + 3)
                v.wait_ge(g_pool, i + 1)
                step(v.tensor_tensor(g_r, g_ve, g_r0, ALU.mult), n + 4)
                step(v.tensor_tensor(g_r, g_r, g_r0, ALU.mult), n + 5)
                step(v.tensor_scalar(g_r, g_r, -0.5, 1.5, ALU.mult, ALU.add), n + 6)
                step(v.tensor_tensor(g_r, g_r, g_r0, ALU.mult), n + 7)
                step(v.tensor_scalar(g_tmp, g_x, g_mv[:, 0:1], g_r, ALU.subtract, ALU.mult), n + 8)
                step(v.tensor_scalar(g_p, g_tmp, -1.0, 1.0, ALU.mult, ALU.add), n + 9)
                step(v.tensor_scalar(g_e, g_p, MASK, None, ALU.mult), n + 10)
            dve, loads, act, pe = TILES * DVE_M, TILES * 16, 0, 0
            for layer in range(2):
                v.wait_ge(g_const, 32 * (layer + 1))
                with v.Fori(0, TILES) as i:
                    n = i * DVE_F + dve
                    v.wait_ge(g_pe, i * PE_F + (pe + 2))
                    step(v.tensor_copy(g_feat, bank[1][:, :]), n + 1)
                    step(v.tensor_tensor(g_tmp, g_feat, g_a[:, 0, :], ALU.mult), n + 2)
                    step(v.reduce_sum(g_sn[:, 0:HEADS], g_tmp.rearrange("p (h o) -> p h o", h=HEADS), axis=AX.X), n + 3)
                    step(v.tensor_tensor(g_tmp, g_feat, g_a[:, 1, :], ALU.mult), n + 4)
                    step(v.reduce_sum(g_sn[:, HEADS:2 * HEADS], g_tmp.rearrange("p (h o) -> p h o", h=HEADS), axis=AX.X), n + 5)
                dve, pe, act, loads = dve + TILES * DVE_F, pe + TILES * PE_F, act + TILES * ACT_F, loads + TILES * 16
                with v.Fori(0, S_ROUNDS) as i:
                    n = i * DVE_S + dve
                    v.wait_ge(g_load, i * 96 + (loads + 96))
                    v.wait_ge(g_act, i * ACT_S + (act + 1))
                    step(v.scalar_tensor_tensor(g_p, g_e, SLOPE, g_e, ALU.mult, ALU.max), n + 1)
                    step(v.tensor_tensor(g_e, g_p, g_mask, ALU.add), n + 2)
                    step(v.reduce_max(g_max, g_e, axis=AX.X), n + 3)
                    step(v.tensor_scalar(g_max, g_max, -1.0, None, ALU.mult), n + 4)
                    v.wait_ge(g_act, i * ACT_S + (act + 2))
                    step(v.reciprocal(g_sum, g_sum), n + 5)
                    v.wait_ge(g_pe, i * PE_S + (pe + 2))
                    step(v.scalar_tensor_tensor(g_z, bank[1][:, 0:F_OUT], g_sum, g_b, ALU.mult, ALU.add), n + 6)
                    v.wait_ge(g_act, i * ACT_S + (act + 4))
                    step(v.tensor_scalar(g_ez, g_ez, 1.0, -1.0, ALU.min, ALU.add), n + 7)
                    if layer == 0:
                        step(v.scalar_tensor_tensor(g_h, g_z, 0.0, g_ez, ALU.max, ALU.add), n + 8)
                    else:
                        v.scalar_tensor_tensor(g_ez, g_z, 0.0, g_ez, ALU.max, ALU.add).then_inc(g_pool, 1)
                        v.wait_ge(g_pool, i + (TILES + 1))
                        step(v.tensor_tensor(g_h, g_ez, g_xp, ALU.add), n + 8)
                dve, pe, act, loads = dve + S_ROUNDS * DVE_S, pe + S_ROUNDS * PE_S, act + S_ROUNDS * ACT_S, loads + S_ROUNDS * 96
            v.wait_ge(g_done, 16 * GRAPHS)
            n = DVE_PASSES
            for t in range(TILES):
                ins = v.bn_stats(g_bn2[:, t, :], xs[:, t, :])
            step(ins, n + 1)
            for t in range(TILES):
                ins = v.bn_aggr(mv[:, t, :], g_bn2[:, t, :])
            step(ins, n + 2)
            step(v.tensor_scalar(ve[:, :], mv[:, :, 1], EPS, None, ALU.add), n + 3)
            v.wait_ge(g_pool, TILES + S_ROUNDS + 1)
            step(v.tensor_tensor(nt1[:, :], ve[:, :], r0[:, :], ALU.mult), n + 4)
            step(v.tensor_tensor(nt1[:, :], nt1[:, :], r0[:, :], ALU.mult), n + 5)
            step(v.tensor_scalar(nt1[:, :], nt1[:, :], -0.5, 1.5, ALU.mult, ALU.add), n + 6)
            step(v.tensor_tensor(rstd[:, :], r0[:, :], nt1[:, :], ALU.mult), n + 7)
            v.scalar_tensor_tensor(nmr[:, :], mv[:, :, 0], -1.0, rstd[:, :], ALU.mult, ALU.mult).then_inc(g_ln, 1)

        def slow_scalar(act_e):
            act, pe, dve, loads = 0, 0, TILES * DVE_M, TILES * 16
            for layer in range(2):
                kc = 1 if layer == 0 else KC
                with act_e.Fori(0, TILES) as i:
                    act_e.wait_ge(g_pe, i * PE_F + (pe + 1))
                    act_e.activation(g_xT[:, 0:kc, :], bank[0][:, 0:kc * P].rearrange("p (c n) -> p c n", c=kc), ACT.Copy).then_inc(g_act, 1)
                    act_e.wait_ge(g_pe, i * PE_F + (pe + 3))
                    act_e.activation(g_snT, bank[0][0:2 * HEADS, 0:P], ACT.Copy).then_inc(g_act, 1)
                dve, pe, act, loads = dve + TILES * DVE_F, pe + TILES * PE_F, act + TILES * ACT_F, loads + TILES * 16
                with act_e.Fori(0, S_ROUNDS) as i:
                    act_e.wait_ge(g_load, i * 96 + (loads + 96))
                    act_e.activation(g_e, g_neigh, ACT.Identity, bias=g_self).then_inc(g_act, 1)
                    act_e.wait_ge(g_dve, i * DVE_S + (dve + 4))
                    act_e.activation(g_tmp, g_e, ACT.Exp, bias=g_max, accum_out=g_sum).then_inc(g_act, 1)
                    act_e.wait_ge(g_pe, i * PE_S + (pe + 1))
                    act_e.activation(g_pT, bank[0][:, :], ACT.Copy).then_inc(g_act, 1)
                    act_e.wait_ge(g_dve, i * DVE_S + (dve + 6))
                    act_e.activation(g_ez, g_z, ACT.Exp).then_inc(g_act, 1)
                dve, pe, act, loads = dve + S_ROUNDS * DVE_S, pe + S_ROUNDS * PE_S, act + S_ROUNDS * ACT_S, loads + S_ROUNDS * 96

            act_e.wait_ge(g_ln, 1)

        def slow_tensor(pe_e):
            act, pe, dve, loads = 0, 0, TILES * DVE_M, TILES * 16
            for layer in range(2):
                kc = 1 if layer == 0 else KC
                w = w0[:, :].unsqueeze(1) if layer == 0 else w1
                with pe_e.Fori(0, TILES) as i:
                    pe_e.wait_ge(g_load, i * 16 + (loads + 16))
                    for c in range(kc):
                        last = pe_e.transpose(bank[0][:, P * c:P * c + P], g_x[:, P * c:P * c + P], ident[:, :])
                    last.then_inc(g_pe, 1)
                    pe_e.wait_ge(g_act, i * ACT_F + (act + 1))
                    for c in range(kc):
                        last = pe_e.matmul(bank[1][:, :], g_xT[:, c, :], w[:, c, :], start=(c == 0), stop=(c == kc - 1))
                    last.then_inc(g_pe, 1)
                    pe_e.wait_ge(g_dve, i * DVE_F + (dve + DVE_F))
                    pe_e.transpose(bank[0][0:2 * HEADS, 0:P], g_sn, ident[:, :]).then_inc(g_pe, 1)
                dve, act, loads = dve + TILES * DVE_F, act + TILES * ACT_F, loads + TILES * 16
                with pe_e.Fori(0, S_ROUNDS) as i:
                    pe_e.wait_ge(g_act, i * ACT_S + (act + 2))
                    for c in range(KC):
                        last = pe_e.transpose(bank[0][:, P * c:P * c + P], g_tmp[:, P * c:P * c + P], ident[:, :])
                    last.then_inc(g_pe, 1)
                    pe_e.wait_ge(g_act, i * ACT_S + (act + 3))
                    for c in range(KC):
                        last = pe_e.matmul(bank[1][:, 0:F_OUT], g_pT[:, P * c:P * c + P], g_f[:, c, :],
                                           start=(c == 0), stop=(c == KC - 1))
                    last.then_inc(g_pe, 1)
                dve, act, loads = dve + S_ROUNDS * DVE_S, act + S_ROUNDS * ACT_S, loads + S_ROUNDS * 96

        def unless_one_hot(eng, slow=None):
            eng.wait_ge(flag_ready, 1)
            one_hot = eng.value_load(fast_flag[0:1, 0:1], min_val=0, max_val=1)
            with eng.If(one_hot == 0):
                slow(eng)
            with eng.Else():
                eng.nop()

        @block.sync
        def _(sp):
            def load_x(g):
                sp.dma_start(xs[:, TPG * g:TPG * g + TPG, :],
                             x[g].rearrange("(p t) d -> p t d", p=P)).then_inc(ld_x[g], 16)

            def load_raw(i):
                w = (None, shared_up, shared_down)[i].rearrange("(c p) k -> p c k", p=P)
                for c in range(KC):
                    sp.dma_start(raw(i)[:, c, :], w[:, c, :]).then_inc(ld_sh[i], 16)

            def store_idx(g):
                sp.wait_ge(idxg_ready, g + 1)
                sp.dma_start(idx_dram[SEQ * g:SEQ * g + SEQ, :].rearrange("(p t) o -> p (t o)", p=P),
                             ixg[:, TPG * g:TPG * g + TPG]).then_inc(idx_stored[g], 16)

            def load_expert(e):
                s = (e + FIRST_SLOT) % RING
                sp.dma_start(ring_gate(e), W_gate[e].rearrange("(p c) i -> p c i", c=KC)).then_inc(ld_w[s], 16)
                sp.dma_start(ring_up(e), W_up[e].rearrange("(p c) i -> p c i", c=KC)).then_inc(ld_w[s], 16)
                sp.dma_start(ring_down(e), W_down[e].rearrange("(c p) d -> p c d", p=P)).then_inc(ld_w[s], 16)

            load_x(0)
            load_x(1)
            store_idx(0)
            load_x(2)
            store_idx(1)
            load_x(3)
            store_idx(2)
            for c in range(KC):
                sp.dma_start(w1[:, c, :].rearrange("f (h o) -> f h o", h=HEADS),
                             W1[:, P * c:P * c + P, :].rearrange("h f o -> f h o")).then_inc(ld_att, 16)
            store_idx(3)
            sp.dma_start(b1r[:, :], b1.rearrange("h o -> (h o)").partition_broadcast(P)).then_inc(ld_att, 16)
            load_raw(1)
            load_raw(2)
            sp.dma_start(rwraw[:, :], router_w).then_inc(ld_sh[3], 16)
            sp.dma_start(ebr[:, :], e_bias.partition_broadcast(P)).then_inc(ld_eb, 16)
            for i, a in enumerate((a_self0, a_neigh0, a_self1, a_neigh1)):
                sp.dma_start(arow[:, i // 2, i % 2, :], a.rearrange("h o -> (h o)").rearrange("(c p) -> p c", p=P),
                             allow_slow_non_contiguous=True).then_inc(ld_chk, 16)
            for g in range(GRAPHS):
                sp.dma_start(ctx_all[:, D * g:D * g + D].rearrange("p (t f) -> p t f", f=F_IN),
                             ctx_in[g].rearrange("(p t) f -> p t f", p=P)).then_inc(ld_chk, 16)
            sp.wait_ge(ctxg_ready[GRAPHS - 1], 16 * TPG)
            for e in range(RING - FIRST_SLOT):
                load_expert(e)
            for e in range(RING - FIRST_SLOT, RING):
                sp.wait_ge(tp_full, G_STEP[f"W{(e + FIRST_SLOT) % RING}"] + KC)
                load_expert(e)
            sp.wait_ge(x1_ready, TILES)
            unless_one_hot(sp, slow_sync)
            for g in range(GRAPHS):
                sp.wait_ge(xn_ready, TPG * (g + 1))
                sp.dma_start(rows_dram[SEQ * g:SEQ * g + SEQ, 0:D].rearrange("(p t) d -> p t d", p=P),
                             xn[g % 2][:, :, :]).then_inc(rows_x[g % 2], 16)
            for g in range(GRAPHS):
                sp.dma_start(out[g].rearrange("(p t) d -> p t d", p=P),
                             xs[:, TPG * g:TPG * g + TPG, :]).then_inc(x1_stored, 16)
            for g in range(GRAPHS):
                sp.wait_ge(wd_ready, g + 1)
                sp.dma_start(rows_dram[SEQ * g:SEQ * g + SEQ, D:ROW].rearrange("(p t) e -> p t e", p=P),
                             wd[:, TPG * g:TPG * g + TPG, :]).then_inc(rows_w, 16)
            for e in range(RING, EXPERTS):
                sp.wait_ge(y_full, output_no["Y", e - RING] + 1)
                load_expert(e)

        @block.gpsimd
        def _(pool):
            pool.memset(ident[:, :], 0.0).then_inc(consts, 1)
            pool.wait_ge(consts, 1)
            pool.affine_select(out=ident[:, :], in_=ident[:, :], compare_op=ALU.not_equal, fill=1.0,
                               base=0, pattern=[[-1, P]], channel_multiplier=1).then_inc(consts, 1)
            pool.iota(iota8[:, :, :], [[0, TPG], [1, GROUPS]], base=0, channel_multiplier=0,
                      allow_small_or_imprecise_dtypes=True).then_inc(consts, 1)
            pool.iota(iota32[:, :, :], [[0, TPG], [1, EXPERTS]], base=0, channel_multiplier=0,
                      allow_small_or_imprecise_dtypes=True).then_inc(consts, 1)
            pool.memset(half[:, :], -0.5).then_inc(consts, 1)

            def gather_idx2(g):
                pool.wait_ge(idx_stored[g], 16)
                for t in range(TPG * g, TPG * g + TPG):
                    pool.indirect_dma_start(
                        out=ix2[:, t:t + 1], out_offset=None, in_=idx_dram,
                        in_offset=bass.IndirectOffsetOnAxis(ap=ixg[:, t:t + 1], axis=0)).then_inc(idx2_ready[g], 16)

            def gather_ctx(g):
                pool.wait_ge(idx2_ready[g], 16 * TPG)
                if g >= 2:
                    pool.wait_ge(tp_full, G_STEP[f"T{g - 2}"] + 1)
                for t in range(TPG):
                    pool.indirect_dma_start(
                        out=ctxg[:, g % 2, t, :], out_offset=None, in_=ctx_rows,
                        in_offset=bass.IndirectOffsetOnAxis(ap=ix2[:, TPG * g + t:TPG * g + t + 1], axis=0)
                    ).then_inc(ctxg_ready[g], 16)

            gather_idx2(0)
            gather_ctx(0)
            gather_idx2(1)
            gather_idx2(2)
            gather_ctx(1)
            gather_idx2(3)
            gather_ctx(2)
            gather_ctx(3)
            pool.wait_ge(consts, 5)
            pool.wait_ge(var0_ready, 1)
            nc.gpsimd.tensor_tensor(chk[:, 3, :, 1], chk[:, 3, :, 0], half[:, :], ALU.pow).then_inc(pow0_ready, 1)
            for g in range(GRAPHS):
                s = slice(TPG * g, TPG * g + TPG)
                pool.wait_ge(ve_ready, g + 1)
                nc.gpsimd.tensor_tensor(r0[:, s], ve[:, s], half[:, s], ALU.pow).then_inc(pow_ready, 1)
            unless_one_hot(pool, slow_pool)

            def gather(e):
                if e >= XRING:
                    pool.wait_ge(y_ready, output_no["Y", e - XRING] + 1)
                pool.indirect_dma_start(
                    out=xg[:, e % XRING, :], out_offset=None, in_=rows_dram,
                    in_offset=bass.IndirectOffsetOnAxis(ap=tok[:, e:e + 1], axis=0)).then_inc(xg_ready[e % XRING], 16)

            for i in range(2):
                pool.wait_ge(rows_x[i], 16 * (GRAPHS // 2))
            pool.wait_ge(tp_full, G_X[3] + TPG)
            pool.iota(key[:, :], [[-1, TOKENS]], base=TOKENS, channel_multiplier=0,
                      allow_small_or_imprecise_dtypes=True).then_inc(consts, 1)
            pool.wait_ge(rows_w, 16 * GRAPHS)
            pool.wait_ge(tp_free, G_TOK + 1)
            pool.wait_ge(x1_stored, 16 * GRAPHS)
            for e in range(AHEAD):
                gather(e)
            for u in adds:
                kind, n = u
                if kind == "Y" and n + AHEAD < EXPERTS:
                    gather(n + AHEAD)
                pool.wait_ge(y_ready, output_no[u] + 1)
                if add_no[u]:
                    pool.wait_ge(added, 16 * add_no[u])
                if kind == "D":
                    g = n // TPG
                    pool.dma_start(out[g].rearrange("(p t) d -> p t d", p=P), ob[:, g % 2, :, :],
                                   accum_op=ALU.add).then_inc(added, 16)
                else:
                    pool.indirect_dma_start(
                        out=out_rows, out_offset=bass.IndirectOffsetOnAxis(ap=tok[:, n:n + 1], axis=0),
                        in_=ey[:, n % 3, :], in_offset=None, compute_op=ALU.add).then_inc(added, 16)
            pool.wait_ge(added, 16 * len(adds))

        @block.scalar
        def _(act):
            act.dma_start(w0[:, :].rearrange("f (h o) -> f h o", h=HEADS),
                          W0.rearrange("h f o -> f h o")).then_inc(ld_att, 16)
            act.dma_start(b0c[:, :], b0.rearrange("h o -> (h o)").rearrange("(c p) -> p c", p=P),
                          allow_slow_non_contiguous=True).then_inc(ld_att, 16)
            act.dma_start(raw(0), shared_gate.rearrange("(c p) k -> p c k", p=P)).then_inc(ld_sh[0], 16)

            def evac(n, dst, width=512, parts=P, shape=None):
                act.wait_ge(tp_full, n + 1)
                src = bank[n % 2][0:parts, 0:width]
                if shape:
                    src = src.rearrange("p (a b) -> p a b", a=shape)
                act.activation(dst, src, ACT.Copy).then_inc(tp_free, 1)

            act.wait_ge(ones_ready, 1)
            for step in att_order:
                g = int(step[1])
                if step[0] == "W":
                    for c in range(KC):
                        evac(G_STEP[step] + c, (gT, uT, dT)[g][:, c, :])
                elif step[0] == "R":
                    evac(G_STEP[step], rwT[:, :, :], KC * EXPERTS, shape=KC)
                elif step[0] == "S":
                    act.wait_ge(ld_att, 16 * 7)
                    for c in range(KC + 1):
                        act.activation(absw[:, c, :], w1[:, c, :] if c < KC else w0[:, :],
                                       ACT.Abs).then_inc(absw_ready, 1)
                elif step[0] == "T":
                    if g >= 2:
                        act.wait_ge(l1_full, KC * (g - 1))
                    evac(G_STEP[step], ctxT[:, g % 2, :])
                elif step[0] == "A":
                    for c in range(KC):
                        n = KC * g + c
                        act.wait_ge(l1_full, n + 1)
                        if n >= 2:
                            act.wait_ge(h1_ready, n - 1)
                        act.activation(he[:, n % 2, :], bank[2 + c][:, :], ACT.Exp, bias=b0c[:, c:c + 1])
                        act.activation(hr[:, n % 2, :], bank[2 + c][:, :], ACT.Relu,
                                       bias=b0c[:, c:c + 1]).then_inc(l1_act, 1)
                else:
                    for t in range(TPG):
                        n = TPG * g + t
                        act.wait_ge(z_ready, n + 1)
                        if n >= 2:
                            act.wait_ge(x1_ready, n - 1)
                        act.activation(th[:, n % 2, :], sg[:, n % 2, :], ACT.Exp,
                                       bias=minus_one[:, :]).then_inc(ez_ready, 1)
            act.wait_ge(x1_ready, TILES)
            act.wait_ge(l2_full, TILES)
            unless_one_hot(act, slow_scalar)

            def normed(g):
                act.wait_ge(ln_ready, g + 1)
                if g >= 2:
                    act.wait_ge(rows_x[g % 2], 16 * (g // 2))
                for n in range(TPG * g, TPG * g + TPG):
                    act.activation(xn[g % 2][:, n % TPG, :], xs[:, n, :], ACT.Identity, bias=nmr[:, n:n + 1],
                                   scale=rstd[:, n:n + 1]).then_inc(xn_ready, 1)

            def logits(g):
                act.wait_ge(r_full, g + 1)
                if g >= 2:
                    act.wait_ge(tp_full, G_L[g - 2] + 1)
                act.activation(sg[0:EXPERTS, g % 2, :], bank[6 + g % 2][0:EXPERTS, :], ACT.Tanh, scale=0.5).then_inc(r_act, 1)

            def logits_out(g):
                if g >= 2:
                    act.wait_ge(sel_ready, g - 1)
                evac(G_L[g], rth[:, g % 2, :, :], TPG * EXPERTS, shape=TPG)

            for g in range(GRAPHS):
                normed(g)
                if g:
                    logits(g - 1)
                for t in range(TPG):
                    n = TPG * g + t
                    evac(G_X[g] + t, xnT[:, :, P * n:P * n + P], shape=KC)
                if g:
                    logits_out(g - 1)
            logits(GRAPHS - 1)
            logits_out(GRAPHS - 1)

            def spread(e):
                if e >= 3:
                    act.wait_ge(gu_full, hidden_no["E", e - 3] + 1)
                evac(G_EXP + e, xgT[:, e % 3, :, :], KC * CAP, shape=KC)

            for u in units:
                kind, n = u
                if kind == "K":
                    for g in range(GRAPHS):
                        evac(G_SEL + g, selT[:, SEQ * g:SEQ * g + SEQ].rearrange("e (p t) -> e t p", t=TPG),
                             parts=EXPERTS, shape=TPG)
                elif kind in "SE":
                    if u == ("E", 0):
                        evac(G_TOK, tok[:, :], EXPERTS, parts=CAP)
                        spread(0)
                    if kind == "E" and n + 1 < EXPERTS:
                        spread(n + 1)
                    i = hidden_no[u]
                    cols = SEQ if kind == "S" else 2 * CAP
                    act.wait_ge(gu_full, i + 1)
                    if i >= 2:
                        act.wait_ge(h_ready, i - 1)
                    act.activation(th[:, i % 2, 0:cols], bank[2 + i % 2][:, 0:cols], ACT.Tanh,
                                   scale=0.5).then_inc(gu_act, 1)
                else:
                    i = output_no[u]
                    act.wait_ge(y_full, i + 1)
                    if kind == "D":
                        g = n // TPG
                        if g >= 2:
                            act.wait_ge(added, 16 * (add_no["D", TPG * (g - 1) - 1] + 1))
                        else:
                            act.wait_ge(x1_stored, 16 * GRAPHS)
                        act.activation(ob[:, g % 2, n % TPG, :], bank[6 + i % 2][:, :], ACT.Copy).then_inc(y_ready, 1)
                    else:
                        if n >= 3:
                            act.wait_ge(added, 16 * (add_no["Y", n - 3] + 1))
                        act.activation(ey[:, n % 3, :], bank[6 + i % 2][0:CAP, :], ACT.Copy,
                                       scale=xg[:, n % XRING, D + n:D + n + 1]).then_inc(y_ready, 1)

        @block.vector
        def _(v):
            done = [0]

            def link(ins):
                done[0] += 1
                ins.then_inc(dve, 1)
                v.wait_ge(dve, done[0])

            v.memset(minus_one[:, :], -1.0)
            v.memset(ones[:, :], 1.0).then_inc(ones_ready, 1)
            for t in range(TILES):
                g = t // TPG
                if t % TPG == 0:
                    v.wait_ge(ld_x[g], 16)
                v.max(mx[:, t, :], xs[:, t, :]).then_inc(top_done, 1)
                v.wait_ge(top_done, t + 1)
                v.max_index(ix[:, t, :], mx[:, t, :], xs[:, t, :]).then_inc(idx_done, 1)
                if t % TPG == TPG - 1:
                    v.wait_ge(idx_done, t + 1)
                    v.tensor_scalar(ixg[:, TPG * g:t + 1], ix[:, TPG * g:t + 1, 0], float(SEQ * g), None,
                                    ALU.add).then_inc(idxg_ready, 1)

            def take_sums():
                v.wait_ge(ld_att, 16 * 7)
                link(v.tensor_scalar(b1r[:, :], b1r[:, :], 1.0, None, ALU.add))
                v.wait_ge(sums_full, 1)
                v.tensor_copy(sums[:, :, :], bank[7][:, 0:2 * KC].rearrange("p (b n) -> p b n", b=2)).then_inc(sums_ready, 1)

            def stats0(t):
                link(v.bn_stats(bn0[:, t % 2, :], xs[:, t, :]))
                link(v.bn_aggr(mv0[:, t, :], bn0[:, t % 2, :]))

            def spread_of_x():
                v.tensor_scalar(chk[:, 3, :, 0], mv0[:, :, 1], EPS, None, ALU.add).then_inc(var0_ready, 1)

            def largest_ctx(i):
                v.wait_ge(ld_chk, 16 * 8)
                v.tensor_reduce(out=worst4[:, i:i + 1], in_=ctx_all[:, D * i:D * i + D], op=ALU.max, axis=AX.X,
                                apply_absolute_value=True).then_inc(worst4_ready, 1)

            def smallest_gap():
                v.wait_ge(pow0_ready, 1)
                link(v.tensor_tensor(chk[:, 0, :, :], mx[:, :, 0:2], mv0[:, :, 0:1].to_broadcast([P, TILES, 2]), ALU.subtract))
                link(v.tensor_tensor(chk[:, 1, :, :], chk[:, 0, :, :], chk[:, 3, :, 1:2].to_broadcast([P, TILES, 2]), ALU.mult))
                link(v.tensor_scalar(chk[:, 0, :, :], chk[:, 1, :, :], -1.0, 1.0, ALU.mult, ALU.add))
                link(v.tensor_scalar(chk[:, 1, :, :], chk[:, 0, :, :], MASK, None, ALU.mult))
                link(v.tensor_tensor(chk[:, 2, :, 0], chk[:, 1, :, 1], chk[:, 1, :, 0], ALU.subtract))
                v.reduce_max(worst[:, 1:2], chk[:, 2, :, 0], axis=AX.X)
                v.wait_ge(worst4_ready, 4)
                v.reduce_max(worst[:, 0:1], worst4[:, :], axis=AX.X)
                v.tensor_reduce(out=worst[:, 2:3], in_=b0c[:, :], op=ALU.max, axis=AX.X, apply_absolute_value=True)
                v.wait_ge(sums_ready, 1)
                v.reduce_max(worst[:, 3:4], sums[:, 0, :], axis=AX.X).then_inc(worst_ready, 1)

            def decide_weights():
                link(v.scalar_tensor_tensor(arow[:, :, :, :], arow[:, :, :, :], -1.0, arow[:, :, :, :], ALU.mult, ALU.max))
                link(v.tensor_tensor(prod[:, :, :], arow[:, :, 0, :], arow[:, :, 1, :], ALU.add))
                v.tensor_tensor(prod[:, :, :], prod[:, :, :], sums[:, :, :], ALU.mult).then_inc(worst_ready, 1)

            def decide():
                b = [bound[:, i:i + 1] for i in range(16)]
                v.wait_ge(worst_full, 1)
                v.reduce_max(bound[:, 2:4], bank[1][0:1, 0:2 * KC].rearrange("p (b n) -> p b n", b=2), axis=AX.X)
                link(v.reduce_max(bound[:, 4:8], bank[0][0:1, :].rearrange("p (b n) -> p b n", b=4), axis=AX.X))
                v.tensor_tensor(b[8], b[4], b[2], ALU.mult)
                link(v.scalar_tensor_tensor(b[12], b[7], b[4], b[6], ALU.mult, ALU.add))
                link(v.scalar_tensor_tensor(b[13], b[12], 1.0, b[3], ALU.add, ALU.mult))
                link(v.tensor_tensor(b[9], b[8], b[13], ALU.max))
                link(v.tensor_scalar(b[10], b[9], LOGIT_FACTOR, ROUNDING, ALU.mult, ALU.add))
                link(v.tensor_tensor(b[11], b[10], b[5], ALU.add))
                v.tensor_scalar(fast_flag[:, :], b[11], 0.0, None, ALU.is_lt).then_inc(flag_ready, 1)

            def first(n):
                v.wait_ge(l2_full, n + 1)
                if n >= 2:
                    v.wait_ge(x1_ready, n - 1)
                v.tensor_tensor(sg[:, n % 2, :], bank[6 + n % 2][:, :], b1r[:, :], ALU.add).then_inc(z_ready, 1)

            def second(n):
                v.wait_ge(ez_ready, n + 1)
                link(v.scalar_tensor_tensor(e1[:, n % 2, :], th[:, n % 2, :], 1.0, sg[:, n % 2, :], ALU.min, ALU.max))
                v.scalar_tensor_tensor(xs[:, n, :], e1[:, n % 2, :], -1.0, xs[:, n, :], ALU.add,
                                       ALU.add).then_inc(x1_ready, 1)

            def row_stats(n):
                v.wait_ge(x1_ready, n + 1)
                v.bn_stats(bn[:, n % TPG, :], xs[:, n, :]).then_inc(bn_done, 1)

            def variances(g):
                v.wait_ge(bn_done, TPG * (g + 1))
                for t in range(TPG * g, TPG * g + TPG):
                    ins = v.bn_aggr(mv[:, t, :], bn[:, t % TPG, :])
                link(ins)
                s = slice(TPG * g, TPG * g + TPG)
                v.tensor_scalar(ve[:, s], mv[:, s, 1], EPS, None, ALU.add).then_inc(ve_ready, 1)

            def scales(g):
                s = slice(TPG * g, TPG * g + TPG)
                v.wait_ge(ve_ready, g + 1)
                v.wait_ge(pow_ready, g + 1)
                link(v.tensor_tensor(nt1[:, s], ve[:, s], r0[:, s], ALU.mult))
                link(v.tensor_tensor(nt1[:, s], nt1[:, s], r0[:, s], ALU.mult))
                link(v.tensor_scalar(nt1[:, s], nt1[:, s], -0.5, 1.5, ALU.mult, ALU.add))
                link(v.tensor_tensor(rstd[:, s], r0[:, s], nt1[:, s], ALU.mult))
                v.scalar_tensor_tensor(nmr[:, s], mv[:, s, 0], -1.0, rstd[:, s], ALU.mult,
                                       ALU.mult).then_inc(ln_ready, 1)

            between = [lambda i=i: largest_ctx(i) for i in range(4)] + [smallest_gap, decide_weights, None, None, decide]
            for step in att_order:
                g = int(step[1])
                if step[0] == "A":
                    for c in range(KC):
                        n = KC * g + c
                        v.wait_ge(l1_act, n + 1)
                        if g >= 2 and c == 0:
                            v.wait_ge(l2_full, TPG * (g - 1))
                        link(v.tensor_scalar(e1[:, n % 2, :], he[:, n % 2, :], 1.0, -1.0, ALU.min, ALU.add))
                        v.tensor_tensor(h1T[:, g % 2, c, :], e1[:, n % 2, :], hr[:, n % 2, :], ALU.add).then_inc(h1_ready, 1)
                    if g < 2:
                        for t in range(2 * TPG * g, 2 * TPG * (g + 1)):
                            stats0(t)
                    if g == 1:
                        spread_of_x()
                elif step[0] == "B":
                    if g == 0:
                        take_sums()
                    first(TPG * g)
                    for n in range(TPG * g, TPG * g + TPG):
                        if n + 1 < TPG * (g + 1):
                            first(n + 1)
                        second(n)
                        if n % TPG:
                            row_stats(n - 1)
                        extra = between.pop(0) if between else None
                        if extra:
                            extra()
                    row_stats(TPG * (g + 1) - 1)
                    variances(g)
                    if g:
                        scales(g - 1)
            scales(GRAPHS - 1)
            v.wait_ge(x1_ready, TILES)
            unless_one_hot(v, slow_vector)

            def route(g):
                v.wait_ge(tp_free, G_L[g] + 1)
                if g:
                    v.wait_ge(wd_ready, g)
                if g == 0:
                    v.wait_ge(ld_eb, 16)
                    v.wait_ge(consts, 5)
                link(v.tensor_scalar(S[:, :, :], rth[:, g % 2, :, :], 0.5, 0.5, ALU.mult, ALU.add))
                link(v.tensor_tensor(SB[:, :, :], S[:, :, :], ebr[:, :].unsqueeze(1).to_broadcast([P, TPG, EXPERTS]), ALU.add))
                q = SB[:, :, :].rearrange("p t (g j) -> p t g j", j=GSIZE)
                a, b, c, d, m, n, top, gs = (rg[:, i, :, :] for i in range(8))
                v.tensor_tensor(a, q[:, :, :, 0], q[:, :, :, 1], ALU.max)
                v.tensor_tensor(b, q[:, :, :, 0], q[:, :, :, 1], ALU.min)
                v.tensor_tensor(c, q[:, :, :, 2], q[:, :, :, 3], ALU.max)
                link(v.tensor_tensor(d, q[:, :, :, 2], q[:, :, :, 3], ALU.min))
                v.tensor_tensor(m, a, c, ALU.min)
                v.tensor_tensor(n, b, d, ALU.max)
                link(v.tensor_tensor(top, a, c, ALU.max))
                link(v.tensor_tensor(m, m, n, ALU.max))
                link(v.tensor_tensor(gs, top, m, ALU.add))
                for t in range(TPG):
                    ins = v.max(rgm[:, t, :], rg[:, 7, t, :])
                link(ins)
                for t in range(TPG):
                    ins = v.max_index(rgi[:, t, :], rgm[:, t, :], rg[:, 7, t, :])
                link(ins)
                link(v.tensor_copy(rgf[:, :, :], rgi[:, :, :]))
                for k in range(TOP_GROUPS):
                    ins = v.tensor_tensor(rg[:, k, :, :], iota8[:, :, :],
                                          rgf[:, :, k:k + 1].to_broadcast([P, TPG, GROUPS]), ALU.is_equal)
                link(ins)
                link(v.tensor_tensor(rg[:, 3, :, :], rg[:, 0, :, :], rg[:, 1, :, :], ALU.add))
                link(v.tensor_tensor(rg[:, 4, :, :], rg[:, 3, :, :], rg[:, 2, :, :], ALU.add))
                link(v.tensor_tensor(q, q, rg[:, 4, :, :].unsqueeze(3).to_broadcast([P, TPG, GROUPS, GSIZE]), ALU.mult))
                for t in range(TPG):
                    ins = v.max(rgm[:, t, :], SB[:, t, :])
                link(ins)
                for t in range(TPG):
                    ins = v.max_index(rgi[:, t, :], rgm[:, t, :], SB[:, t, :])
                link(ins)
                link(v.tensor_copy(rgf[:, :, :], rgi[:, :, :]))
                for k in range(TOP_K):
                    ins = v.tensor_tensor(eq[:, k, :, :], iota32[:, :, :],
                                          rgf[:, :, k:k + 1].to_broadcast([P, TPG, EXPERTS]), ALU.is_equal)
                link(ins)
                link(v.tensor_tensor(eq[:, 0:2, :, :], eq[:, 0:2, :, :], eq[:, 2:4, :, :], ALU.add))
                so = sel[:, TPG * g:TPG * g + TPG, :]
                v.tensor_tensor(so, eq[:, 0, :, :], eq[:, 1, :, :], ALU.add).then_inc(sel_ready, 1)
                v.wait_ge(sel_ready, g + 1)
                link(v.tensor_tensor(S[:, :, :], S[:, :, :], so, ALU.mult))
                link(v.reduce_sum(den[:, :], S[:, :, :], axis=AX.X))
                link(v.tensor_scalar(den[:, :], den[:, :], 1e-20, None, ALU.add))
                link(v.reciprocal(den[:, :], den[:, :]))
                v.scalar_tensor_tensor(wd[:, TPG * g:TPG * g + TPG, :], S[:, :, :], SCALE,
                                       den[:, :].unsqueeze(2).to_broadcast([P, TPG, EXPERTS]), ALU.mult,
                                       ALU.mult).then_inc(wd_ready, 1)

            def hidden(u):
                kind, n = u
                i = hidden_no[u]
                if u == ("S", KC):
                    v.wait_ge(rows_x[1], 16 * (GRAPHS // 2))
                v.wait_ge(gu_act, i + 1)
                if kind == "S":
                    g, cols, up = n // KC, SEQ, bank[4 + i % 2][:, :]
                    dst = hT[:, g % 2, n % KC, :]
                    if n % KC == 0 and g >= 2:
                        v.wait_ge(y_full, output_no["D", TPG * (g - 1) - 1] + 1)
                else:
                    cols, up, dst = 2 * CAP, bank[2 + i % 2][:, 2 * CAP:4 * CAP], ehT[:, n % 2, :]
                link(v.scalar_tensor_tensor(sg[:, i % 2, 0:cols], th[:, i % 2, 0:cols], 1.0,
                                            bank[2 + i % 2][:, 0:cols], ALU.add, ALU.mult))
                if kind == "E" and n >= 2:
                    v.wait_ge(y_full, output_no["Y", n - 2] + 1)
                v.scalar_tensor_tensor(dst, sg[:, i % 2, 0:cols], 0.5, up, ALU.mult, ALU.mult).then_inc(h_ready, 1)

            def top(r, part):
                k8 = kk[:, 8 * r:8 * r + 8]
                if part == 0:
                    link(v.max(k8, key[:, :]))
                elif r + 1 < ROUNDS:
                    link(v.match_replace(key[:, :], k8, key[:, :], RETIRED))

            early = [("S", n) for n in range(2 * KC)]
            for g in range(GRAPHS):
                route(g)
            hidden(early.pop(0))
            hidden(early.pop(0))
            v.wait_ge(tp_free, G_SEL + GRAPHS)
            v.wait_ge(consts, 6)
            link(v.scalar_tensor_tensor(key[:, :], selT[:, :], float(TOKENS), key[:, :], ALU.mult, ALU.add))
            for i in range(2 * ROUNDS):
                top(i // 2, i % 2)
                if early and i % 3 == 1:
                    hidden(early.pop(0))
            link(v.tensor_scalar(kt[:, :], kk[:, :], float(TOKENS), float(TOKENS), ALU.is_gt, ALU.mult))
            v.scalar_tensor_tensor(tokf[:, :], kt[:, :], float(TOKENS), kk[:, :], ALU.add,
                                   ALU.subtract).then_inc(tok_ready, 1)
            for u in early + [u for u in mixed_part if u[0] in "SE"]:
                hidden(u)

        @block.tensor
        def _(pe):
            def group(n, parts):
                if n >= 2:
                    pe.wait_ge(tp_free, n - 1)
                for dst, src in parts:
                    k = src.shape[0]
                    last = pe.transpose(dst(bank[n % 2]), src, ident[0:k, 0:k])
                last.then_inc(tp_full, 1)

            pe.wait_ge(consts, 2)
            for step in att_order:
                g = int(step[1])
                if step[0] == "W":
                    pe.wait_ge(ld_sh[g], 16 if g == 0 else 16 * KC)
                    for c in range(KC):
                        group(G_STEP[step] + c,
                              [(lambda b, r=r: b[:, P * r:P * r + P], raw(g)[:, r, P * c:P * c + P]) for r in range(KC)])
                elif step[0] == "R":
                    pe.wait_ge(ld_sh[3], 16)
                    group(G_STEP[step], [(lambda b, c=c: b[:, EXPERTS * c:EXPERTS * c + EXPERTS],
                                          rwraw[:, P * c:P * c + P]) for c in range(KC)])
                elif step[0] == "S":
                    pe.wait_ge(ones_ready, 1)
                    pe.wait_ge(absw_ready, KC + 1)
                    for m in range(KC):
                        pe.matmul(bank[7][:, m:m + 1], absw[:, KC, P * m:P * m + P], ones[:, 0:1], start=True, stop=True)
                    for m in range(KC):
                        for c in range(KC):
                            last = pe.matmul(bank[7][:, KC + m:KC + m + 1], absw[:, c, P * m:P * m + P], ones[:, 0:1],
                                             start=(c == 0), stop=(c == KC - 1))
                    last.then_inc(sums_full, 1)
                elif step[0] == "T":
                    pe.wait_ge(ctxg_ready[g], 16 * TPG)
                    group(G_STEP[step], [(lambda b, t=t: b[:, P * t:P * t + P], ctxg[:, g % 2, t, :]) for t in range(TPG)])
                elif step[0] == "A":
                    pe.wait_ge(tp_free, G_STEP[step.replace("A", "T")] + 1)
                    if g == 0:
                        pe.wait_ge(ld_att, 16 * 7)
                    for c in range(KC):
                        n = KC * g + c
                        if g:
                            pe.wait_ge(l1_act, n - KC + 1)
                        pe.matmul(bank[2 + c][:, :], w0[:, P * c:P * c + P], ctxT[:, g % 2, :],
                                  start=True, stop=True).then_inc(l1_full, 1)
                else:
                    pe.wait_ge(h1_ready, KC * (g + 1))
                    if g == 0:
                        pe.wait_ge(sums_ready, 1)
                    if g == 2:
                        pe.wait_ge(tp_free, G_XN)
                        pe.wait_ge(worst_ready, 2)
                        for c in range(4):
                            pe.transpose(bank[0][0:1, P * c:P * c + P], worst[:, c:c + 1], ident[:, :])
                        pe.matmul(bank[1][:, 0:2 * KC], ones[:, :], prod[:, :, :], start=True, stop=True).then_inc(worst_full, 1)
                    for t in range(TPG):
                        n = TPG * g + t
                        if n >= 2:
                            pe.wait_ge(z_ready, n - 1)
                        for c in range(KC):
                            last = pe.matmul(bank[6 + n % 2][:, :], h1T[:, g % 2, c, P * t:P * t + P], w1[:, c, :],
                                             start=(c == 0), stop=(c == KC - 1))
                        last.then_inc(l2_full, 1)
            unless_one_hot(pe, slow_tensor)
            def transposed(g):
                for t in range(TPG):
                    pe.wait_ge(xn_ready, TPG * g + t + 1)
                    group(G_X[g] + t, [(lambda b, c=c: b[:, P * c:P * c + P], xn[g % 2][:, t, P * c:P * c + P])
                                       for c in range(KC)])

            def router(g):
                if g == 0:
                    pe.wait_ge(z_ready, TILES)
                if g >= 2:
                    pe.wait_ge(r_act, g - 1)
                pe.wait_ge(tp_free, G_X[g] + TPG)
                for c in range(KC):
                    last = pe.matmul(bank[6 + g % 2][0:EXPERTS, :], rwT[:, c, :], xnT[:, c, SEQ * g:SEQ * g + SEQ],
                                     start=(c == 0), stop=(c == KC - 1))
                last.then_inc(r_full, 1)

            def logits_out(g):
                pe.wait_ge(r_act, g + 1)
                group(G_L[g], [(lambda b, t=t: b[:, EXPERTS * t:EXPERTS * t + EXPERTS],
                                sg[0:EXPERTS, g % 2, P * t:P * t + P]) for t in range(TPG)])

            for g in range(GRAPHS):
                transposed(g)
                if g:
                    logits_out(g - 1)
                router(g)
            logits_out(GRAPHS - 1)

            def shared_hidden(n, i):
                g, part = n // KC, n % KC
                for b, w in ((2, gT), (4, uT)):
                    for c in range(KC):
                        last = pe.matmul(bank[b + i % 2][:, :], w[:, c, P * part:P * part + P],
                                         xnT[:, c, SEQ * g:SEQ * g + SEQ], start=(c == 0), stop=(c == KC - 1))
                last.then_inc(gu_full, 1)

            def expert_hidden(e, i):
                pe.wait_ge(tp_free, G_EXP + e + 1)
                pe.wait_ge(ld_w[(e + FIRST_SLOT) % RING], 48 * (e // RING + 1))
                for j, w in enumerate((ring_gate(e), ring_up(e))):
                    for k in range(IC):
                        at = CAP * (IC * j + k)
                        for c in range(KC):
                            last = pe.matmul(bank[2 + i % 2][:, at:at + CAP], w[:, c, P * k:P * k + P],
                                             xgT[:, e % 3, c, :], start=(c == 0), stop=(c == KC - 1))
                last.then_inc(gu_full, 1)

            def shared_out(n, i):
                g, t = n // TPG, n % TPG
                pe.wait_ge(h_ready, hidden_no["S", KC * g + KC - 1] + 1)
                for c in range(KC):
                    last = pe.matmul(bank[6 + i % 2][:, :], hT[:, g % 2, c, P * t:P * t + P], dT[:, c, :],
                                     start=(c == 0), stop=(c == KC - 1))
                last.then_inc(y_full, 1)

            def expert_out(e, i):
                pe.wait_ge(h_ready, hidden_no["E", e] + 1)
                for k in range(IC):
                    last = pe.matmul(bank[6 + i % 2][0:CAP, :], ehT[:, e % 2, CAP * k:CAP * k + CAP],
                                     ring_down(e)[:, k, :], start=(k == 0), stop=(k == IC - 1))
                last.then_inc(y_full, 1)

            def spread(e):
                pe.wait_ge(xg_ready[e % XRING], 16 * (e // XRING + 1))
                group(G_EXP + e, [(lambda b, c=c: b[:, CAP * c:CAP * c + CAP], xg[:, e % XRING, c:D:KC])
                                  for c in range(KC)])

            pe.wait_ge(l1_act, KC * GRAPHS)
            for u in units:
                kind, n = u
                if kind == "K":
                    for g in range(GRAPHS):
                        pe.wait_ge(sel_ready, g + 1)
                        group(G_SEL + g, [(lambda b, t=t: b[0:EXPERTS, P * t:P * t + P], sel[:, TPG * g + t, :])
                                          for t in range(TPG)])
                elif kind in "SE":
                    i = hidden_no[u]
                    if u == ("E", 0):
                        pe.wait_ge(tok_ready, 1)
                        group(G_TOK, [(lambda b: b[0:CAP, 0:EXPERTS], tokf[:, :])])
                        spread(0)
                    if kind == "E" and n + 1 < EXPERTS:
                        spread(n + 1)
                    if i >= 2:
                        pe.wait_ge(h_ready, i - 1)
                    (shared_hidden if kind == "S" else expert_hidden)(n, i)
                else:
                    i = output_no[u]
                    if i >= 2:
                        pe.wait_ge(y_ready, i - 1)
                    else:
                        pe.wait_ge(r_act, GRAPHS)
                    (shared_out if kind == "D" else expert_out)(n, i)


_INS = ['x', 'ctx_512', 'L0_xattn_W0', 'L0_xattn_a_self0', 'L0_xattn_a_neigh0', 'L0_xattn_b0', 'L0_xattn_W1',
        'L0_xattn_a_self1', 'L0_xattn_a_neigh1', 'L0_xattn_b1', 'L0_ffn_router_w', 'L0_ffn_e_bias',
        'L0_ffn_W_gate', 'L0_ffn_W_up', 'L0_ffn_W_down', 'L0_ffn_shared_gate', 'L0_ffn_shared_up',
        'L0_ffn_shared_down']
_OUTS = [((GRAPHS, SEQ, D), 'float32')]


def kernel(**inputs):
    import numpy as _np
    import concourse.bacc as _bacc
    from concourse import mybir as _mybir
    from concourse.bass_utils import run_bass_kernel_spmd as _run

    nc = _bacc.Bacc("TRN2", target_bir_lowering=False, num_devices=1)
    arrays, args = {}, []
    for name in _INS:
        a = _np.ascontiguousarray(inputs[name])
        arrays[f"in_{name}_dram"] = a
        args.append(nc.dram_tensor(f"in_{name}_dram", a.shape, _mybir.dt.from_np(a.dtype), kind="ExternalInput").ap())
    for i, (shape, dtype) in enumerate(_OUTS):
        dt = _mybir.dt.from_np(_np.dtype(dtype))
        args.append(nc.dram_tensor(f"out_{i}_dram", shape, dt, kind="ExternalOutput").ap())
    xattn_moe(nc, *args)
    r = _run(nc, [arrays], core_ids=[0])
    return r.results[0]["out_0_dram"]
```

```python
import concourse.bass as bass
from concourse import mybir
from contextlib import ExitStack

GRAPHS, SEQ, D = 4, 512, 512
P = 128
TPG = SEQ // P
TILES = GRAPHS * TPG
TOKENS = GRAPHS * SEQ
F_IN, HEADS, F_OUT = 128, 8, 64
F_HID = HEADS * F_OUT
KC = D // P
EXPERTS, GROUPS, GSIZE, TOP_GROUPS, TOP_K = 32, 8, 4, 3, 4
INNER = 256
IC = INNER // P
CAP = 80
ROW = D + EXPERTS
SCALE = 2.5
EPS = 1e-5
MASK = -1e10
SLOPE = 0.2
RING = 3
XRING = 7
AHEAD = 5
ROUNDS = CAP // 8
RETIRED = -1.0
LOGIT_FACTOR = 4.1
ROUNDING = 40000.0


def xattn_moe(nc, x, ctx_in, W0, a_self0, a_neigh0, b0, W1, a_self1, a_neigh1, b1,
              router_w, e_bias, W_gate, W_up, W_down, shared_gate, shared_up, shared_down, out):
    f32, u32, f32r = mybir.dt.float32, mybir.dt.uint32, mybir.dt.float32r
    ALU = mybir.AluOpType
    ACT = mybir.ActivationFunctionType
    AX = mybir.AxisListType

    x_rows = x.rearrange("g s d -> (g s) d")
    out_rows = out.rearrange("g s d -> (g s) d")
    ctx_rows = ctx_in.rearrange("g s f -> (g s) f")
    idx_dram = nc.dram_tensor("idx_dram", (TOKENS, 1), u32).ap()
    rows_dram = nc.dram_tensor("rows_dram", (TOKENS, ROW), f32).ap()

    es = ExitStack()
    with es:
        def sb(name, shape, dt=f32):
            return es.enter_context(nc.sbuf_tensor(name, shape, dt))

        def sem(name):
            return es.enter_context(nc.semaphore(name))

        ident = sb("ident", [P, P])
        ones = sb("ones", [P, P])
        at_xs = nc.sbuf_base
        xs = sb("xs", [P, TILES, D])
        at_room = nc.sbuf_base
        room = sb("room", [P, KC * TOKENS])
        w0 = sb("w0", [P, F_HID])
        at_w1 = nc.sbuf_base
        w1 = sb("w1", [P, KC, F_HID])
        b0c = sb("b0c", [P, KC])
        b1r = room[:, 12 * D:13 * D]
        ebr = sb("ebr", [P, EXPERTS])
        ring = sb("ring", [P, RING, 3072])
        HIGH, LOW = 0, 1
        gT = sb("gT", [P, 2, KC, D], f32r)
        uT = sb("uT", [P, 2, KC, D], f32r)
        dT = sb("dT", [P, 2, KC, D], f32r)
        normed_high_low = [nc.alloc_sbuf_tensor_at(f"normed{i}", [P, 2 * 2 * KC * SEQ], f32r, offset=at)
                           for i, at in enumerate((at_room, at_xs))]
        ob = room[:, 0:2 * TPG * D].rearrange("p (b t d) -> p b t d", b=2, t=TPG)
        xg = room[0:CAP, 2 * TPG * D:2 * TPG * D + XRING * ROW].rearrange("p (b r) -> p b r", b=XRING)

        def xT(g, part):
            at = (g % 2 * 2 + part) * KC * SEQ
            return normed_high_low[g // 2][:, at:at + KC * SEQ].rearrange("p (c n) -> p c n", c=KC)

        rwraw = room[0:EXPERTS, 13 * D:14 * D]
        rwT = sb("rwT", [P, 2, KC, EXPERTS], f32r)
        mx = sb("mx", [P, TILES, 8])
        ix = sb("ix", [P, TILES, 8], u32)
        ixg = sb("ixg", [P, TILES], u32)
        ix2 = sb("ix2", [P, TILES], u32)
        ctx_buf = sb("ctx_buf", [P, 4, SEQ])
        ctxg = ctx_buf[:, 0:2, :].rearrange("p b (t f) -> p b t f", f=F_IN)
        ctxT = ctx_buf[:, 2:4, :]
        at_h1T = nc.sbuf_base
        h1T = sb("h1T", [P, 2, KC, SEQ])
        he = room[:, 10 * D:12 * D].rearrange("p (b n) -> p b n", b=2)
        at_e1r = nc.sbuf_base
        e1r = sb("e1r", [P, 4, SEQ])
        e1, hr = e1r[:, 0:2, :], e1r[:, 2:4, :]
        bn0 = sb("bn0", [P, 2, 6])
        bn = sb("bn", [P, TPG, 6])
        minus_one = sb("minus_one", [P, 1])
        mv = sb("mv", [P, TILES, 2])
        ve = sb("ve", [P, TILES])
        half = sb("half", [P, TILES])
        r0 = sb("r0", [P, TILES])
        nt1 = sb("nt1", [P, TILES])
        rstd = sb("rstd", [P, TILES])
        nmr = sb("nmr", [P, TILES])
        xn = [ctx_buf, h1T[:, 1, :, :]]
        hT = nc.alloc_sbuf_tensor_at("hT", [P, 2, KC, SEQ], f32r, offset=at_h1T)
        th = sb("th", [P, 2, SEQ])
        sg = sb("sg", [P, 2, SEQ])
        selT = e1r[:, 0, :]
        key = ctx_buf[:, 0, :]
        key2 = ctx_buf[0:EXPERTS, 1, 0:GRAPHS * CAP]
        kk1 = sb("kk1", [P, CAP])
        ey = ctx_buf[0:CAP, 0:3, :]
        kk = sb("kk", [EXPERTS, CAP])
        kt = sb("kt", [EXPERTS, CAP])
        tokf = sb("tokf", [EXPERTS, CAP])
        tok = sb("tok", [CAP, EXPERTS], u32)
        rth = sb("rth", [P, GRAPHS, TPG, EXPERTS])
        at = [0]

        def in_w1(*dims):
            n = 1
            for k in dims:
                n *= k
            at[0] += n
            names = "abcd"[:len(dims)]
            v = w1[:, :, :].rearrange("p c n -> p (c n)")[:, at[0] - n:at[0]]
            return v.rearrange(f"p ({' '.join(names)}) -> p {' '.join(names)}", **dict(zip(names, dims)))

        PAIR = 2 * TPG
        S = in_w1(PAIR, EXPERTS)
        SB = in_w1(PAIR, EXPERTS)
        rg = in_w1(8, PAIR, GROUPS)
        rgi = sb("rgi", [P, PAIR, 8], u32)
        rgm = sb("rgm", [P, PAIR, 8])
        rgf = sb("rgf", [P, PAIR, 8])
        eq = e1r[:, 2:4, :].rearrange("p a b -> p (a b)").rearrange("p (k t e) -> p k t e", k=TOP_K, t=PAIR)
        sel = in_w1(TILES, EXPERTS)
        den = sb("den", [P, PAIR])
        wd = in_w1(TILES, EXPERTS)
        iota8 = sb("iota8", [P, 1, GROUPS])
        iota32 = sb("iota32", [P, 1, EXPERTS])
        flat = e1r[:, :, :].rearrange("p a b -> p (a b)")
        xgT = flat[:, 0:3 * KC * CAP].rearrange("p (b c n) -> p b c n", b=3, c=KC)
        ehT = nc.alloc_sbuf_tensor_at("ehT", [P, 2, 2, 2 * CAP], f32r, offset=at_e1r + 4 * 3 * KC * CAP)
        down = nc.alloc_sbuf_tensor_at("down", [P, 2, IC, D], f32r, offset=at_w1)

        bank = [es.enter_context(nc.psum_tensor(f"bank{i}", [P, 512], f32)) for i in range(8)]

        ld_x = [sem(f"ld_x{g}") for g in range(GRAPHS)]
        ld_sh = [sem(f"ld_sh{i}") for i in range(4)]
        ld_l0, ld_att = sem("ld_l0"), sem("ld_att")
        ld_eb = sem("ld_eb")
        ld_gate_up = [sem(f"ld_gate_up{i}") for i in range(RING)]
        ld_down = [sem(f"ld_down{i}") for i in range(RING)]
        consts = sem("consts")
        top_done, idx_done, idxg_ready = sem("top_done"), sem("idx_done"), sem("idxg_ready")
        idx_stored = [sem(f"idx_stored{g}") for g in range(GRAPHS)]
        idx2_ready = [sem(f"idx2_ready{g}") for g in range(GRAPHS)]
        ctxg_ready = [sem(f"ctxg_ready{g}") for g in range(GRAPHS)]
        tp_full, tp_free, tp_low = sem("tp_full"), sem("tp_free"), sem("tp_low")
        l1_full, l1_act, h1_ready = sem("l1_full"), sem("l1_act"), sem("h1_ready")
        l2_full, z_ready, ez_ready, x1_ready = sem("l2_full"), sem("z_ready"), sem("ez_ready"), sem("x1_ready")
        dve = sem("dve")
        ones_ready, bn_done = sem("ones_ready"), sem("bn_done")
        ve_ready, pow_ready, ln_ready, xn_ready = sem("ve_ready"), sem("pow_ready"), sem("ln_ready"), sem("xn_ready")
        rows_x, rows_w = [sem("rows_x0"), sem("rows_x1")], sem("rows_w")
        r_full, r_act, sel_ready, wd_ready = sem("r_full"), sem("r_act"), sem("sel_ready"), sem("wd_ready")
        x1_stored = [sem(f"x1_stored{g}") for g in range(GRAPHS)]
        gu_free, down_high, down_low = sem("gu_free"), sem("down_high"), sem("down_low")
        gu_full, gu_act, h_ready = sem("gu_full"), sem("gu_act"), sem("h_ready")
        y_full, y_ready = sem("y_full"), sem("y_ready")
        kk1_ready, tok_ready = sem("kk1_ready"), sem("tok_ready")
        xg_ready = [sem(f"xg_ready{i}") for i in range(XRING)]
        added = sem("added")

        att_order = ["W0", "T0", "A0", "W1", "T1", "V0", "A1", "S0", "B0", "T2", "A2", "B1", "T3", "A3", "B2", "B3", "W2", "R0"]
        G_STEP, G_XN = {}, 0
        for step in att_order:
            G_STEP[step] = G_XN
            G_XN += {"W": KC, "R": 1, "T": 1}.get(step[0], 0)
        G_X, G_L, n = {}, {}, G_XN
        for step in ("X0", "X1", "X2", "L0", "X3", "L1", "L2", "L3"):
            (G_X if step[0] == "X" else G_L)[int(step[1])] = n
            n += TPG if step[0] == "X" else 1
        G_SEL = n
        G_MERGE = G_SEL + 1
        G_TOK = G_MERGE + 1
        G_EXP = G_TOK + 1

        tp_bank = [(n - G_STEP["W2"]) % 6 if G_STEP["W2"] <= n < G_SEL else n % 2 for n in range(G_EXP + EXPERTS)]
        last_in_bank = [max([m for m in range(n) if tp_bank[m] == tp_bank[n]], default=None) for n in range(len(tp_bank))]
        split_groups = [G_STEP[f"W{i}"] + c for i in range(3) for c in range(KC)] + [G_STEP["R0"]]
        split_groups += [G_X[g] + t for g in range(GRAPHS) for t in range(TPG)]
        low_no = {n: i for i, n in enumerate(split_groups)}

        first_part = [("S", n) for n in range(3)] + [("K", 0), ("S", 3), ("S", 4)] + [("D", n) for n in range(TPG)]
        first_part += [("S", 5), ("M", 0), ("S", 6), ("S", 7)] + [("D", n) for n in range(TPG, 2 * TPG)] + [("T", 0), ("S", 8), ("S", 9)]
        shared_rest = [("S", n) for n in (10, 11)] + [("D", n) for n in range(2 * TPG, 3 * TPG)]
        shared_rest += [("S", n) for n in range(3 * KC, 4 * KC)] + [("D", n) for n in range(3 * TPG, 4 * TPG)]
        weight = {"S": 2, "D": 1}
        total, spent = sum(weight[k] for k, n in shared_rest), 0
        mixed_part = []
        for e in range(EXPERTS):
            mixed_part.append(("E", e))
            while shared_rest and spent + weight[shared_rest[0][0]] <= total * (e + 1) / EXPERTS:
                spent += weight[shared_rest[0][0]]
                mixed_part.append(shared_rest.pop(0))
            if e:
                mixed_part.append(("Y", e - 1))
        mixed_part += shared_rest + [("Y", EXPERTS - 1)]
        units = first_part + mixed_part
        hidden_no = {u: i for i, u in enumerate(u for u in units if u[0] in "SE")}
        output_no = {u: i for i, u in enumerate(u for u in units if u[0] in "DY")}
        adds = [u for u in units if u[0] == "Y" or u[0] == "D" and u[1] % TPG == TPG - 1]
        add_no = {u: i for i, u in enumerate(adds)}

        def ring_gate(e):
            return ring[:, e % RING, 0:1024].rearrange("p (c i) -> p c i", c=KC)

        def ring_up(e):
            return ring[:, e % RING, 1024:2048].rearrange("p (c i) -> p c i", c=KC)

        def ring_down(e):
            return ring[:, e % RING, 2048:3072].rearrange("p (c d) -> p c d", c=IC)

        def raw(i):
            return ring[:, i, 0:2048].rearrange("p (c k) -> p c k", c=KC)

        ctx_all = room[:, 0:TOKENS]
        absw = room[:, 2048:2048 + 5 * D].rearrange("p (b n) -> p b n", b=KC + 1)
        arow = sb("arow", [P, 2, 2, KC])
        sums = sb("sums", [P, 2, KC])
        prod = sb("prod", [P, 2, KC])
        mv0 = sb("mv0", [P, TILES, 2])
        chk = sb("chk", [P, 4, TILES, 2])
        worst4 = sb("worst4", [P, 4])
        worst = sb("worst", [P, 4])
        bound = sb("bound", [1, 16])
        fast_flag = sb("fast_flag", [1, 1], u32)
        ld_chk, absw_ready, sums_full = sem("ld_chk"), sem("absw_ready"), sem("sums_full")
        worst4_ready = sem("worst4_ready")
        sums_ready, var0_ready, pow0_ready, worst_ready = sem("sums_ready"), sem("var0_ready"), sem("pow0_ready"), sem("worst_ready")
        worst_full, flag_ready = sem("worst_full"), sem("flag_ready")

        mask_dram = nc.dram_tensor("mask_dram", (TOKENS, SEQ), f32).ap()
        feat_dram = nc.dram_tensor("feat_dram", (TOKENS, F_HID), f32).ap()
        sn_dram = nc.dram_tensor("sn_dram", (2 * HEADS, TOKENS), f32).ap()
        hid_dram = [nc.dram_tensor(f"hid_dram{i}", (TOKENS, F_HID), f32).ap() for i in range(2)]
        g_x = room[:, 0:D]
        g_xT = room[:, D:2 * D].rearrange("p (c n) -> p c n", c=KC)
        g_a = room[:, 2 * D:4 * D].rearrange("p (b n) -> p b n", b=2)
        g_feat = room[:, 4 * D:5 * D]
        g_tmp = room[:, 5 * D:6 * D]
        g_mask = room[:, 6 * D:7 * D]
        g_neigh = room[:, 7 * D:8 * D]
        g_e = room[:, 8 * D:9 * D]
        g_p = room[:, 9 * D:10 * D]
        g_pT = room[:, 10 * D:11 * D]
        g_f = room[:, 11 * D:11 * D + KC * F_OUT].rearrange("p (c o) -> p c o", c=KC)
        g_b, g_xp, g_z, g_ez, g_h = (room[:, 12 * D + F_OUT * i:12 * D + F_OUT * i + F_OUT] for i in range(5))
        g_sn = room[:, 13 * D:13 * D + 2 * HEADS]
        g_snT = room[0:2 * HEADS, 13 * D + 32:13 * D + 32 + P]
        g_self, g_max, g_sum, g_ve, g_r0, g_r = (room[:, 14 * D + i:14 * D + i + 1] for i in range(6))
        g_bn = room[:, 14 * D + 16:14 * D + 22]
        g_bn2 = room[:, 14 * D + 32:14 * D + 32 + 6 * TILES].rearrange("p (t b) -> p t b", t=TILES)
        g_mv = room[:, 14 * D + 24:14 * D + 26]
        g_load, g_const, g_store, g_done = sem("g_load"), sem("g_const"), sem("g_store"), sem("g_done")
        g_stored = sem("g_stored")
        g_held, g_ln = sem("g_held"), sem("g_ln")
        g_pe, g_act, g_dve, g_pool = sem("g_pe"), sem("g_act"), sem("g_dve"), sem("g_pool")
        a_pair = [(a_self0, a_neigh0, b0), (a_self1, a_neigh1, b1)]

        block = es.enter_context(nc.Block())

        DVE_M, ACT_F, PE_F, DVE_F, PE_S, ACT_S, DVE_S = 10, 2, 3, 5, 2, 4, 8
        S_ROUNDS = TILES * HEADS
        DVE_PASSES = TILES * DVE_M + 2 * (TILES * DVE_F + S_ROUNDS * DVE_S)

        def held(eng, what, value):
            eng.wait_ge(what, value)
            eng.sem_inc(g_held)

        def slow_sync(sp):
            loads = stores = consts_in = 0
            with sp.Fori(0, TILES) as i:
                sp.dma_start(g_x, x_rows[bass.ds(i * P, P), :]).then_inc(g_load, 16)
                held(sp, g_dve, i * DVE_M + DVE_M)
                sp.dma_start(mask_dram[bass.ds(i * P, P), :], g_e).then_inc(g_store, 16)
                held(sp, g_store, i * 16 + 16)
            dve, loads, stores, act, pe = TILES * DVE_M, TILES * 16, TILES * 16, 0, 0
            for layer in range(2):
                sp.dma_start(g_a[:, 0, :], a_pair[layer][0].rearrange("h o -> (h o)").partition_broadcast(P)).then_inc(g_const, 16)
                sp.dma_start(g_a[:, 1, :], a_pair[layer][1].rearrange("h o -> (h o)").partition_broadcast(P)).then_inc(g_const, 16)
                with sp.Fori(0, TILES) as i:
                    src = ctx_rows if layer == 0 else hid_dram[0]
                    sp.dma_start(g_x[:, 0:src.shape[1]], src[bass.ds(i * P, P), :]).then_inc(g_load, 16)
                    held(sp, g_act, i * ACT_F + (act + ACT_F))
                    sp.dma_start(sn_dram[:, bass.ds(i * P, P)], g_snT).then_inc(g_store, 16)
                    sp.dma_start(feat_dram[bass.ds(i * P, P), :], g_feat).then_inc(g_store, 16)
                    held(sp, g_store, i * 32 + (stores + 32))
                act, dve, loads, stores = act + TILES * ACT_F, dve + TILES * DVE_F, loads + TILES * 16, stores + TILES * 32
                with sp.Fori(0, GRAPHS) as g:
                    with sp.Fori(0, TPG) as t:
                        with sp.Fori(0, HEADS) as h:
                            i = g * (TPG * HEADS) + t * HEADS + h
                            rows = g * SEQ + t * P
                            sp.dma_start(g_mask, mask_dram[bass.ds(rows, P), :]).then_inc(g_load, 16)
                            sp.dma_start(g_neigh, sn_dram[bass.ds(h + HEADS, 1), bass.ds(g * SEQ, SEQ)]
                                         .to_broadcast([P, SEQ])).then_inc(g_load, 16)
                            sp.dma_start(g_self, sn_dram[bass.ds(h, 1), bass.ds(rows, P)].rearrange("a p -> p a"),
                                         allow_slow_non_contiguous=True).then_inc(g_load, 16)
                            sp.dma_start(g_f, feat_dram[bass.ds(g * SEQ, SEQ), bass.ds(h * F_OUT, F_OUT)]
                                         .rearrange("(c p) o -> p c o", p=P)).then_inc(g_load, 16)
                            sp.dma_start(g_b, a_pair[layer][2][bass.ds(h, 1), :].to_broadcast([P, F_OUT])).then_inc(g_load, 16)
                            sp.dma_start(g_xp, x_rows[bass.ds(rows, P), bass.ds(h * F_OUT, F_OUT)]).then_inc(g_load, 16)
                            held(sp, g_dve, i * DVE_S + (dve + DVE_S))
                            sp.dma_start(hid_dram[layer][bass.ds(rows, P), bass.ds(h * F_OUT, F_OUT)], g_h).then_inc(g_store, 16)
                            held(sp, g_store, i * 16 + (stores + 16))
                act, dve, loads, stores = act + S_ROUNDS * ACT_S, dve + S_ROUNDS * DVE_S, loads + S_ROUNDS * 96, stores + S_ROUNDS * 16
            for g in range(GRAPHS - 1):
                sp.wait_ge(x1_stored[g], 16)
            for g in range(GRAPHS):
                sp.dma_start(xs[:, TPG * g:TPG * g + TPG, :],
                             hid_dram[1][SEQ * g:SEQ * g + SEQ, :].rearrange("(p t) d -> p t d", p=P)).then_inc(g_done, 16)
            sp.wait_ge(g_done, 16 * GRAPHS)
            for g in range(GRAPHS - 1):
                sp.dma_start(out[g].rearrange("(p t) d -> p t d", p=P),
                             xs[:, TPG * g:TPG * g + TPG, :]).then_inc(g_stored, 16)
            sp.wait_ge(g_stored, 16 * (GRAPHS - 1))

        def slow_pool(pool):
            with pool.Fori(0, TILES) as i:
                pool.wait_ge(g_dve, i * DVE_M + 3)
                nc.gpsimd.tensor_tensor(g_r0, g_ve, half[:, 0:1], ALU.pow).then_inc(g_pool, 1)
            pool.wait_ge(g_dve, DVE_PASSES + 3)
            nc.gpsimd.tensor_tensor(r0[:, :], ve[:, :], half[:, :], ALU.pow).then_inc(g_pool, 1)

        def slow_vector(v):
            def step(ins, n):
                ins.then_inc(g_dve, 1)
                held(v, g_dve, n)

            with v.Fori(0, TILES) as i:
                n = i * DVE_M
                v.wait_ge(g_load, i * 16 + 16)
                step(v.bn_stats(g_bn, g_x), n + 1)
                step(v.bn_aggr(g_mv, g_bn), n + 2)
                step(v.tensor_scalar(g_ve, g_mv[:, 1:2], EPS, None, ALU.add), n + 3)
                v.wait_ge(g_pool, i + 1)
                step(v.tensor_tensor(g_r, g_ve, g_r0, ALU.mult), n + 4)
                step(v.tensor_tensor(g_r, g_r, g_r0, ALU.mult), n + 5)
                step(v.tensor_scalar(g_r, g_r, -0.5, 1.5, ALU.mult, ALU.add), n + 6)
                step(v.tensor_tensor(g_r, g_r, g_r0, ALU.mult), n + 7)
                step(v.tensor_scalar(g_tmp, g_x, g_mv[:, 0:1], g_r, ALU.subtract, ALU.mult), n + 8)
                step(v.tensor_scalar(g_p, g_tmp, -1.0, 1.0, ALU.mult, ALU.add), n + 9)
                step(v.tensor_scalar(g_e, g_p, MASK, None, ALU.mult), n + 10)
            dve, loads, act, pe = TILES * DVE_M, TILES * 16, 0, 0
            for layer in range(2):
                v.wait_ge(g_const, 32 * (layer + 1))
                with v.Fori(0, TILES) as i:
                    n = i * DVE_F + dve
                    v.wait_ge(g_pe, i * PE_F + (pe + 2))
                    step(v.tensor_copy(g_feat, bank[1][:, :]), n + 1)
                    step(v.tensor_tensor(g_tmp, g_feat, g_a[:, 0, :], ALU.mult), n + 2)
                    step(v.reduce_sum(g_sn[:, 0:HEADS], g_tmp.rearrange("p (h o) -> p h o", h=HEADS), axis=AX.X), n + 3)
                    step(v.tensor_tensor(g_tmp, g_feat, g_a[:, 1, :], ALU.mult), n + 4)
                    step(v.reduce_sum(g_sn[:, HEADS:2 * HEADS], g_tmp.rearrange("p (h o) -> p h o", h=HEADS), axis=AX.X), n + 5)
                dve, pe, act, loads = dve + TILES * DVE_F, pe + TILES * PE_F, act + TILES * ACT_F, loads + TILES * 16
                with v.Fori(0, S_ROUNDS) as i:
                    n = i * DVE_S + dve
                    v.wait_ge(g_load, i * 96 + (loads + 96))
                    v.wait_ge(g_act, i * ACT_S + (act + 1))
                    step(v.scalar_tensor_tensor(g_p, g_e, SLOPE, g_e, ALU.mult, ALU.max), n + 1)
                    step(v.tensor_tensor(g_e, g_p, g_mask, ALU.add), n + 2)
                    step(v.reduce_max(g_max, g_e, axis=AX.X), n + 3)
                    step(v.tensor_scalar(g_max, g_max, -1.0, None, ALU.mult), n + 4)
                    v.wait_ge(g_act, i * ACT_S + (act + 2))
                    step(v.reciprocal(g_sum, g_sum), n + 5)
                    v.wait_ge(g_pe, i * PE_S + (pe + 2))
                    step(v.scalar_tensor_tensor(g_z, bank[1][:, 0:F_OUT], g_sum, g_b, ALU.mult, ALU.add), n + 6)
                    v.wait_ge(g_act, i * ACT_S + (act + 4))
                    step(v.tensor_scalar(g_ez, g_ez, 1.0, -1.0, ALU.min, ALU.add), n + 7)
                    if layer == 0:
                        step(v.scalar_tensor_tensor(g_h, g_z, 0.0, g_ez, ALU.max, ALU.add), n + 8)
                    else:
                        v.scalar_tensor_tensor(g_ez, g_z, 0.0, g_ez, ALU.max, ALU.add).then_inc(g_pool, 1)
                        v.wait_ge(g_pool, i + (TILES + 1))
                        step(v.tensor_tensor(g_h, g_ez, g_xp, ALU.add), n + 8)
                dve, pe, act, loads = dve + S_ROUNDS * DVE_S, pe + S_ROUNDS * PE_S, act + S_ROUNDS * ACT_S, loads + S_ROUNDS * 96
            v.wait_ge(g_done, 16 * GRAPHS)
            n = DVE_PASSES
            for t in range(TILES):
                ins = v.bn_stats(g_bn2[:, t, :], xs[:, t, :])
            step(ins, n + 1)
            for t in range(TILES):
                ins = v.bn_aggr(mv[:, t, :], g_bn2[:, t, :])
            step(ins, n + 2)
            step(v.tensor_scalar(ve[:, :], mv[:, :, 1], EPS, None, ALU.add), n + 3)
            v.wait_ge(g_pool, TILES + S_ROUNDS + 1)
            step(v.tensor_tensor(nt1[:, :], ve[:, :], r0[:, :], ALU.mult), n + 4)
            step(v.tensor_tensor(nt1[:, :], nt1[:, :], r0[:, :], ALU.mult), n + 5)
            step(v.tensor_scalar(nt1[:, :], nt1[:, :], -0.5, 1.5, ALU.mult, ALU.add), n + 6)
            step(v.tensor_tensor(rstd[:, :], r0[:, :], nt1[:, :], ALU.mult), n + 7)
            v.scalar_tensor_tensor(nmr[:, :], mv[:, :, 0], -1.0, rstd[:, :], ALU.mult, ALU.mult).then_inc(g_ln, 1)

        def slow_scalar(act_e):
            act, pe, dve, loads = 0, 0, TILES * DVE_M, TILES * 16
            for layer in range(2):
                kc = 1 if layer == 0 else KC
                with act_e.Fori(0, TILES) as i:
                    act_e.wait_ge(g_pe, i * PE_F + (pe + 1))
                    act_e.activation(g_xT[:, 0:kc, :], bank[0][:, 0:kc * P].rearrange("p (c n) -> p c n", c=kc), ACT.Copy).then_inc(g_act, 1)
                    act_e.wait_ge(g_pe, i * PE_F + (pe + 3))
                    act_e.activation(g_snT, bank[0][0:2 * HEADS, 0:P], ACT.Copy).then_inc(g_act, 1)
                dve, pe, act, loads = dve + TILES * DVE_F, pe + TILES * PE_F, act + TILES * ACT_F, loads + TILES * 16
                with act_e.Fori(0, S_ROUNDS) as i:
                    act_e.wait_ge(g_load, i * 96 + (loads + 96))
                    act_e.activation(g_e, g_neigh, ACT.Identity, bias=g_self).then_inc(g_act, 1)
                    act_e.wait_ge(g_dve, i * DVE_S + (dve + 4))
                    act_e.activation(g_tmp, g_e, ACT.Exp, bias=g_max, accum_out=g_sum).then_inc(g_act, 1)
                    act_e.wait_ge(g_pe, i * PE_S + (pe + 1))
                    act_e.activation(g_pT, bank[0][:, :], ACT.Copy).then_inc(g_act, 1)
                    act_e.wait_ge(g_dve, i * DVE_S + (dve + 6))
                    act_e.activation(g_ez, g_z, ACT.Exp).then_inc(g_act, 1)
                dve, pe, act, loads = dve + S_ROUNDS * DVE_S, pe + S_ROUNDS * PE_S, act + S_ROUNDS * ACT_S, loads + S_ROUNDS * 96

            act_e.wait_ge(g_ln, 1)

        def slow_tensor(pe_e):
            act, pe, dve, loads = 0, 0, TILES * DVE_M, TILES * 16
            for layer in range(2):
                kc = 1 if layer == 0 else KC
                w = w0[:, :].unsqueeze(1) if layer == 0 else w1
                with pe_e.Fori(0, TILES) as i:
                    pe_e.wait_ge(g_load, i * 16 + (loads + 16))
                    for c in range(kc):
                        last = pe_e.transpose(bank[0][:, P * c:P * c + P], g_x[:, P * c:P * c + P], ident[:, :])
                    last.then_inc(g_pe, 1)
                    pe_e.wait_ge(g_act, i * ACT_F + (act + 1))
                    for c in range(kc):
                        last = pe_e.matmul(bank[1][:, :], g_xT[:, c, :], w[:, c, :], start=(c == 0), stop=(c == kc - 1))
                    last.then_inc(g_pe, 1)
                    pe_e.wait_ge(g_dve, i * DVE_F + (dve + DVE_F))
                    pe_e.transpose(bank[0][0:2 * HEADS, 0:P], g_sn, ident[:, :]).then_inc(g_pe, 1)
                dve, act, loads = dve + TILES * DVE_F, act + TILES * ACT_F, loads + TILES * 16
                with pe_e.Fori(0, S_ROUNDS) as i:
                    pe_e.wait_ge(g_act, i * ACT_S + (act + 2))
                    for c in range(KC):
                        last = pe_e.transpose(bank[0][:, P * c:P * c + P], g_tmp[:, P * c:P * c + P], ident[:, :])
                    last.then_inc(g_pe, 1)
                    pe_e.wait_ge(g_act, i * ACT_S + (act + 3))
                    for c in range(KC):
                        last = pe_e.matmul(bank[1][:, 0:F_OUT], g_pT[:, P * c:P * c + P], g_f[:, c, :],
                                           start=(c == 0), stop=(c == KC - 1))
                    last.then_inc(g_pe, 1)
                dve, act, loads = dve + S_ROUNDS * DVE_S, act + S_ROUNDS * ACT_S, loads + S_ROUNDS * 96

        def unless_one_hot(eng, slow=None):
            eng.wait_ge(flag_ready, 1)
            one_hot = eng.value_load(fast_flag[0:1, 0:1], min_val=0, max_val=1)
            with eng.If(one_hot == 0):
                slow(eng)
            with eng.Else():
                eng.nop()

        @block.sync
        def _(sp):
            def store_x1(g, stored):
                sp.dma_start(out[g].rearrange("(p t) d -> p t d", p=P),
                             xs[:, TPG * g:TPG * g + TPG, :]).then_inc(stored, 16)

            def load_x(g):
                sp.dma_start(xs[:, TPG * g:TPG * g + TPG, :],
                             x[g].rearrange("(p t) d -> p t d", p=P)).then_inc(ld_x[g], 16)

            def load_raw(i):
                w = (None, shared_up, shared_down)[i].rearrange("(c p) k -> p c k", p=P)
                for c in range(KC):
                    sp.dma_start(raw(i)[:, c, :], w[:, c, :]).then_inc(ld_sh[i], 16)

            def store_idx(g):
                sp.wait_ge(idxg_ready, g + 1)
                sp.dma_start(idx_dram[SEQ * g:SEQ * g + SEQ, :].rearrange("(p t) o -> p (t o)", p=P),
                             ixg[:, TPG * g:TPG * g + TPG]).then_inc(idx_stored[g], 16)

            def load_gate_up(e):
                sp.dma_start(ring_gate(e), W_gate[e].rearrange("(p c) i -> p c i", c=KC)).then_inc(ld_gate_up[e % RING], 16)
                sp.dma_start(ring_up(e), W_up[e].rearrange("(p c) i -> p c i", c=KC)).then_inc(ld_gate_up[e % RING], 16)

            def load_down(e):
                sp.dma_start(ring_down(e), W_down[e].rearrange("(c p) d -> p c d", p=P)).then_inc(ld_down[e % RING], 16)

            load_x(0)
            load_x(1)
            store_idx(0)
            load_x(2)
            store_idx(1)
            load_x(3)
            store_idx(2)
            load_raw(1)
            for c in range(KC):
                sp.dma_start(w1[:, c, :].rearrange("f (h o) -> f h o", h=HEADS),
                             W1[:, P * c:P * c + P, :].rearrange("h f o -> f h o")).then_inc(ld_att, 16)
            store_idx(3)
            sp.dma_start(b1r[:, :], b1.rearrange("h o -> (h o)").partition_broadcast(P)).then_inc(ld_att, 16)
            load_raw(2)
            sp.dma_start(rwraw[:, :], router_w).then_inc(ld_sh[3], 16)
            sp.dma_start(ebr[:, :], e_bias.partition_broadcast(P)).then_inc(ld_eb, 16)
            for i, a in enumerate((a_self0, a_neigh0, a_self1, a_neigh1)):
                sp.dma_start(arow[:, i // 2, i % 2, :], a.rearrange("h o -> (h o)").rearrange("(c p) -> p c", p=P),
                             allow_slow_non_contiguous=True).then_inc(ld_chk, 16)
            for g in range(GRAPHS):
                sp.dma_start(ctx_all[:, D * g:D * g + D].rearrange("p (t f) -> p t f", f=F_IN),
                             ctx_in[g].rearrange("(p t) f -> p t f", p=P)).then_inc(ld_chk, 16)
            sp.wait_ge(ctxg_ready[GRAPHS - 1], 16 * TPG)
            for e in range(RING - 1):
                sp.wait_ge(tp_full, G_STEP[f"W{e}"] + KC)
                load_gate_up(e)
                load_down(e)
            for g in range(GRAPHS - 1):
                sp.wait_ge(x1_ready, TPG * (g + 1))
                store_x1(g, x1_stored[g])
            sp.wait_ge(x1_ready, TILES)
            unless_one_hot(sp, slow_sync)
            for g in range(GRAPHS):
                sp.wait_ge(xn_ready, TPG * (g + 1))
                sp.dma_start(rows_dram[SEQ * g:SEQ * g + SEQ, 0:D].rearrange("(p t) d -> p t d", p=P),
                             xn[g % 2][:, :, :]).then_inc(rows_x[g % 2], 16)
                if g == 1:
                    store_x1(GRAPHS - 1, x1_stored[GRAPHS - 1])
            sp.wait_ge(tp_full, G_STEP[f"W{RING - 1}"] + KC)
            load_gate_up(RING - 1)
            load_down(RING - 1)
            for g in range(GRAPHS):
                sp.wait_ge(wd_ready, g // 2 + 1)
                sp.dma_start(rows_dram[SEQ * g:SEQ * g + SEQ, D:ROW].rearrange("(p t) e -> p t e", p=P),
                             wd[:, TPG * g:TPG * g + TPG, :]).then_inc(rows_w, 16)
            for e in range(RING, EXPERTS + 1):
                if e < EXPERTS:
                    sp.wait_ge(gu_full, hidden_no["E", e - RING] + 1)
                    load_gate_up(e)
                if e > RING:
                    sp.wait_ge(down_low, e - RING)
                    load_down(e - 1)

        @block.gpsimd
        def _(pool):
            pool.memset(ident[:, :], 0.0).then_inc(consts, 1)
            pool.wait_ge(consts, 1)
            pool.affine_select(out=ident[:, :], in_=ident[:, :], compare_op=ALU.not_equal, fill=1.0,
                               base=0, pattern=[[-1, P]], channel_multiplier=1).then_inc(consts, 1)
            pool.iota(iota8[:, :, :], [[0, 1], [1, GROUPS]], base=0, channel_multiplier=0,
                      allow_small_or_imprecise_dtypes=True).then_inc(consts, 1)
            pool.iota(iota32[:, :, :], [[0, 1], [1, EXPERTS]], base=0, channel_multiplier=0,
                      allow_small_or_imprecise_dtypes=True).then_inc(consts, 1)
            pool.memset(half[:, :], -0.5).then_inc(consts, 1)

            def gather_idx2(g):
                pool.wait_ge(idx_stored[g], 16)
                for t in range(TPG * g, TPG * g + TPG):
                    pool.indirect_dma_start(
                        out=ix2[:, t:t + 1], out_offset=None, in_=idx_dram,
                        in_offset=bass.IndirectOffsetOnAxis(ap=ixg[:, t:t + 1], axis=0)).then_inc(idx2_ready[g], 16)

            def gather_ctx(g):
                pool.wait_ge(idx2_ready[g], 16 * TPG)
                if g >= 2:
                    pool.wait_ge(tp_full, G_STEP[f"T{g - 2}"] + 1)
                for t in range(TPG):
                    pool.indirect_dma_start(
                        out=ctxg[:, g % 2, t, :], out_offset=None, in_=ctx_rows,
                        in_offset=bass.IndirectOffsetOnAxis(ap=ix2[:, TPG * g + t:TPG * g + t + 1], axis=0)
                    ).then_inc(ctxg_ready[g], 16)

            gather_idx2(0)
            gather_ctx(0)
            gather_idx2(1)
            gather_idx2(2)
            gather_ctx(1)
            gather_idx2(3)
            gather_ctx(2)
            gather_ctx(3)
            pool.wait_ge(consts, 5)
            pool.wait_ge(var0_ready, 1)
            nc.gpsimd.tensor_tensor(chk[:, 3, :, 1], chk[:, 3, :, 0], half[:, :], ALU.pow).then_inc(pow0_ready, 1)
            for g in range(GRAPHS):
                s = slice(TPG * g, TPG * g + TPG)
                pool.wait_ge(ve_ready, g + 1)
                nc.gpsimd.tensor_tensor(r0[:, s], ve[:, s], half[:, s], ALU.pow).then_inc(pow_ready, 1)
            unless_one_hot(pool, slow_pool)
            def gather(e):
                if e >= XRING:
                    pool.wait_ge(y_ready, output_no["Y", e - XRING] + 1)
                pool.indirect_dma_start(
                    out=xg[:, e % XRING, :], out_offset=None, in_=rows_dram,
                    in_offset=bass.IndirectOffsetOnAxis(ap=tok[:, e:e + 1], axis=0)).then_inc(xg_ready[e % XRING], 16)

            for i in range(2):
                pool.wait_ge(rows_x[i], 16 * (GRAPHS // 2))
            pool.wait_ge(tp_full, G_X[3] + TPG)
            for g in range(GRAPHS):
                pool.iota(key[EXPERTS * g:EXPERTS * g + EXPERTS, :].rearrange("e (t p) -> e t p", t=TPG),
                          [[-1, TPG], [-TPG, P]], base=TOKENS - SEQ * g, channel_multiplier=0,
                          allow_small_or_imprecise_dtypes=True).then_inc(consts, 1)
            pool.wait_ge(rows_w, 16 * GRAPHS)
            pool.wait_ge(tp_free, G_TOK + 1)
            pool.wait_ge(gu_full, hidden_no["S", 2 * KC - 1] + 1)
            pool.wait_ge(x1_stored[GRAPHS - 1], 16)
            for e in range(AHEAD):
                gather(e)
            for u in adds:
                kind, n = u
                if kind == "Y" and n + AHEAD < EXPERTS:
                    gather(n + AHEAD)
                pool.wait_ge(y_ready, output_no[u] + 1)
                if add_no[u]:
                    pool.wait_ge(added, 16 * add_no[u])
                if kind == "D":
                    g = n // TPG
                    pool.dma_start(out[g].rearrange("(p t) d -> p t d", p=P), ob[:, g % 2, :, :],
                                   accum_op=ALU.add).then_inc(added, 16)
                else:
                    pool.indirect_dma_start(
                        out=out_rows, out_offset=bass.IndirectOffsetOnAxis(ap=tok[:, n:n + 1], axis=0),
                        in_=ey[:, n % 3, :], in_offset=None, compute_op=ALU.add).then_inc(added, 16)
            pool.wait_ge(added, 16 * len(adds))

        @block.scalar
        def _(act):
            act.dma_start(w0[:, :].rearrange("f (h o) -> f h o", h=HEADS),
                          W0.rearrange("h f o -> f h o")).then_inc(ld_l0, 16)
            act.dma_start(b0c[:, :], b0.rearrange("h o -> (h o)").rearrange("(c p) -> p c", p=P),
                          allow_slow_non_contiguous=True).then_inc(ld_l0, 16)
            act.dma_start(raw(0), shared_gate.rearrange("(c p) k -> p c k", p=P)).then_inc(ld_sh[0], 16)

            def evac(n, dst, width=512, parts=P, shape=None):
                act.wait_ge(tp_full, n + 1)
                src = bank[tp_bank[n]][0:parts, 0:width]
                if shape:
                    src = src.rearrange("p (a b) -> p a b", a=shape)
                act.activation(dst, src, ACT.Copy).then_inc(tp_free, 1)

            act.wait_ge(ones_ready, 1)
            for step in [step for step in att_order if step[0] != "S"]:
                g = int(step[1])
                if step[0] == "W":
                    for c in range(KC):
                        evac(G_STEP[step] + c, (gT, uT, dT)[g][:, HIGH, c, :])
                elif step[0] == "R":
                    evac(G_STEP[step], rwT[:, HIGH, :, :], KC * EXPERTS, shape=KC)
                elif step[0] == "V":
                    act.wait_ge(ld_att, 16 * 5)
                    for c in range(KC + 1):
                        act.activation(absw[:, c, :], w1[:, c, :] if c < KC else w0[:, :],
                                       ACT.Abs).then_inc(absw_ready, 1)
                elif step[0] == "T":
                    if g >= 2:
                        act.wait_ge(l1_full, KC * (g - 1))
                    evac(G_STEP[step], ctxT[:, g % 2, :])
                elif step[0] == "A":
                    if g == 0:
                        act.wait_ge(ld_l0, 32)
                    for c in range(KC):
                        n = KC * g + c
                        act.wait_ge(l1_full, n + 1)
                        if n >= 2:
                            act.wait_ge(h1_ready, n - 1)
                        act.activation(he[:, n % 2, :], bank[2 + c][:, :], ACT.Exp, bias=b0c[:, c:c + 1])
                        act.activation(hr[:, n % 2, :], bank[2 + c][:, :], ACT.Relu,
                                       bias=b0c[:, c:c + 1]).then_inc(l1_act, 1)
                else:
                    for t in range(TPG):
                        n = TPG * g + t
                        act.wait_ge(z_ready, n + 1)
                        if n >= 2:
                            act.wait_ge(x1_ready, n - 1)
                        act.activation(th[:, n % 2, :], sg[:, n % 2, :], ACT.Exp,
                                       bias=minus_one[:, :]).then_inc(ez_ready, 1)
            act.wait_ge(x1_ready, TILES)
            act.wait_ge(l2_full, TILES)
            unless_one_hot(act, slow_scalar)

            def normed(g, tiles):
                act.wait_ge(ln_ready, g + 1)
                if g >= 2:
                    act.wait_ge(rows_x[g % 2], 16 * (g // 2))
                for n in [TPG * g + t for t in tiles]:
                    act.activation(xn[g % 2][:, n % TPG, :], xs[:, n, :], ACT.Identity, bias=nmr[:, n:n + 1],
                                   scale=rstd[:, n:n + 1]).then_inc(xn_ready, 1)

            def logits(g):
                act.wait_ge(r_full, g + 1)
                if g >= 2:
                    act.wait_ge(tp_full, G_L[g - 2] + 1)
                act.activation(sg[0:EXPERTS, g % 2, :], bank[6 + g % 2][0:EXPERTS, :], ACT.Tanh, scale=0.5).then_inc(r_act, 1)

            def logits_out(g):
                evac(G_L[g], rth[:, g, :, :], TPG * EXPERTS, shape=TPG)

            normed(0, range(TPG))
            for g in range(GRAPHS):
                if g >= 2:
                    act.wait_ge(xn_ready, TPG * (2 * g - 2) if g == 2 else TILES)
                    for b in range(2 * (g - 2), 2 * (g - 1)):
                        act.wait_ge(x1_stored[b], 16)
                for t in range(TPG):
                    if g + 1 < GRAPHS:
                        normed(g + 1, [t])
                    evac(G_X[g] + t, xT(g, HIGH)[:, :, P * t:P * t + P], shape=KC)
                if g >= 2:
                    logits_out(g - 2)
                if g:
                    logits(g - 1)
            logits_out(GRAPHS - 2)
            logits(GRAPHS - 1)
            logits_out(GRAPHS - 1)

            def spread(e):
                if e >= 3:
                    act.wait_ge(gu_full, hidden_no["E", e - 3] + 1)
                evac(G_EXP + e, xgT[:, e % 3, :, :], KC * CAP, shape=KC)

            def split_down(e):
                act.wait_ge(ld_down[e % RING], 16 * (e // RING + 1))
                if e:
                    act.wait_ge(y_full, output_no["Y", e - 1] + 1)
                else:
                    act.wait_ge(rows_w, 16 * GRAPHS)
                act.activation(down[:, HIGH, :, :], ring_down(e), ACT.Copy).then_inc(down_high, 1)

            for u in units:
                kind, n = u
                if kind == "Y" and n + 1 < EXPERTS:
                    split_down(n + 1)
                if kind == "K":
                    evac(G_SEL, selT, D)
                elif kind == "M":
                    evac(G_MERGE, key2, GRAPHS * CAP, parts=EXPERTS)
                elif kind == "T":
                    evac(G_TOK, tok[:, :], EXPERTS, parts=CAP)
                elif kind in "SE":
                    if u == ("E", 0):
                        split_down(0)
                        spread(0)
                    if kind == "E" and n + 1 < EXPERTS:
                        spread(n + 1)
                    i = hidden_no[u]
                    cols = SEQ if kind == "S" else 2 * CAP
                    act.wait_ge(gu_full, i + 1)
                    if i >= 2:
                        act.wait_ge(h_ready, i - 1)
                    act.activation(th[:, i % 2, 0:cols], bank[2 + i % 2][:, 0:cols], ACT.Tanh,
                                   scale=0.5).then_inc(gu_act, 1)
                else:
                    i = output_no[u]
                    act.wait_ge(y_full, i + 1)
                    if kind == "D":
                        g = n // TPG
                        if g >= 2:
                            act.wait_ge(added, 16 * (add_no["D", TPG * (g - 1) - 1] + 1))
                        act.activation(ob[:, g % 2, n % TPG, :], bank[6 + i % 2][:, :], ACT.Copy).then_inc(y_ready, 1)
                    else:
                        if n >= 3:
                            act.wait_ge(added, 16 * (add_no["Y", n - 3] + 1))
                        act.activation(ey[:, n % 3, :], bank[6 + i % 2][0:CAP, :], ACT.Copy,
                                       scale=xg[:, n % XRING, D + n:D + n + 1]).then_inc(y_ready, 1)

        @block.vector
        def _(v):
            done = [0]

            def link(ins):
                done[0] += 1
                ins.then_inc(dve, 1)
                v.wait_ge(dve, done[0])

            def low(n, dst, shape=None):
                part, width = dst
                v.wait_ge(tp_free, n + 1)
                src = bank[tp_bank[n]][:, 0:width]
                if shape:
                    src = src.rearrange("p (a b) -> p a b", a=shape)
                v.tensor_tensor(part(LOW), src, part(HIGH).bitcast(f32), ALU.subtract).then_inc(tp_low, 1)

            def low_weights(i):
                for c in range(KC):
                    low(G_STEP[f"W{i}"] + c, (lambda h: (gT, uT, dT)[i][:, h, c, :], D))

            v.memset(minus_one[:, :], -1.0)
            v.memset(ones[:, :], 1.0).then_inc(ones_ready, 1)
            for t in range(TILES):
                g = t // TPG
                if t % TPG == 0:
                    v.wait_ge(ld_x[g], 16)
                v.max(mx[:, t, :], xs[:, t, :]).then_inc(top_done, 1)
                v.wait_ge(top_done, t + 1)
                v.max_index(ix[:, t, :], mx[:, t, :], xs[:, t, :]).then_inc(idx_done, 1)
                if t % TPG == TPG - 1:
                    v.wait_ge(idx_done, t + 1)
                    v.tensor_scalar(ixg[:, TPG * g:t + 1], ix[:, TPG * g:t + 1, 0], float(SEQ * g), None,
                                    ALU.add).then_inc(idxg_ready, 1)
                    if g == 1:
                        low_weights(0)

            def take_sums():
                v.wait_ge(ld_l0, 32)
                v.wait_ge(ld_att, 16 * 5)
                link(v.tensor_scalar(b1r[:, :], b1r[:, :], 1.0, None, ALU.add))
                v.wait_ge(sums_full, 1)
                v.tensor_copy(sums[:, :, :], bank[7][:, 0:2 * KC].rearrange("p (b n) -> p b n", b=2)).then_inc(sums_ready, 1)

            def stats0(t):
                link(v.bn_stats(bn0[:, t % 2, :], xs[:, t, :]))
                link(v.bn_aggr(mv0[:, t, :], bn0[:, t % 2, :]))

            def spread_of_x():
                v.tensor_scalar(chk[:, 3, :, 0], mv0[:, :, 1], EPS, None, ALU.add).then_inc(var0_ready, 1)

            def largest_ctx(i):
                v.wait_ge(ld_chk, 16 * 8)
                v.tensor_reduce(out=worst4[:, i:i + 1], in_=ctx_all[:, D * i:D * i + D], op=ALU.max, axis=AX.X,
                                apply_absolute_value=True).then_inc(worst4_ready, 1)

            def smallest_gap():
                v.wait_ge(pow0_ready, 1)
                link(v.tensor_tensor(chk[:, 0, :, :], mx[:, :, 0:2], mv0[:, :, 0:1].to_broadcast([P, TILES, 2]), ALU.subtract))
                link(v.tensor_tensor(chk[:, 1, :, :], chk[:, 0, :, :], chk[:, 3, :, 1:2].to_broadcast([P, TILES, 2]), ALU.mult))
                link(v.tensor_scalar(chk[:, 0, :, :], chk[:, 1, :, :], -1.0, 1.0, ALU.mult, ALU.add))
                link(v.tensor_scalar(chk[:, 1, :, :], chk[:, 0, :, :], MASK, None, ALU.mult))
                link(v.tensor_tensor(chk[:, 2, :, 0], chk[:, 1, :, 1], chk[:, 1, :, 0], ALU.subtract))
                v.reduce_max(worst[:, 1:2], chk[:, 2, :, 0], axis=AX.X)
                v.wait_ge(worst4_ready, 4)
                v.reduce_max(worst[:, 0:1], worst4[:, :], axis=AX.X)
                v.tensor_reduce(out=worst[:, 2:3], in_=b0c[:, :], op=ALU.max, axis=AX.X, apply_absolute_value=True)
                v.wait_ge(sums_ready, 1)
                v.reduce_max(worst[:, 3:4], sums[:, 0, :], axis=AX.X).then_inc(worst_ready, 1)

            def decide_weights():
                link(v.scalar_tensor_tensor(arow[:, :, :, :], arow[:, :, :, :], -1.0, arow[:, :, :, :], ALU.mult, ALU.max))
                link(v.tensor_tensor(prod[:, :, :], arow[:, :, 0, :], arow[:, :, 1, :], ALU.add))
                v.tensor_tensor(prod[:, :, :], prod[:, :, :], sums[:, :, :], ALU.mult).then_inc(worst_ready, 1)

            def decide():
                b = [bound[:, i:i + 1] for i in range(16)]
                v.wait_ge(worst_full, 1)
                v.reduce_max(bound[:, 2:4], bank[1][0:1, 0:2 * KC].rearrange("p (b n) -> p b n", b=2), axis=AX.X)
                link(v.reduce_max(bound[:, 4:8], bank[0][0:1, :].rearrange("p (b n) -> p b n", b=4), axis=AX.X))
                v.tensor_tensor(b[8], b[4], b[2], ALU.mult)
                link(v.scalar_tensor_tensor(b[12], b[7], b[4], b[6], ALU.mult, ALU.add))
                link(v.scalar_tensor_tensor(b[13], b[12], 1.0, b[3], ALU.add, ALU.mult))
                link(v.tensor_tensor(b[9], b[8], b[13], ALU.max))
                link(v.tensor_scalar(b[10], b[9], LOGIT_FACTOR, ROUNDING, ALU.mult, ALU.add))
                link(v.tensor_tensor(b[11], b[10], b[5], ALU.add))
                v.tensor_scalar(fast_flag[:, :], b[11], 0.0, None, ALU.is_lt).then_inc(flag_ready, 1)

            def first(n):
                v.wait_ge(l2_full, n + 1)
                if n >= 2:
                    v.wait_ge(x1_ready, n - 1)
                v.tensor_tensor(sg[:, n % 2, :], bank[6 + n % 2][:, :], b1r[:, :], ALU.add).then_inc(z_ready, 1)

            def second(n):
                v.wait_ge(ez_ready, n + 1)
                link(v.scalar_tensor_tensor(e1[:, n % 2, :], th[:, n % 2, :], 1.0, sg[:, n % 2, :], ALU.min, ALU.max))
                v.scalar_tensor_tensor(xs[:, n, :], e1[:, n % 2, :], -1.0, xs[:, n, :], ALU.add,
                                       ALU.add).then_inc(x1_ready, 1)

            def row_stats(n):
                v.wait_ge(x1_ready, n + 1)
                v.bn_stats(bn[:, n % TPG, :], xs[:, n, :]).then_inc(bn_done, 1)

            def variances(g):
                v.wait_ge(bn_done, TPG * (g + 1))
                for t in range(TPG * g, TPG * g + TPG):
                    ins = v.bn_aggr(mv[:, t, :], bn[:, t % TPG, :])
                link(ins)
                s = slice(TPG * g, TPG * g + TPG)
                v.tensor_scalar(ve[:, s], mv[:, s, 1], EPS, None, ALU.add).then_inc(ve_ready, 1)

            def scales(g):
                s = slice(TPG * g, TPG * g + TPG)
                v.wait_ge(ve_ready, g + 1)
                v.wait_ge(pow_ready, g + 1)
                link(v.tensor_tensor(nt1[:, s], ve[:, s], r0[:, s], ALU.mult))
                link(v.tensor_tensor(nt1[:, s], nt1[:, s], r0[:, s], ALU.mult))
                link(v.tensor_scalar(nt1[:, s], nt1[:, s], -0.5, 1.5, ALU.mult, ALU.add))
                link(v.tensor_tensor(rstd[:, s], r0[:, s], nt1[:, s], ALU.mult))
                v.scalar_tensor_tensor(nmr[:, s], mv[:, s, 0], -1.0, rstd[:, s], ALU.mult,
                                       ALU.mult).then_inc(ln_ready, 1)

            between = [lambda t=t: (stats0(t), stats0(t + 1)) for t in range(2 * TPG, TILES, 2)]
            between[-1] = lambda: (stats0(TILES - 2), stats0(TILES - 1), spread_of_x())
            between += [lambda i=i: largest_ctx(i) for i in range(4)] + [smallest_gap, decide_weights, None, None, decide]
            for step in att_order:
                g = int(step[1])
                if step[0] == "A":
                    for c in range(KC):
                        n = KC * g + c
                        v.wait_ge(l1_act, n + 1)
                        if g >= 2 and c == 0:
                            v.wait_ge(l2_full, TPG * (g - 1))
                        link(v.tensor_scalar(e1[:, n % 2, :], he[:, n % 2, :], 1.0, -1.0, ALU.min, ALU.add))
                        v.tensor_tensor(h1T[:, g % 2, c, :], e1[:, n % 2, :], hr[:, n % 2, :], ALU.add).then_inc(h1_ready, 1)
                elif step == "W1":
                    low_weights(g)
                    for t in range(2 * TPG):
                        stats0(t)
                elif step == "W2":
                    low_weights(g)
                elif step[0] == "R":
                    low(G_STEP[step], (lambda h: rwT[:, h, :, :], KC * EXPERTS), shape=KC)
                elif step[0] == "B":
                    if g == 0:
                        take_sums()
                    first(TPG * g)
                    for n in range(TPG * g, TPG * g + TPG):
                        if n + 1 < TPG * (g + 1):
                            first(n + 1)
                        second(n)
                        if n % TPG:
                            row_stats(n - 1)
                        extra = between.pop(0) if between else None
                        if extra:
                            extra()
                    row_stats(TPG * (g + 1) - 1)
                    variances(g)
                    if g:
                        scales(g - 1)
            scales(GRAPHS - 1)
            v.wait_ge(x1_ready, TILES)
            unless_one_hot(v, slow_vector)

            def route_steps(pair):
                v.wait_ge(tp_free, G_L[2 * pair + 1] + 1)
                tiles = slice(PAIR * pair, PAIR * pair + PAIR)
                if pair:
                    v.wait_ge(wd_ready, pair)
                if pair == 0:
                    v.wait_ge(ld_eb, 16)
                    v.wait_ge(consts, 5)
                link(v.tensor_scalar(S[:, :, :], rth[:, 2 * pair:2 * pair + 2, :, :].rearrange("p g t e -> p (g t) e"), 0.5, 0.5, ALU.mult, ALU.add))
                yield
                link(v.tensor_tensor(SB[:, :, :], S[:, :, :], ebr[:, :].unsqueeze(1).to_broadcast([P, PAIR, EXPERTS]), ALU.add))
                yield
                q = SB[:, :, :].rearrange("p t (g j) -> p t g j", j=GSIZE)
                a, b, c, d, m, n, top, gs = (rg[:, i, :, :] for i in range(8))
                v.tensor_tensor(a, q[:, :, :, 0], q[:, :, :, 1], ALU.max)
                v.tensor_tensor(b, q[:, :, :, 0], q[:, :, :, 1], ALU.min)
                v.tensor_tensor(c, q[:, :, :, 2], q[:, :, :, 3], ALU.max)
                link(v.tensor_tensor(d, q[:, :, :, 2], q[:, :, :, 3], ALU.min))
                yield
                v.tensor_tensor(m, a, c, ALU.min)
                v.tensor_tensor(n, b, d, ALU.max)
                link(v.tensor_tensor(top, a, c, ALU.max))
                yield
                link(v.tensor_tensor(m, m, n, ALU.max))
                yield
                link(v.tensor_tensor(gs, top, m, ALU.add))
                yield
                for t in range(PAIR):
                    ins = v.max(rgm[:, t, :], rg[:, 7, t, :])
                link(ins)
                yield
                for t in range(PAIR):
                    ins = v.max_index(rgi[:, t, :], rgm[:, t, :], rg[:, 7, t, :])
                link(ins)
                yield
                link(v.tensor_copy(rgf[:, :, :], rgi[:, :, :]))
                yield
                for k in range(TOP_GROUPS):
                    ins = v.tensor_tensor(rg[:, k, :, :], iota8[:, :, :].to_broadcast([P, PAIR, GROUPS]),
                                          rgf[:, :, k:k + 1].to_broadcast([P, PAIR, GROUPS]), ALU.is_equal)
                link(ins)
                yield
                link(v.tensor_tensor(rg[:, 3, :, :], rg[:, 0, :, :], rg[:, 1, :, :], ALU.add))
                yield
                link(v.tensor_tensor(rg[:, 4, :, :], rg[:, 3, :, :], rg[:, 2, :, :], ALU.add))
                yield
                link(v.tensor_tensor(q, q, rg[:, 4, :, :].unsqueeze(3).to_broadcast([P, PAIR, GROUPS, GSIZE]), ALU.mult))
                yield
                for t in range(PAIR):
                    ins = v.max(rgm[:, t, :], SB[:, t, :])
                link(ins)
                yield
                for t in range(PAIR):
                    ins = v.max_index(rgi[:, t, :], rgm[:, t, :], SB[:, t, :])
                link(ins)
                yield
                link(v.tensor_copy(rgf[:, :, :], rgi[:, :, :]))
                yield
                for k in range(TOP_K):
                    ins = v.tensor_tensor(eq[:, k, :, :], iota32[:, :, :].to_broadcast([P, PAIR, EXPERTS]),
                                          rgf[:, :, k:k + 1].to_broadcast([P, PAIR, EXPERTS]), ALU.is_equal)
                link(ins)
                yield
                link(v.tensor_tensor(eq[:, 0:2, :, :], eq[:, 0:2, :, :], eq[:, 2:4, :, :], ALU.add))
                yield
                so = sel[:, tiles, :]
                v.tensor_tensor(so, eq[:, 0, :, :], eq[:, 1, :, :], ALU.add).then_inc(sel_ready, 1)
                v.wait_ge(sel_ready, pair + 1)
                link(v.tensor_tensor(S[:, :, :], S[:, :, :], so, ALU.mult))
                yield
                link(v.reduce_sum(den[:, :], S[:, :, :], axis=AX.X))
                yield
                link(v.tensor_scalar(den[:, :], den[:, :], 1e-20, None, ALU.add))
                yield
                link(v.reciprocal(den[:, :], den[:, :]))
                yield
                v.scalar_tensor_tensor(wd[:, tiles, :], S[:, :, :], SCALE,
                                       den[:, :].unsqueeze(2).to_broadcast([P, PAIR, EXPERTS]), ALU.mult,
                                       ALU.mult).then_inc(wd_ready, 1)

            def hidden(u):
                kind, n = u
                i = hidden_no[u]
                if u == ("S", 0):
                    v.wait_ge(rows_x[1], 16 * (GRAPHS // 2))
                v.wait_ge(gu_act, i + 1)
                if kind == "S":
                    g, cols, up = n // KC, SEQ, bank[4 + i % 2][:, :]
                    if n % KC == 0 and g:
                        v.wait_ge(y_full, output_no["D", TPG * g - 1] + 1)
                    parts = [hT[:, h, n % KC, :] for h in (HIGH, LOW)]
                else:
                    cols, up = 2 * CAP, bank[2 + i % 2][:, 2 * CAP:4 * CAP]
                    parts = [ehT[:, n % 2, h, :] for h in (HIGH, LOW)]
                    if n >= 2:
                        v.wait_ge(y_full, output_no["Y", n - 2] + 1)
                h = th[:, i % 2, 0:cols]
                link(v.scalar_tensor_tensor(sg[:, i % 2, 0:cols], h, 1.0, bank[2 + i % 2][:, 0:cols], ALU.add, ALU.mult))
                v.scalar_tensor_tensor(h, sg[:, i % 2, 0:cols], 0.5, up, ALU.mult, ALU.mult).then_inc(gu_free, 1)
                v.wait_ge(gu_free, i + 1)
                link(v.tensor_copy(parts[HIGH], h))
                v.tensor_tensor(parts[LOW], h, parts[HIGH].bitcast(f32), ALU.subtract).then_inc(h_ready, 1)

            def low_down(e):
                v.wait_ge(down_high, e + 1)
                v.tensor_tensor(down[:, LOW, :, :], ring_down(e), down[:, HIGH, :, :].bitcast(f32),
                                ALU.subtract).then_inc(down_low, 1)

            def top(keys, best, step):
                r, part = divmod(step, 2)
                k8 = best[:, 8 * r:8 * r + 8]
                if part == 0:
                    link(v.max(k8, keys))
                    if keys is key and r + 1 == ROUNDS:
                        v.sem_inc(kk1_ready)
                elif r + 1 < ROUNDS:
                    link(v.match_replace(keys, k8, keys, RETIRED))

            early = [u for u in first_part if u[0] == "S"]
            routes = [route_steps(pair) for pair in range(GRAPHS // 2)]
            for g in range(GRAPHS):
                for t in range(TPG):
                    low(G_X[g] + t, (lambda h: xT(g, h)[:, :, P * t:P * t + P], D), shape=KC)

            def some(steps, n):
                for i in range(n):
                    next(steps, None)

            some(routes[0], 99)
            some(routes[1], 8)
            hidden(early.pop(0))
            some(routes[1], 99)
            hidden(early.pop(0))
            hidden(early.pop(0))
            v.wait_ge(tp_free, G_SEL + 1)
            v.wait_ge(consts, 5 + GRAPHS)
            link(v.scalar_tensor_tensor(key, selT, float(TOKENS), key, ALU.mult, ALU.add))
            for i in range(2 * ROUNDS):
                top(key, kk1[:, :], i)
                if i in (3, 15):
                    hidden(early.pop(0))
            v.wait_ge(tp_free, G_MERGE + 1)
            for i in range(2 * ROUNDS):
                top(key2, kk[:, :], i)
                if i in (1, 4, 7):
                    hidden(early.pop(0))
            link(v.tensor_scalar(kt[:, :], kk[:, :], float(TOKENS), float(TOKENS), ALU.is_gt, ALU.mult))
            v.scalar_tensor_tensor(tokf[:, :], kt[:, :], float(TOKENS), kk[:, :], ALU.add,
                                   ALU.subtract).then_inc(tok_ready, 1)
            for u in early:
                hidden(u)
            low_down(0)
            for u in mixed_part:
                if u[0] in "SE":
                    hidden(u)
                elif u[0] == "Y" and u[1] + 1 < EXPERTS:
                    low_down(u[1] + 1)

        @block.tensor
        def _(pe):
            def bank_free(n):
                if last_in_bank[n] is not None:
                    pe.wait_ge(tp_free, last_in_bank[n] + 1)
                    if last_in_bank[n] in low_no:
                        pe.wait_ge(tp_low, low_no[last_in_bank[n]] + 1)

            def group(n, parts):
                bank_free(n)
                for dst, src in parts:
                    k = src.shape[0]
                    last = pe.transpose(dst(bank[tp_bank[n]]), src, ident[0:k, 0:k])
                last.then_inc(tp_full, 1)

            def product(dst, w, t, start, stop):
                pe.matmul(dst, w(HIGH), t(HIGH), start=start, stop=False)
                pe.matmul(dst, w(HIGH), t(LOW), start=False, stop=False)
                return pe.matmul(dst, w(LOW), t(HIGH), start=False, stop=stop)

            pe.wait_ge(consts, 2)
            for step in [step for step in att_order if step[0] != "V"]:
                g = int(step[1])
                if step[0] == "W":
                    if g == 2:
                        pe.wait_ge(l1_act, KC * GRAPHS)
                        pe.wait_ge(flag_ready, 1)
                    pe.wait_ge(ld_sh[g], 16 if g == 0 else 16 * KC)
                    for c in range(KC):
                        group(G_STEP[step] + c,
                              [(lambda b, r=r: b[:, P * r:P * r + P], raw(g)[:, r, P * c:P * c + P]) for r in range(KC)])
                elif step[0] == "R":
                    pe.wait_ge(ld_sh[3], 16)
                    group(G_STEP[step], [(lambda b, c=c: b[:, EXPERTS * c:EXPERTS * c + EXPERTS],
                                          rwraw[:, P * c:P * c + P]) for c in range(KC)])
                elif step[0] == "S":
                    pe.wait_ge(ones_ready, 1)
                    pe.wait_ge(absw_ready, KC + 1)
                    for m in range(KC):
                        pe.matmul(bank[7][:, m:m + 1], absw[:, KC, P * m:P * m + P], ones[:, 0:1], start=True, stop=True)
                    for m in range(KC):
                        for c in range(KC):
                            last = pe.matmul(bank[7][:, KC + m:KC + m + 1], absw[:, c, P * m:P * m + P], ones[:, 0:1],
                                             start=(c == 0), stop=(c == KC - 1))
                    last.then_inc(sums_full, 1)
                elif step[0] == "T":
                    pe.wait_ge(ctxg_ready[g], 16 * TPG)
                    group(G_STEP[step], [(lambda b, t=t: b[:, P * t:P * t + P], ctxg[:, g % 2, t, :]) for t in range(TPG)])
                elif step[0] == "A":
                    pe.wait_ge(tp_free, G_STEP[step.replace("A", "T")] + 1)
                    if g == 0:
                        pe.wait_ge(ld_l0, 32)
                    for c in range(KC):
                        n = KC * g + c
                        if g:
                            pe.wait_ge(l1_act, n - KC + 1)
                        pe.matmul(bank[2 + c][:, :], w0[:, P * c:P * c + P], ctxT[:, g % 2, :],
                                  start=True, stop=True).then_inc(l1_full, 1)
                else:
                    pe.wait_ge(h1_ready, KC * (g + 1))
                    if g == 0:
                        pe.wait_ge(sums_ready, 1)
                    if g == 3:
                        pe.wait_ge(tp_free, G_STEP["W2"])
                        pe.wait_ge(worst_ready, 2)
                        for c in range(4):
                            pe.transpose(bank[0][0:1, P * c:P * c + P], worst[:, c:c + 1], ident[:, :])
                        pe.matmul(bank[1][:, 0:2 * KC], ones[:, :], prod[:, :, :], start=True, stop=True).then_inc(worst_full, 1)
                    for t in range(TPG):
                        n = TPG * g + t
                        if n >= 2:
                            pe.wait_ge(z_ready, n - 1)
                        for c in range(KC):
                            last = pe.matmul(bank[6 + n % 2][:, :], h1T[:, g % 2, c, P * t:P * t + P], w1[:, c, :],
                                             start=(c == 0), stop=(c == KC - 1))
                        last.then_inc(l2_full, 1)
            unless_one_hot(pe, slow_tensor)
            def transposed(g):
                for t in range(TPG):
                    pe.wait_ge(xn_ready, TPG * g + t + 1)
                    group(G_X[g] + t, [(lambda b, c=c: b[:, P * c:P * c + P], xn[g % 2][:, t, P * c:P * c + P])
                                       for c in range(KC)])

            def router(g):
                if g == 0:
                    pe.wait_ge(z_ready, TILES)
                if g >= 2:
                    pe.wait_ge(r_act, g - 1)
                pe.wait_ge(tp_low, low_no[G_X[g] + TPG - 1] + 1)
                for c in range(KC):
                    last = product(bank[6 + g % 2][0:EXPERTS, :], lambda h: rwT[:, h, c, :], lambda h: xT(g, h)[:, c, :],
                                   start=(c == 0), stop=(c == KC - 1))
                last.then_inc(r_full, 1)

            def logits_out(g):
                pe.wait_ge(r_act, g + 1)
                group(G_L[g], [(lambda b, t=t: b[:, EXPERTS * t:EXPERTS * t + EXPERTS],
                                sg[0:EXPERTS, g % 2, P * t:P * t + P]) for t in range(TPG)])

            transposed(0)
            for g in range(1, GRAPHS):
                transposed(g)
                if g >= 2:
                    logits_out(g - 2)
                router(g - 1)
            logits_out(GRAPHS - 2)
            router(GRAPHS - 1)
            logits_out(GRAPHS - 1)
            pe.wait_ge(tp_free, G_SEL)

            def shared_hidden(n, i):
                g, part = n // KC, n % KC
                for b, w in ((2, gT), (4, uT)):
                    for c in range(KC):
                        last = product(bank[b + i % 2][:, :], lambda h: w[:, h, c, P * part:P * part + P],
                                       lambda h: xT(g, h)[:, c, :], start=(c == 0), stop=(c == KC - 1))
                last.then_inc(gu_full, 1)

            def expert_hidden(e, i):
                pe.wait_ge(tp_free, G_EXP + e + 1)
                pe.wait_ge(ld_gate_up[e % RING], 32 * (e // RING + 1))
                for j, w in enumerate((ring_gate(e), ring_up(e))):
                    for k in range(IC):
                        at = CAP * (IC * j + k)
                        for c in range(KC):
                            last = pe.matmul(bank[2 + i % 2][:, at:at + CAP], w[:, c, P * k:P * k + P],
                                             xgT[:, e % 3, c, :], start=(c == 0), stop=(c == KC - 1))
                last.then_inc(gu_full, 1)

            def shared_out(n, i):
                g, t = n // TPG, n % TPG
                pe.wait_ge(h_ready, hidden_no["S", KC * g + KC - 1] + 1)
                for c in range(KC):
                    last = product(bank[6 + i % 2][:, :], lambda h: hT[:, h, c, P * t:P * t + P],
                                   lambda h: dT[:, h, c, :], start=(c == 0), stop=(c == KC - 1))
                last.then_inc(y_full, 1)

            def expert_out(e, i):
                pe.wait_ge(h_ready, hidden_no["E", e] + 1)
                pe.wait_ge(down_low, e + 1)
                for k in range(IC):
                    last = product(bank[6 + i % 2][0:CAP, :], lambda h: ehT[:, e % 2, h, CAP * k:CAP * k + CAP],
                                   lambda h: down[:, h, k, :], start=(k == 0), stop=(k == IC - 1))
                last.then_inc(y_full, 1)

            def spread(e):
                pe.wait_ge(xg_ready[e % XRING], 16 * (e // XRING + 1))
                group(G_EXP + e, [(lambda b, c=c: b[:, CAP * c:CAP * c + CAP], xg[:, e % XRING, c:D:KC])
                                  for c in range(KC)])

            for u in units:
                kind, n = u
                if kind == "K":
                    b = bank[tp_bank[G_SEL]]
                    bank_free(G_SEL)
                    for g in range(GRAPHS):
                        pe.wait_ge(sel_ready, g // 2 + 1)
                        for t in range(TPG):
                            last = pe.matmul(b[EXPERTS * g:EXPERTS * g + EXPERTS, P * t:P * t + P],
                                             sel[:, TPG * g + t, :], ident[:, :], start=True, stop=True)
                    last.then_inc(tp_full, 1)
                elif kind == "T":
                    pe.wait_ge(tok_ready, 1)
                    group(G_TOK, [(lambda b: b[0:CAP, 0:EXPERTS], tokf[:, :])])
                elif kind == "M":
                    b = bank[tp_bank[G_MERGE]]
                    bank_free(G_MERGE)
                    pe.wait_ge(kk1_ready, 1)
                    for g in range(GRAPHS):
                        last = pe.matmul(b[0:EXPERTS, CAP * g:CAP * g + CAP], ident[:, EXPERTS * g:EXPERTS * g + EXPERTS],
                                         kk1[:, :], start=True, stop=True)
                    last.then_inc(tp_full, 1)
                elif kind in "SE":
                    i = hidden_no[u]
                    if u == ("E", 0):
                        spread(0)
                    if kind == "E" and n + 1 < EXPERTS:
                        spread(n + 1)
                    if i >= 2:
                        pe.wait_ge(gu_free, i - 1)
                    (shared_hidden if kind == "S" else expert_hidden)(n, i)
                else:
                    i = output_no[u]
                    if i >= 2:
                        pe.wait_ge(y_ready, i - 1)
                    else:
                        pe.wait_ge(r_act, GRAPHS)
                    (shared_out if kind == "D" else expert_out)(n, i)


_INS = ['x', 'ctx_512', 'L0_xattn_W0', 'L0_xattn_a_self0', 'L0_xattn_a_neigh0', 'L0_xattn_b0', 'L0_xattn_W1',
        'L0_xattn_a_self1', 'L0_xattn_a_neigh1', 'L0_xattn_b1', 'L0_ffn_router_w', 'L0_ffn_e_bias',
        'L0_ffn_W_gate', 'L0_ffn_W_up', 'L0_ffn_W_down', 'L0_ffn_shared_gate', 'L0_ffn_shared_up',
        'L0_ffn_shared_down']
_OUTS = [((GRAPHS, SEQ, D), 'float32')]


def kernel(**inputs):
    import numpy as _np
    import concourse.bacc as _bacc
    from concourse import mybir as _mybir
    from concourse.bass_utils import run_bass_kernel_spmd as _run

    nc = _bacc.Bacc("TRN2", target_bir_lowering=False, num_devices=1)
    arrays, args = {}, []
    for name in _INS:
        a = _np.ascontiguousarray(inputs[name])
        arrays[f"in_{name}_dram"] = a
        args.append(nc.dram_tensor(f"in_{name}_dram", a.shape, _mybir.dt.from_np(a.dtype), kind="ExternalInput").ap())
    for i, (shape, dtype) in enumerate(_OUTS):
        dt = _mybir.dt.from_np(_np.dtype(dtype))
        args.append(nc.dram_tensor(f"out_{i}_dram", shape, dt, kind="ExternalOutput").ap())
    xattn_moe(nc, *args)
    r = _run(nc, [arrays], core_ids=[0])
    return r.results[0]["out_0_dram"]
```
